# Optimizing a Trainium2 kernel written in Bass

```python
import numpy as np
import jax
import jax.numpy as jnp

def _softmax(x, axis=-1):
    return jax.nn.softmax(x, axis=axis)

def _gelu(x):
    return jax.nn.gelu(x, approximate=True)

def _silu(x):
    return jax.nn.silu(x)

def _sigmoid(x):
    return jax.nn.sigmoid(x)

def _layernorm(x, axis=-1, eps=1e-05):
    m = jnp.mean(x, axis=axis, keepdims=True)
    v = jnp.var(x, axis=axis, keepdims=True)
    return (x - m) / jnp.sqrt(v + eps)

def _scatter_add(tgt, idx, src, axis=0):
    return tgt.at[idx].add(src)

def _segment_sum(src, seg, n):
    return jax.ops.segment_sum(src, seg, n)
kernel_name = 'mk_conv_preact_d4_conv_nhwc192_r2_9f517b'

def setup_inputs(seed: int=0):
    np.random.seed(seed)
    _w = jnp.asarray

    def _rec_inputs():
        import jax
        import jax.numpy as jnp
        _gk = jax.random.key(seed)
        x = -0.0005963 + 1.001 * jax.random.normal(jax.random.fold_in(_gk, 1), (4, 32, 32, 96), jnp.float32)
        return x
    x = _rec_inputs()

    def _L0_conv_setup():
        import jax, jax.numpy as jnp
        import numpy as np
        D_MODEL = 96
        D_STATE = 16
        D_INNER = 192
        DT_RANK = 12
        K = 4
        B_, H_, W_ = (4, 32, 32)
        EPS = 1e-06

        def _selective_scan(u, delta, A, Bs, Cs, Ds, delta_bias):
            Bb, KD, L = u.shape
            N = A.shape[1]
            D = KD // K
            delta = jax.nn.softplus(delta + delta_bias[None, :, None])
            u_k = u.reshape(Bb, K, D, L)
            d_k = delta.reshape(Bb, K, D, L)
            A_k = A.reshape(K, D, N)

            def step(h, inp):
                dt, ut, bt, ct = inp
                dA = jnp.exp(dt[..., None] * A_k[None])
                dBu = dt[..., None] * bt[:, :, None, :] * ut[..., None]
                h = dA * h + dBu
                y = jnp.einsum('bkdn,bkn->bkd', h, ct)
                return (h, y)
            h0 = jnp.zeros((Bb, K, D, N), u.dtype)
            inps = (jnp.moveaxis(d_k, -1, 0), jnp.moveaxis(u_k, -1, 0), jnp.moveaxis(Bs, -1, 0), jnp.moveaxis(Cs, -1, 0))
            _, ys = jax.lax.scan(step, h0, inps)
            y = jnp.moveaxis(ys, 0, -1).reshape(Bb, KD, L)
            return y + u * Ds[None, :, None]
        key = jax.random.key(seed)
        ks = jax.random.split(key, 7)
        x = jax.random.normal(ks[0], (B_, H_, W_, D_MODEL), jnp.float32)
        in_proj_weight = jax.random.normal(ks[1], (2 * D_INNER, D_MODEL), jnp.float32) * D_MODEL ** (-0.5)
        out_proj_weight = jax.random.normal(ks[2], (D_MODEL, D_INNER), jnp.float32) * D_INNER ** (-0.5)
        x_proj_weight = jax.random.normal(ks[3], (K, DT_RANK + 2 * D_STATE, D_INNER), jnp.float32) * 0.02
        dt_projs_weight = jax.random.normal(ks[4], (K, D_INNER, DT_RANK), jnp.float32) * DT_RANK ** (-0.5)
        dt = jnp.exp(jax.random.uniform(ks[5], (K, D_INNER)) * (np.log(0.1) - np.log(0.001)) + np.log(0.001))
        dt = jnp.clip(dt, 0.0001, None)
        dt_projs_bias = dt + jnp.log(-jnp.expm1(-dt))
        A_logs = jnp.log(jnp.tile(jnp.arange(1, D_STATE + 1, dtype=jnp.float32)[None, :], (K * D_INNER, 1)))
        Ds = jnp.ones((K * D_INNER,), jnp.float32)
        out_norm_weight = jnp.ones((D_INNER,), jnp.float32)
        out_norm_bias = jnp.zeros((D_INNER,), jnp.float32)
        return dict(x=x, in_proj_weight=in_proj_weight, out_proj_weight=out_proj_weight, x_proj_weight=x_proj_weight, dt_projs_weight=dt_projs_weight, dt_projs_bias=dt_projs_bias, A_logs=A_logs, Ds=Ds, out_norm_weight=out_norm_weight, out_norm_bias=out_norm_bias)
    _L0_conv_all = _L0_conv_setup()
    _L0_conv_in = {k: v for k, v in _L0_conv_all.items() if k in ('in_proj_weight', 'out_proj_weight', 'x_proj_weight', 'dt_projs_weight', 'dt_projs_bias', 'A_logs', 'Ds', 'out_norm_weight', 'out_norm_bias')}
    del _L0_conv_all

    def _L1_conv_setup():
        import jax, jax.numpy as jnp
        import numpy as np
        G = 16
        K = 3
        key = jax.random.key(seed)
        feature = jax.random.normal(key, (2, 64, 96, 96), dtype=jnp.float32)
        return {'feature': feature}
    _L1_conv_all = _L1_conv_setup()
    _L1_conv_in = {k: v for k, v in _L1_conv_all.items() if k in ()}
    del _L1_conv_all

    def _L2_conv_setup():
        import jax, jax.numpy as jnp
        import numpy as np
        D_MODEL = 96
        D_STATE = 16
        D_CONV = 3
        EXPAND = 2
        D_INNER = EXPAND * D_MODEL
        DT_RANK = -(-D_MODEL // 16)
        B, H, W = (2, 32, 32)
        key = jax.random.key(seed)
        ks = jax.random.split(key, 8)
        rn = lambda k, shape, s: jax.random.normal(k, shape, jnp.float32) * s
        x = rn(ks[0], (B, H, W, D_MODEL), 1.0)
        in_proj_w = rn(ks[1], (2 * D_INNER, D_MODEL), D_MODEL ** (-0.5))
        in_proj_b = jnp.zeros((2 * D_INNER,), jnp.float32)
        conv_w = rn(ks[2], (D_INNER, 1, D_CONV, D_CONV), 0.3)
        conv_b = jnp.zeros((D_INNER,), jnp.float32)
        x_proj_w = rn(ks[3], (DT_RANK + 2 * D_STATE, D_INNER), D_INNER ** (-0.5))
        dt_std = DT_RANK ** (-0.5)
        dt_proj_w = jax.random.uniform(ks[4], (D_INNER, DT_RANK), jnp.float32, -dt_std, dt_std)
        dt = jnp.exp(jax.random.uniform(ks[5], (D_INNER,), jnp.float32) * (np.float32(np.log(0.1)) - np.float32(np.log(0.001))) + np.float32(np.log(0.001)))
        dt = jnp.clip(dt, 0.0001, None)
        dt_proj_b = dt + jnp.log(-jnp.expm1(-dt))
        A_log = jnp.log(jnp.tile(jnp.arange(1, D_STATE + 1, dtype=jnp.float32)[None, :], (D_INNER, 1)))
        Ds = jnp.ones((D_INNER,), jnp.float32)
        ln_g = jnp.ones((D_INNER,), jnp.float32)
        ln_b = jnp.zeros((D_INNER,), jnp.float32)
        out_proj_w = rn(ks[6], (D_MODEL, D_INNER), D_INNER ** (-0.5))
        out_proj_b = jnp.zeros((D_MODEL,), jnp.float32)
        return dict(x=x, in_proj_w=in_proj_w, in_proj_b=in_proj_b, conv_w=conv_w, conv_b=conv_b, x_proj_w=x_proj_w, dt_proj_w=dt_proj_w, dt_proj_b=dt_proj_b, A_log=A_log, Ds=Ds, ln_g=ln_g, ln_b=ln_b, out_proj_w=out_proj_w, out_proj_b=out_proj_b)
    _L2_conv_all = _L2_conv_setup()
    _L2_conv_in = {k: v for k, v in _L2_conv_all.items() if k in ('in_proj_w', 'in_proj_b', 'conv_w', 'conv_b', 'x_proj_w', 'dt_proj_w', 'dt_proj_b', 'A_log', 'Ds', 'ln_g', 'ln_b', 'out_proj_w', 'out_proj_b')}
    del _L2_conv_all

    def _L3_conv_setup():
        import jax, jax.numpy as jnp
        import numpy as np
        D_MODEL = 96
        D_STATE = 16
        D_INNER = 192
        DT_RANK = 12
        K = 4
        B_, H_, W_ = (4, 32, 32)
        EPS = 1e-06

        def _selective_scan(u, delta, A, Bs, Cs, Ds, delta_bias):
            Bb, KD, L = u.shape
            N = A.shape[1]
            D = KD // K
            delta = jax.nn.softplus(delta + delta_bias[None, :, None])
            u_k = u.reshape(Bb, K, D, L)
            d_k = delta.reshape(Bb, K, D, L)
            A_k = A.reshape(K, D, N)

            def step(h, inp):
                dt, ut, bt, ct = inp
                dA = jnp.exp(dt[..., None] * A_k[None])
                dBu = dt[..., None] * bt[:, :, None, :] * ut[..., None]
                h = dA * h + dBu
                y = jnp.einsum('bkdn,bkn->bkd', h, ct)
                return (h, y)
            h0 = jnp.zeros((Bb, K, D, N), u.dtype)
            inps = (jnp.moveaxis(d_k, -1, 0), jnp.moveaxis(u_k, -1, 0), jnp.moveaxis(Bs, -1, 0), jnp.moveaxis(Cs, -1, 0))
            _, ys = jax.lax.scan(step, h0, inps)
            y = jnp.moveaxis(ys, 0, -1).reshape(Bb, KD, L)
            return y + u * Ds[None, :, None]
        key = jax.random.key(seed)
        ks = jax.random.split(key, 7)
        x = jax.random.normal(ks[0], (B_, H_, W_, D_MODEL), jnp.float32)
        in_proj_weight = jax.random.normal(ks[1], (2 * D_INNER, D_MODEL), jnp.float32) * D_MODEL ** (-0.5)
        out_proj_weight = jax.random.normal(ks[2], (D_MODEL, D_INNER), jnp.float32) * D_INNER ** (-0.5)
        x_proj_weight = jax.random.normal(ks[3], (K, DT_RANK + 2 * D_STATE, D_INNER), jnp.float32) * 0.02
        dt_projs_weight = jax.random.normal(ks[4], (K, D_INNER, DT_RANK), jnp.float32) * DT_RANK ** (-0.5)
        dt = jnp.exp(jax.random.uniform(ks[5], (K, D_INNER)) * (np.log(0.1) - np.log(0.001)) + np.log(0.001))
        dt = jnp.clip(dt, 0.0001, None)
        dt_projs_bias = dt + jnp.log(-jnp.expm1(-dt))
        A_logs = jnp.log(jnp.tile(jnp.arange(1, D_STATE + 1, dtype=jnp.float32)[None, :], (K * D_INNER, 1)))
        Ds = jnp.ones((K * D_INNER,), jnp.float32)
        out_norm_weight = jnp.ones((D_INNER,), jnp.float32)
        out_norm_bias = jnp.zeros((D_INNER,), jnp.float32)
        return dict(x=x, in_proj_weight=in_proj_weight, out_proj_weight=out_proj_weight, x_proj_weight=x_proj_weight, dt_projs_weight=dt_projs_weight, dt_projs_bias=dt_projs_bias, A_logs=A_logs, Ds=Ds, out_norm_weight=out_norm_weight, out_norm_bias=out_norm_bias)
    _L3_conv_all = _L3_conv_setup()
    _L3_conv_in = {k: v for k, v in _L3_conv_all.items() if k in ('in_proj_weight', 'out_proj_weight', 'x_proj_weight', 'dt_projs_weight', 'dt_projs_bias', 'A_logs', 'Ds', 'out_norm_weight', 'out_norm_bias')}
    del _L3_conv_all
    return {'x': x, 'L0_conv_in_proj_weight': _L0_conv_in['in_proj_weight'], 'L0_conv_out_proj_weight': _L0_conv_in['out_proj_weight'], 'L0_conv_x_proj_weight': _L0_conv_in['x_proj_weight'], 'L0_conv_dt_projs_weight': _L0_conv_in['dt_projs_weight'], 'L0_conv_dt_projs_bias': _L0_conv_in['dt_projs_bias'], 'L0_conv_A_logs': _L0_conv_in['A_logs'], 'L0_conv_Ds': _L0_conv_in['Ds'], 'L0_conv_out_norm_weight': _L0_conv_in['out_norm_weight'], 'L0_conv_out_norm_bias': _L0_conv_in['out_norm_bias'], 'L2_conv_in_proj_w': _L2_conv_in['in_proj_w'], 'L2_conv_in_proj_b': _L2_conv_in['in_proj_b'], 'L2_conv_conv_w': _L2_conv_in['conv_w'], 'L2_conv_conv_b': _L2_conv_in['conv_b'], 'L2_conv_x_proj_w': _L2_conv_in['x_proj_w'], 'L2_conv_dt_proj_w': _L2_conv_in['dt_proj_w'], 'L2_conv_dt_proj_b': _L2_conv_in['dt_proj_b'], 'L2_conv_A_log': _L2_conv_in['A_log'], 'L2_conv_Ds': _L2_conv_in['Ds'], 'L2_conv_ln_g': _L2_conv_in['ln_g'], 'L2_conv_ln_b': _L2_conv_in['ln_b'], 'L2_conv_out_proj_w': _L2_conv_in['out_proj_w'], 'L2_conv_out_proj_b': _L2_conv_in['out_proj_b'], 'L3_conv_in_proj_weight': _L3_conv_in['in_proj_weight'], 'L3_conv_out_proj_weight': _L3_conv_in['out_proj_weight'], 'L3_conv_x_proj_weight': _L3_conv_in['x_proj_weight'], 'L3_conv_dt_projs_weight': _L3_conv_in['dt_projs_weight'], 'L3_conv_dt_projs_bias': _L3_conv_in['dt_projs_bias'], 'L3_conv_A_logs': _L3_conv_in['A_logs'], 'L3_conv_Ds': _L3_conv_in['Ds'], 'L3_conv_out_norm_weight': _L3_conv_in['out_norm_weight'], 'L3_conv_out_norm_bias': _L3_conv_in['out_norm_bias']}

def reference(x, L0_conv_in_proj_weight, L0_conv_out_proj_weight, L0_conv_x_proj_weight, L0_conv_dt_projs_weight, L0_conv_dt_projs_bias, L0_conv_A_logs, L0_conv_Ds, L0_conv_out_norm_weight, L0_conv_out_norm_bias, L2_conv_in_proj_w, L2_conv_in_proj_b, L2_conv_conv_w, L2_conv_conv_b, L2_conv_x_proj_w, L2_conv_dt_proj_w, L2_conv_dt_proj_b, L2_conv_A_log, L2_conv_Ds, L2_conv_ln_g, L2_conv_ln_b, L2_conv_out_proj_w, L2_conv_out_proj_b, L3_conv_in_proj_weight, L3_conv_out_proj_weight, L3_conv_x_proj_weight, L3_conv_dt_projs_weight, L3_conv_dt_projs_bias, L3_conv_A_logs, L3_conv_Ds, L3_conv_out_norm_weight, L3_conv_out_norm_bias):
    import jax
    import jax.numpy as jnp

    def _L0_conv_ref(x, in_proj_weight, out_proj_weight, x_proj_weight, dt_projs_weight, dt_projs_bias, A_logs, Ds, out_norm_weight, out_norm_bias):
        import jax, jax.numpy as jnp
        import numpy as np
        D_MODEL = 96
        D_STATE = 16
        D_INNER = 192
        DT_RANK = 12
        K = 4
        B_, H_, W_ = (4, 32, 32)
        EPS = 1e-06

        def _selective_scan(u, delta, A, Bs, Cs, Ds, delta_bias):
            Bb, KD, L = u.shape
            N = A.shape[1]
            D = KD // K
            delta = jax.nn.softplus(delta + delta_bias[None, :, None])
            u_k = u.reshape(Bb, K, D, L)
            d_k = delta.reshape(Bb, K, D, L)
            A_k = A.reshape(K, D, N)

            def step(h, inp):
                dt, ut, bt, ct = inp
                dA = jnp.exp(dt[..., None] * A_k[None])
                dBu = dt[..., None] * bt[:, :, None, :] * ut[..., None]
                h = dA * h + dBu
                y = jnp.einsum('bkdn,bkn->bkd', h, ct)
                return (h, y)
            h0 = jnp.zeros((Bb, K, D, N), u.dtype)
            inps = (jnp.moveaxis(d_k, -1, 0), jnp.moveaxis(u_k, -1, 0), jnp.moveaxis(Bs, -1, 0), jnp.moveaxis(Cs, -1, 0))
            _, ys = jax.lax.scan(step, h0, inps)
            y = jnp.moveaxis(ys, 0, -1).reshape(Bb, KD, L)
            return y + u * Ds[None, :, None]
        Bb, H, W, C = x.shape
        L = H * W
        xz = jnp.einsum('bhwc,ec->bhwe', x, in_proj_weight)
        xin, z = jnp.split(xz, 2, axis=-1)
        xc = jnp.transpose(xin, (0, 3, 1, 2))
        x_hw = xc.reshape(Bb, D_INNER, L)
        x_wh = jnp.transpose(xc, (0, 1, 3, 2)).reshape(Bb, D_INNER, L)
        x_hwwh = jnp.stack([x_hw, x_wh], axis=1)
        xs = jnp.concatenate([x_hwwh, jnp.flip(x_hwwh, axis=-1)], axis=1)
        x_dbl = jnp.einsum('bkdl,kcd->bkcl', xs, x_proj_weight)
        dts = x_dbl[:, :, :DT_RANK]
        Bs = x_dbl[:, :, DT_RANK:DT_RANK + D_STATE]
        Cs = x_dbl[:, :, DT_RANK + D_STATE:]
        dts = jnp.einsum('bkrl,kdr->bkdl', dts, dt_projs_weight)
        As = -jnp.exp(A_logs)
        out_y = _selective_scan(xs.reshape(Bb, -1, L), dts.reshape(Bb, -1, L), As, Bs, Cs, Ds, dt_projs_bias.reshape(-1)).reshape(Bb, K, D_INNER, L)
        inv_y = jnp.flip(out_y[:, 2:4], axis=-1)
        wh_y = jnp.transpose(out_y[:, 1].reshape(Bb, D_INNER, W, H), (0, 1, 3, 2)).reshape(Bb, D_INNER, L)
        invwh_y = jnp.transpose(inv_y[:, 1].reshape(Bb, D_INNER, W, H), (0, 1, 3, 2)).reshape(Bb, D_INNER, L)
        y = out_y[:, 0] + inv_y[:, 0] + wh_y + invwh_y
        y4 = y.reshape(Bb, D_INNER, H, W)
        mu = y4.mean(1, keepdims=True)
        var = ((y4 - mu) ** 2).mean(1, keepdims=True)
        y4 = (y4 - mu) / jnp.sqrt(var + EPS)
        y4 = out_norm_weight[None, :, None, None] * y4 + out_norm_bias[None, :, None, None]
        y = jnp.transpose(y4, (0, 2, 3, 1))
        y = y * jax.nn.silu(z)
        return jnp.einsum('bhwd,cd->bhwc', y, out_proj_weight)

    def _L1_conv_ref(feature):
        import jax, jax.numpy as jnp
        import numpy as np
        G = 16
        K = 3
        B, C, H, W = feature.shape
        Cg = C // G
        Hm, Wm = (H - K + 1, W - K + 1)
        L = Hm * Wm
        slices = [feature[:, :, ki:ki + Hm, kj:kj + Wm] for ki in range(K) for kj in range(K)]
        patches = jnp.stack(slices, axis=2)
        motif = patches.reshape(B, G, Cg * 9, L).reshape(B, G, 9, Cg, L)
        gram = jnp.einsum('bgjcl,bgjdl->bgjcd', motif, motif)
        sq = jnp.einsum('bgjcl,bgjcl->bgjc', motif, motif)
        d2 = sq[..., :, None] + sq[..., None, :] - 2.0 * gram
        eye = jnp.eye(Cg, dtype=bool)
        d2 = jnp.where(eye, jnp.inf, d2)
        nn_idx = jnp.argmin(d2, axis=-1)
        u_max = jnp.max(nn_idx, axis=-1)
        c_max = jnp.sum(nn_idx == u_max[..., None], axis=-1).astype(feature.dtype)
        motif_nn = jnp.take_along_axis(motif, u_max[..., None, None], axis=3)
        term = jnp.floor(motif * motif_nn * c_max[..., None, None] / Cg)
        batch_mask = (jnp.arange(B) != 0).astype(feature.dtype).reshape(B, 1, 1, 1, 1)
        out_ser = motif * batch_mask + term
        ser2 = out_ser.reshape(B, G, 9 * Cg, L).reshape(B, G, Cg, 9, Hm, Wm)
        out = jnp.zeros((B, G, Cg, H, W), feature.dtype)
        for k in range(K * K):
            ki, kj = (k // K, k % K)
            out = out.at[:, :, :, ki:ki + Hm, kj:kj + Wm].add(ser2[:, :, :, k])
        return out.reshape(B, C, H, W)

    def _L2_conv_ref(x, in_proj_w, in_proj_b, conv_w, conv_b, x_proj_w, dt_proj_w, dt_proj_b, A_log, Ds, ln_g, ln_b, out_proj_w, out_proj_b):
        import jax, jax.numpy as jnp
        import numpy as np
        D_MODEL = 96
        D_STATE = 16
        D_CONV = 3
        EXPAND = 2
        D_INNER = EXPAND * D_MODEL
        DT_RANK = -(-D_MODEL // 16)
        B, H, W = (2, 32, 32)
        b, h, w, _ = x.shape
        L = h * w
        xz = x @ in_proj_w.T + in_proj_b
        xin, z = jnp.split(xz, 2, axis=-1)
        xc = jnp.transpose(xin, (0, 3, 1, 2))
        pad = (D_CONV - 1) // 2
        xc = jax.lax.conv_general_dilated(xc, conv_w, window_strides=(1, 1), padding=((pad, pad), (pad, pad)), feature_group_count=D_INNER, dimension_numbers=('NCHW', 'OIHW', 'NCHW'))
        xc = jax.nn.silu(xc + conv_b[None, :, None, None])
        u = xc.reshape(b, D_INNER, L)
        x_dbl = jnp.einsum('bdl,kd->blk', u, x_proj_w)
        dt, Bv, Cv = jnp.split(x_dbl, [DT_RANK, DT_RANK + D_STATE], axis=-1)
        dt = jnp.einsum('blr,dr->bdl', dt, dt_proj_w)
        A = -jnp.exp(A_log)
        delta = jax.nn.softplus(dt + dt_proj_b[None, :, None])
        dA = jnp.exp(jnp.einsum('bdl,dn->lbdn', delta, A))
        dBu = jnp.einsum('bdl,bln->lbdn', delta * u, Bv)

        def step(hst, inp):
            dA_t, dBu_t = inp
            hst = dA_t * hst + dBu_t
            return (hst, hst)
        h0 = jnp.zeros((b, D_INNER, D_STATE), x.dtype)
        _, hs = jax.lax.scan(step, h0, (dA, dBu))
        y = jnp.einsum('lbdn,bln->bdl', hs, Cv) + u * Ds[None, :, None]
        y = jnp.transpose(y, (0, 2, 1)).reshape(b, h, w, D_INNER)
        mu = y.mean(-1, keepdims=True)
        var = y.var(-1, keepdims=True)
        y = (y - mu) * jax.lax.rsqrt(var + 1e-05) * ln_g + ln_b
        y = y * jax.nn.silu(z)
        return y @ out_proj_w.T + out_proj_b

    def _L3_conv_ref(x, in_proj_weight, out_proj_weight, x_proj_weight, dt_projs_weight, dt_projs_bias, A_logs, Ds, out_norm_weight, out_norm_bias):
        import jax, jax.numpy as jnp
        import numpy as np
        D_MODEL = 96
        D_STATE = 16
        D_INNER = 192
        DT_RANK = 12
        K = 4
        B_, H_, W_ = (4, 32, 32)
        EPS = 1e-06

        def _selective_scan(u, delta, A, Bs, Cs, Ds, delta_bias):
            Bb, KD, L = u.shape
            N = A.shape[1]
            D = KD // K
            delta = jax.nn.softplus(delta + delta_bias[None, :, None])
            u_k = u.reshape(Bb, K, D, L)
            d_k = delta.reshape(Bb, K, D, L)
            A_k = A.reshape(K, D, N)

            def step(h, inp):
                dt, ut, bt, ct = inp
                dA = jnp.exp(dt[..., None] * A_k[None])
                dBu = dt[..., None] * bt[:, :, None, :] * ut[..., None]
                h = dA * h + dBu
                y = jnp.einsum('bkdn,bkn->bkd', h, ct)
                return (h, y)
            h0 = jnp.zeros((Bb, K, D, N), u.dtype)
            inps = (jnp.moveaxis(d_k, -1, 0), jnp.moveaxis(u_k, -1, 0), jnp.moveaxis(Bs, -1, 0), jnp.moveaxis(Cs, -1, 0))
            _, ys = jax.lax.scan(step, h0, inps)
            y = jnp.moveaxis(ys, 0, -1).reshape(Bb, KD, L)
            return y + u * Ds[None, :, None]
        Bb, H, W, C = x.shape
        L = H * W
        xz = jnp.einsum('bhwc,ec->bhwe', x, in_proj_weight)
        xin, z = jnp.split(xz, 2, axis=-1)
        xc = jnp.transpose(xin, (0, 3, 1, 2))
        x_hw = xc.reshape(Bb, D_INNER, L)
        x_wh = jnp.transpose(xc, (0, 1, 3, 2)).reshape(Bb, D_INNER, L)
        x_hwwh = jnp.stack([x_hw, x_wh], axis=1)
        xs = jnp.concatenate([x_hwwh, jnp.flip(x_hwwh, axis=-1)], axis=1)
        x_dbl = jnp.einsum('bkdl,kcd->bkcl', xs, x_proj_weight)
        dts = x_dbl[:, :, :DT_RANK]
        Bs = x_dbl[:, :, DT_RANK:DT_RANK + D_STATE]
        Cs = x_dbl[:, :, DT_RANK + D_STATE:]
        dts = jnp.einsum('bkrl,kdr->bkdl', dts, dt_projs_weight)
        As = -jnp.exp(A_logs)
        out_y = _selective_scan(xs.reshape(Bb, -1, L), dts.reshape(Bb, -1, L), As, Bs, Cs, Ds, dt_projs_bias.reshape(-1)).reshape(Bb, K, D_INNER, L)
        inv_y = jnp.flip(out_y[:, 2:4], axis=-1)
        wh_y = jnp.transpose(out_y[:, 1].reshape(Bb, D_INNER, W, H), (0, 1, 3, 2)).reshape(Bb, D_INNER, L)
        invwh_y = jnp.transpose(inv_y[:, 1].reshape(Bb, D_INNER, W, H), (0, 1, 3, 2)).reshape(Bb, D_INNER, L)
        y = out_y[:, 0] + inv_y[:, 0] + wh_y + invwh_y
        y4 = y.reshape(Bb, D_INNER, H, W)
        mu = y4.mean(1, keepdims=True)
        var = ((y4 - mu) ** 2).mean(1, keepdims=True)
        y4 = (y4 - mu) / jnp.sqrt(var + EPS)
        y4 = out_norm_weight[None, :, None, None] * y4 + out_norm_bias[None, :, None, None]
        y = jnp.transpose(y4, (0, 2, 3, 1))
        y = y * jax.nn.silu(z)
        return jnp.einsum('bhwd,cd->bhwc', y, out_proj_weight)

    def _gn(v, G=32, eps=1e-05):
        B_, H_, W_, C_ = v.shape
        g = v.reshape(B_, H_, W_, G, C_ // G)
        m = jnp.mean(g, axis=(1, 2, 4), keepdims=True)
        s = jnp.var(g, axis=(1, 2, 4), keepdims=True)
        return ((g - m) / jnp.sqrt(s + eps)).reshape(v.shape)

    def _ln_c(v, eps=1e-06):
        m = jnp.mean(v, axis=-1, keepdims=True)
        s = jnp.var(v, axis=-1, keepdims=True)
        return (v - m) / jnp.sqrt(s + eps)

    def _ln_t(v, eps=1e-05):
        m = jnp.mean(v, axis=-1, keepdims=True)
        s = jnp.var(v, axis=-1, keepdims=True)
        return (v - m) / jnp.sqrt(s + eps)

    def _to_tokens(v):
        B_, H_, W_, C_ = v.shape
        return v.reshape(B_, H_ * W_, C_)

    def _from_tokens(t, like):
        return t.reshape(like.shape)
    x = x + _L0_conv_ref(_gn(x), L0_conv_in_proj_weight, L0_conv_out_proj_weight, L0_conv_x_proj_weight, L0_conv_dt_projs_weight, L0_conv_dt_projs_bias, L0_conv_A_logs, L0_conv_Ds, L0_conv_out_norm_weight, L0_conv_out_norm_bias)
    x = x + _L1_conv_ref(_gn(x))
    x = x + _L2_conv_ref(_gn(x), L2_conv_in_proj_w, L2_conv_in_proj_b, L2_conv_conv_w, L2_conv_conv_b, L2_conv_x_proj_w, L2_conv_dt_proj_w, L2_conv_dt_proj_b, L2_conv_A_log, L2_conv_Ds, L2_conv_ln_g, L2_conv_ln_b, L2_conv_out_proj_w, L2_conv_out_proj_b)
    x = x + _L3_conv_ref(_gn(x), L3_conv_in_proj_weight, L3_conv_out_proj_weight, L3_conv_x_proj_weight, L3_conv_dt_projs_weight, L3_conv_dt_projs_bias, L3_conv_A_logs, L3_conv_Ds, L3_conv_out_norm_weight, L3_conv_out_norm_bias)
    return x

_drawn_inputs = setup_inputs


def setup_inputs(seed=0):
    import zlib

    import numpy as np

    out = dict(_drawn_inputs(seed))
    spreads = {'L0_conv_Ds': (1.0, 0.2),
     'L0_conv_out_norm_weight': (1.0, 0.2),
     'L0_conv_out_norm_bias': (0.0, 0.1),
     'L2_conv_in_proj_b': (0.0, 0.778),
     'L2_conv_conv_b': (0.0, 0.8),
     'L2_conv_Ds': (1.0, 0.6),
     'L2_conv_ln_g': (1.0, 0.6),
     'L2_conv_ln_b': (0.0, 0.8),
     'L2_conv_out_proj_b': (0.0, 0.745),
     'L3_conv_Ds': (1.0, 0.6),
     'L3_conv_out_norm_weight': (1.0, 0.6),
     'L3_conv_out_norm_bias': (0.0, 0.8)}
    factors = {'L0_conv_dt_projs_weight': 19.771,
     'L0_conv_dt_projs_bias': 10.418,
     'L0_conv_A_logs': 15.288,
     'L2_conv_x_proj_w': 7.642,
     'L2_conv_dt_proj_w': 8.0,
     'L2_conv_dt_proj_b': 8.0,
     'L2_conv_A_log': 8.0,
     'L3_conv_x_proj_weight': 8.0,
     'L3_conv_dt_projs_weight': 8.0,
     'L3_conv_dt_projs_bias': 8.0,
     'L3_conv_A_logs': 8.0,
     'L0_conv_x_proj_weight': 4.045}
    for name, (base, spread) in spreads.items():
        noise = np.random.default_rng([zlib.crc32(name.encode()), seed]).standard_normal(out[name].shape)
        drawn = base * np.exp(spread * noise) if base else spread * noise
        out[name] = jnp.asarray(drawn.astype(out[name].dtype))
    for name, factor in factors.items():
        out[name] = (out[name] * factor).astype(out[name].dtype)
    return out
```

```python
from contextlib import ExitStack, contextmanager

import concourse.bass as bass
from concourse import mybir

F32 = mybir.dt.float32
BF16 = mybir.dt.bfloat16
ALU = mybir.AluOpType
ACT = mybir.ActivationFunctionType

B, H, W, C = 4, 32, 32, 96
L = H * W
DI = 192
NS = 16
HALF = 512
BLK = 64
NBLK = DI // BLK
NP = NS // 2
RING = 3
ROUND = 12582912.0
GN_EPS = 1e-5


def halves():
    return [(i, slice(i * HALF, (i + 1) * HALF)) for i in range(L // HALF)]


@contextmanager
def cleared(nc):
    sems = []
    with ExitStack() as ctx:
        yield ctx, sems
    nc.clear_and_free_semaphores(sems)
    nc.all_engine_barrier()


def group_norm(nc, name, x_cm, g_cm, group_mean):
    with cleared(nc) as (ctx, sems):
        def sb(n, shape):
            return ctx.enter_context(nc.sbuf_tensor(f"{name}_{n}", shape, F32))

        def sem(n):
            sems.append(nc.alloc_semaphore(name=f"{name}_{n}"))
            return sems[-1]

        stats = sb("stats", [C, B, 2, 6])
        mv = sb("mv", [C, B, 2])
        spread = sb("spread", [C, B])
        mean = sb("mean", [C, B])
        vare = sb("vare", [C, B])
        logv = sb("logv", [C, B])
        rstd = sb("rstd", [C, B])
        newton = sb("newton", [C, B])
        eps = sb("eps", [C, 1])
        ps = ctx.enter_context(nc.psum_tensor(f"{name}_ps", [C, 2, HALF], F32))
        dve_step, means_ready, vars_ready, logs, roots = (
            sem(s) for s in ("dve_step", "means_ready", "vars_ready", "logs", "roots"))
        block = ctx.enter_context(nc.Block())
        n_stats = 2 * B + B + 1

        @block.vector
        def _(dve):
            done = [0]

            def chained(ins):
                done[0] += 1
                ins.then_inc(dve_step, 1)
                dve.wait_ge(dve_step, done[0])

            for b in range(B):
                for i in range(2):
                    chained(nc.vector.bn_stats(stats[:, b, i, :], x_cm[:, b * L + i * HALF:b * L + (i + 1) * HALF]))
                chained(nc.vector.bn_aggr(mv[:, b, :], stats[:, b, :, :]))
            chained(nc.vector.memset(eps[:, :], GN_EPS))
            dve.wait_ge(means_ready, 1)
            chained(nc.vector.tensor_copy(mean[:, :], ps[:, 0, 0:B]))
            chained(nc.vector.tensor_tensor(spread[:, :], mv[:, :, 0], mean[:, :], ALU.subtract))
            chained(nc.vector.tensor_tensor(spread[:, :], spread[:, :], spread[:, :], ALU.mult))
            chained(nc.vector.tensor_tensor(spread[:, :], spread[:, :], mv[:, :, 1], ALU.add))
            dve.wait_ge(vars_ready, 1)
            chained(nc.vector.tensor_scalar(vare[:, :], ps[:, 1, 0:B], GN_EPS, None, ALU.add))
            dve.wait_ge(roots, 1)
            chained(nc.vector.tensor_tensor(newton[:, :], rstd[:, :], rstd[:, :], ALU.mult))
            chained(nc.vector.tensor_tensor(newton[:, :], newton[:, :], vare[:, :], ALU.mult))
            chained(nc.vector.tensor_scalar(newton[:, :], newton[:, :], -0.5, 1.5, ALU.mult, ALU.add))
            chained(nc.vector.tensor_tensor(rstd[:, :], rstd[:, :], newton[:, :], ALU.mult))
            for b in range(B):
                chained(nc.vector.tensor_scalar(g_cm[:, b * L:(b + 1) * L], x_cm[:, b * L:(b + 1) * L],
                                                mean[:, b:b + 1], rstd[:, b:b + 1], ALU.subtract, ALU.mult))

        @block.tensor
        def _(pe):
            pe.wait_ge(dve_step, n_stats)
            nc.tensor.matmul(ps[:, 0, 0:B], group_mean, mv[:, :, 0], start=True, stop=True).then_inc(means_ready, 1)
            pe.wait_ge(dve_step, n_stats + 4)
            nc.tensor.matmul(ps[:, 1, 0:B], group_mean, spread[:, :], start=True, stop=True).then_inc(vars_ready, 1)

        @block.scalar
        def _(act):
            act.wait_ge(dve_step, n_stats + 5)
            nc.scalar.activation(logv[:, :], vare[:, :], ACT.Ln).then_inc(logs, 1)
            act.wait_ge(logs, 1)
            nc.scalar.activation(rstd[:, :], logv[:, :], ACT.Exp, scale=-0.5).then_inc(roots, 1)


def motif_layer(nc, x_cm, g_cm, ident, cols):
    with cleared(nc) as (ctx, sems):
        def sb(n, shape=(128, W, C)):
            return ctx.enter_context(nc.sbuf_tensor(f"motif_{n}", list(shape), F32))

        def sem(n):
            sems.append(nc.alloc_semaphore(name=f"motif_{n}"))
            return sems[-1]

        f, below, base, own, right, diag, cross, acc, val, rnd = (
            sb(n) for n in ("f", "below", "base", "own", "right", "diag", "cross", "acc", "val", "rnd"))
        ps = ctx.enter_context(nc.psum_tensor("motif_ps", [128, 8, HALF], F32))
        turned, f_ready, below_ready, dve_step, back, added = (
            sem(s) for s in ("turned", "f_ready", "below_ready", "dve_step", "back", "added"))
        block = ctx.enter_context(nc.Block())
        g_v = g_cm.rearrange("p (q w) -> p q w", w=W)
        x_v = x_cm.rearrange("p (q w) -> p q w", w=W)
        per_bank, back_bank = 5, 4
        banks_in = -(-W // per_bank)
        banks_out = W // back_bank
        motif_steps = 2 + 4 * 5 + 9 * 3

        @block.tensor
        def _(pe):
            for k in range(banks_in):
                ws = range(k * per_bank, min((k + 1) * per_bank, W))
                if k >= 8:
                    pe.wait_ge(f_ready, k - 7)
                for j, w in enumerate(ws):
                    t = nc.tensor.transpose(ps[:, k % 8, j * C:(j + 1) * C], g_v[:, :, w], ident[0:C, 0:C])
                t.then_inc(turned, 1)
            pe.wait_ge(dve_step, motif_steps)
            pe.wait_ge(f_ready, banks_in)
            for k in range(banks_out):
                for j in range(back_bank):
                    t = nc.tensor.transpose(ps[0:C, k % 8, j * 128:(j + 1) * 128], acc[:, k * back_bank + j, :], ident)
                t.then_inc(back, 1)

        @block.scalar
        def _(act):
            for k in range(banks_in):
                a, z = k * per_bank, min((k + 1) * per_bank, W)
                act.wait_ge(turned, k + 1)
                nc.scalar.copy(f[:, a:z, :], ps[:, k % 8, 0:(z - a) * C]).then_inc(f_ready, 1)

        @block.sync
        def _(sp):
            sp.wait_ge(below_ready, 1)
            sp.wait_ge(f_ready, banks_in)
            sp.dma_start(below[0:127, :, :], f[1:128, :, :]).then_inc(below_ready, 16)

        even, odd, mask = cols[:, 0:1], cols[:, 1:2], cols[:, 2:3]
        R, S = H - 2, C - 2

        @block.vector
        def _(dve):
            done = [0]

            def chained(ins):
                done[0] += 1
                ins.then_inc(dve_step, 1)
                dve.wait_ge(dve_step, done[0])

            def floored(dst, a, b, rows, chans):
                d, v, r = (t[:, rows, chans] for t in (dst, val, rnd))
                chained(nc.vector.scalar_tensor_tensor(out=v, in0=a, scalar=0.5, in1=b, op0=ALU.mult, op1=ALU.mult))
                chained(nc.vector.tensor_scalar(r, v, ROUND, None, ALU.add))
                chained(nc.vector.tensor_scalar(r, r, ROUND, None, ALU.subtract))
                chained(nc.vector.tensor_tensor(v, r, v, ALU.is_gt))
                chained(nc.vector.tensor_tensor(d, r, v, ALU.subtract))

            nc.vector.memset(below[:, :, :], 0.0).then_inc(below_ready, 1)
            dve.wait_ge(f_ready, banks_in)
            chained(nc.vector.memset(acc[:, :, :], 0.0))
            chained(nc.vector.tensor_scalar(base[:, :, :], f[:, :, :], mask, None, ALU.mult))
            floored(own, f[:, :, :], f[:, :, :], slice(0, W), slice(0, C))
            floored(right, f[:, :, 0:C - 1], f[:, :, 1:C], slice(0, W), slice(0, C - 1))
            floored(diag, f[:, 0:W - 1, 2:C], f[:, 1:W, 0:C - 2], slice(0, W - 1), slice(2, C))
            dve.wait_ge(below_ready, 17)
            floored(cross, f[:, 2:W, 2:C], below[:, 0:W - 2, 0:C - 2], slice(2, W), slice(2, C))
            partner = [(right, own), (own, right), (diag, own), (own, right), (right, own), (own, diag),
                       (right, own), (own, right), (cross, own)]
            for k, (pe_, po_) in enumerate(partner):
                ki, kj = divmod(k, 3)
                at = (slice(None), slice(ki, ki + R), slice(kj, kj + S))
                chained(nc.vector.scalar_tensor_tensor(out=val[at], in0=pe_[at], scalar=even, in1=base[at],
                                                       op0=ALU.mult, op1=ALU.add))
                chained(nc.vector.scalar_tensor_tensor(out=val[at], in0=po_[at], scalar=odd, in1=val[at],
                                                       op0=ALU.mult, op1=ALU.add))
                chained(nc.vector.tensor_tensor(acc[at], acc[at], val[at], ALU.add))
            assert done[0] == motif_steps
            for k in range(banks_out):
                dve.wait_ge(back, k + 1)
                xs = x_v[:, :, k * back_bank:(k + 1) * back_bank].rearrange("p q w -> p w q")
                nc.vector.tensor_tensor(xs, xs, ps[0:C, k % 8, :].rearrange("p (w q) -> p w q", w=back_bank),
                                        ALU.add).then_inc(added, 1)


class Uses:

    def __init__(self, keys):
        self.index = {k: i for i, (k, _) in enumerate(keys)}
        self.buf = dict(keys)
        self.nth, count = {}, [0, 0]
        for k, b in keys:
            self.nth[k] = count[b]
            count[b] += 1
        self.count, self.total = count, len(keys)


def scan_layer(nc, name, x_cm, g_cm, ident, cols_e, hbm, orders, dirs, rank, conv, eps):
    NJ = -(-dirs * NBLK // 2)
    NT = dirs * NP * NBLK
    RANKS = dirs * rank
    rows_of = [min(128, dirs * DI - 128 * j) for j in range(NJ)]
    with cleared(nc) as (ctx, sems):
        def sb(n, shape, dt=F32):
            return ctx.enter_context(nc.sbuf_tensor(f"{name}_{n}", shape, dt))

        def sem(n):
            sems.append(nc.alloc_semaphore(name=f"{name}_{n}"))
            return sems[-1]

        w_u = sb("w_u", [C, 2 * DI])
        w_z = sb("w_z", [C, 256])
        w_bc_a = sb("w_bc_a", [128, orders * dirs, 128])
        w_bc_b = sb("w_bc_b", [BLK, orders * dirs, 128])
        w_r_a = sb("w_r_a", [128, orders, RANKS])
        w_r_b = sb("w_r_b", [BLK, orders, RANKS])
        w_dt = sb("w_dt", [RANKS, orders, 128 * NJ])
        dt_bias = sb("dt_bias", [128, orders, NJ])
        a_neg = sb("a_neg", [128, orders * dirs, NBLK, NP])
        skip_w = sb("skip_w", [128, orders, dirs, 2])
        skip_sum = sb("skip_sum", [128, orders, 2])
        skip_diag = sb("skip_diag", [128, orders, 2, 128])
        norm_w = sb("norm_w", [128, 2, 2])
        w_o_a = sb("w_o_a", [128, C])
        w_o_b = sb("w_o_b", [BLK, C])
        pick = sb("pick", [128, 2 * NS, BLK], BF16)
        fold = sb("fold", [128, 3 * BLK])
        mean_w = sb("mean_w", [128, 128])
        eps_col = sb("eps_col", [128, 1])
        loads = [(w_u, "w_u"), (w_z, "w_z"), (w_bc_a, "w_bc_a"), (w_bc_b, "w_bc_b"), (w_r_a, "w_r_a"),
                 (w_r_b, "w_r_b"), (w_dt, "w_dt"), (dt_bias, "dt_bias"), (a_neg, "a_logs"), (skip_w, "skip"),
                 (norm_w, "norm"), (w_o_a, "w_o_a"), (w_o_b, "w_o_b")]
        if conv:
            conv_w = sb("conv_w", [128, 2, 9])
            in_bias = sb("in_bias", [128, 2, 2])
            conv_b = sb("conv_b", [128, 2])
            out_bias = sb("out_bias", [C, 1])
            padded = sb("padded", [128, 2, H + 2, W + 2])
            conved = sb("conved", [128, 2, L])
            loads += [(conv_w, "conv_w"), (in_bias, "in_bias"), (conv_b, "conv_b"), (out_bias, "out_bias")]

        u = sb("u", [128, NJ, L])
        ranks = sb("ranks", [RANKS, L])
        bc = sb("bc", [128, dirs, L], BF16)
        sp_e, sp_l, sp_r, sp_w = (sb(n, [128, L]) for n in ("sp_e", "sp_l", "sp_r", "sp_w"))
        rest = sp_r
        delta = sb("delta", [128, NJ, L])
        du = sb("du", [128, NJ, L])
        delta2 = sb("delta2", [128, dirs * NBLK, L])
        du2 = sb("du2", [128, dirs * NBLK, L])
        decay = sb("decay", [128, 2, L])
        state = sb("state", [128, RING, L])
        read = sb("read", [128, RING, L])
        c_rows = sb("c_rows", [128, 2, L])
        y_a = sb("y_a", [128, L])
        y_b = sb("y_b", [BLK, L])

        y_ps = ctx.enter_context(nc.psum_tensor(f"{name}_y_ps", [128, 3, HALF], F32))
        work0 = ctx.enter_context(nc.psum_tensor(f"{name}_work0", [128, L], F32))
        work1 = ctx.enter_context(nc.psum_tensor(f"{name}_work1", [128, L], F32))
        c_ps = ctx.enter_context(nc.psum_tensor(f"{name}_c_ps", [128, HALF], F32))
        work = [work0, work1]
        inject_ps, b_ps = work0, work1
        y_flat = y_ps[:, 0:2, :].rearrange("p a n -> p (a n)")

        (weights, w_used, set_up, consts, conv_padded, conv_step, conved_s, u_ready, ranks_ready, bc_hi, bc_rest, bc_mid,
         bc_ready, sp_abs, sp_exp, sp_one, sp_log, sp_step, decay_ready, scanned, injected, b_ready, c_ready, c_copied,
         multiplied, y_added, y_free, y_out, y_summed, centred, squared, logged, rooted, scaled, affine, gated,
         silued, z_done, x_added, ctx_done) = (
            sem(s) for s in (
                "weights", "w_used", "set_up", "consts", "conv_padded", "conv_step", "conved", "u_ready", "ranks_ready",
                "bc_hi", "bc_rest", "bc_mid", "bc_ready", "sp_abs", "sp_exp", "sp_one", "sp_log", "sp_step", "decay_ready",
                "scanned", "injected", "b_ready", "c_ready", "c_copied", "multiplied", "y_added", "y_free", "y_out",
                "y_summed", "centred", "squared", "logged", "rooted", "scaled", "affine", "gated", "silued", "z_done",
                "x_added", "ctx_done"))
        work_ready = sem("work_ready")
        work_free = [sem("work_free0"), sem("work_free1")]
        delta2_in = [sem(f"delta2_in{d}") for d in range(dirs)]
        du2_in = [sem(f"du2_in{d}") for d in range(dirs)]

        keys = []
        for o in range(orders):
            seq = [("u", o, j) for j in range(2 if conv else NJ)] + [("ranks", o, 0)]
            seq += [("bc", o, d) for d in range(dirs)] + [("dt", o, j) for j in range(NJ)]
            keys += [(k, i % 2) for i, k in enumerate(seq)]
        keys += [(("mean", 0, 0), 0), (("var", 0, 0), 1), (("z", 0, 0), 0), (("z", 0, 1), 1), (("out", 0, 0), 0)]
        uses = Uses(keys)

        def wait_work(eng, b, key):
            eng.wait_ge(work_ready, b * uses.total + uses.index[key] + 1)

        def free_work(ins, key):
            ins.then_inc(work_free[uses.buf[key]], 1)

        def turn(b, o):
            return b * orders + o

        block = ctx.enter_context(nc.Block())
        tiles = [(d, p, c) for d in range(dirs) for p in range(NP) for c in range(NBLK)]
        n_setup = 2 + orders * (1 + 2) + 2 * NS + 3 + 1 + (1 if conv else 0)

        @block.sync
        def _(sp):
            for t, key in loads:
                sp.dma_start(t[tuple(slice(None) for _ in t.shape)], hbm[key]).then_inc(weights, 16)
            with sp.Fori(0, B) as b:
                for o in range(orders):
                    it = turn(b, o)
                    sp.wait_ge(y_added, it * NT + RING)
                    for q in range(dirs * NBLK):
                        j, half = q // 2, q % 2
                        rows = slice(half * BLK, half * BLK + BLK)
                        sp.wait_ge(sp_step, (it * NJ + j) * 4 + 4)
                        for side in range(2):
                            to = slice(side * BLK, side * BLK + BLK)
                            sp.dma_start(delta2[to, q, :], delta[rows, j, :]).then_inc(delta2_in[q // NBLK], 16)
                            sp.dma_start(du2[to, q, :], du[rows, j, :]).then_inc(du2_in[q // NBLK], 16)

        @block.tensor
        def _(pe):
            pe.wait_ge(weights, 16 * len(loads))
            pe.wait_ge(set_up, n_setup)

            with pe.Fori(0, B) as b:
                def claim(key):
                    k = uses.buf[key]
                    pe.wait_ge(work_free[k], b * uses.count[k] + uses.nth[key] + 1)
                    return work[k]

                def product(key, rows, parts):
                    dst = claim(key)
                    for i, s in halves():
                        for n, (lhs, rhs) in enumerate(parts):
                            m = nc.tensor.matmul(dst[0:rows, s], lhs, rhs(i, s), start=(n == 0),
                                                 stop=(n == len(parts) - 1))
                    m.then_inc(work_ready, 1)

                def g_half(o):
                    img = g_cm[:, bass.ts(b, L)]
                    if o == 0:
                        return lambda i, s: img[:, s]
                    turned = img.rearrange("p (h w) -> p w h", w=W)
                    return lambda i, s: turned[:, i * (W // 2):(i + 1) * (W // 2), :]

                for o in range(orders):
                    it = turn(b, o)
                    for j in range(2 if conv else NJ):
                        product(("u", o, j), 128, [(w_u[:, j * 128:(j + 1) * 128], g_half(o))])
                    pe.wait_ge(u_ready, it * NJ + NJ)
                    u_parts = (lambda i, s: u[:, 0, s], lambda i, s: u[0:BLK, 1, s])
                    product(("ranks", o, 0), RANKS, [(w_r_a[:, o, :], u_parts[0]), (w_r_b[:, o, :], u_parts[1])])
                    for d in range(dirs):
                        product(("bc", o, d), 128, [(w_bc_a[:, o * dirs + d, :], u_parts[0]),
                                                    (w_bc_b[:, o * dirs + d, :], u_parts[1])])
                    pe.wait_ge(ranks_ready, it + 1)
                    for j in range(NJ):
                        product(("dt", o, j), rows_of[j], [(w_dt[:, o, j * 128:j * 128 + rows_of[j]],
                                                            lambda i, s: ranks[:, s])])
                    pe.wait_ge(y_free, it + 1)
                    for i, s in halves():
                        nc.tensor.matmul(y_ps[:, i, :], skip_diag[:, o, 0, :], u[:, 0, s], start=True, stop=False)
                    for i, s in halves():
                        nc.tensor.matmul(y_ps[i * BLK:(i + 1) * BLK, 2, :], skip_diag[0:BLK, o, 1, 0:BLK],
                                         u[0:BLK, 1, s], start=True, stop=False, skip_group_check=True)

                    def spread_rows(g, d, p):
                        G = it * dirs * NP + g
                        pe.wait_ge(bc_ready, it * dirs + d + 1)
                        pe.wait_ge(injected, G * NBLK + 1)
                        for i, s in halves():
                            m = nc.tensor.matmul(b_ps[:, s], pick[:, 2 * p:2 * p + 2, :], bc[:, d, s],
                                                 start=True, stop=True)
                        m.then_inc(b_ready, 1)
                        for i, s in halves():
                            pe.wait_ge(c_copied, G * 2 + i + 1)
                            nc.tensor.matmul(c_ps[:, :], pick[:, NS + 2 * p:NS + 2 * p + 2, :], bc[:, d, s],
                                             start=True, stop=True).then_inc(c_ready, 1)

                    def sum_states(t, c):
                        pe.wait_ge(multiplied, it * NT + t + 1 + RING + 1)
                        for i, s in halves():
                            src = read[:, t % RING, s]
                            if c < 2:
                                lhs = fold[:, BLK * (1 - c):BLK * (1 - c) + 128]
                                m = nc.tensor.matmul(y_ps[:, i, :], lhs, src, start=False, stop=(t == NT - 2))
                            else:
                                m = nc.tensor.matmul(y_ps[i * BLK:(i + 1) * BLK, 2, :], fold[:, BLK:2 * BLK], src,
                                                     start=False, stop=(t == NT - 1), skip_group_check=True)
                        m.then_inc(y_added, 1)

                    for k in range(2):
                        last = [key for key in uses.buf if uses.buf[key] == k and key[1] == o and
                                key[0] in ("u", "ranks", "bc", "dt")][-1]
                        pe.wait_ge(work_free[k], b * uses.count[k] + uses.nth[last] + 2)
                    spread_rows(0, 0, 0)
                    for t, (d, p, c) in enumerate(tiles):
                        if c == 1 and t // NBLK + 1 < dirs * NP:
                            g = t // NBLK + 1
                            spread_rows(g, g // NP, g % NP)
                        sum_states(t, c)

                pe.wait_ge(y_summed, b + 1)
                product(("mean", 0, 0), 128, [(mean_w[:, :], lambda i, s: y_a[:, s]),
                                              (mean_w[0:BLK, :], lambda i, s: y_b[:, s])])
                pe.wait_ge(squared, b * 2 + 2)
                product(("var", 0, 0), 128, [(mean_w[:, :], lambda i, s: sp_e[:, s]),
                                             (mean_w[0:BLK, :], lambda i, s: sp_l[0:BLK, s])])
                product(("z", 0, 0), 128, [(w_z[:, 0:128], g_half(0))])
                product(("z", 0, 1), 128, [(w_z[:, 128:256], g_half(0))])
                pe.wait_ge(gated, b * 2 + 2)
                product(("out", 0, 0), C, [(w_o_a[:, :], lambda i, s: y_a[:, s]),
                                           (w_o_b[:, :], lambda i, s: y_b[:, s])])
                pe.wait_ge(x_added, b + 1)

        @block.scalar
        def _(act):
            act.wait_ge(weights, 16 * len(loads))
            nc.scalar.activation(a_neg[:, :, :, :], a_neg[:, :, :, :], ACT.Exp).then_inc(consts, 1)
            act.wait_ge(consts, 1)
            nc.scalar.mul(a_neg[:, :, :, :], a_neg[:, :, :, :], -1.0).then_inc(consts, 1)
            act.wait_ge(consts, 2)
            act.wait_ge(set_up, n_setup)
            with act.Fori(0, B) as b:
                for o in range(orders):
                    it = turn(b, o)
                    if conv:
                        for j in range(2):
                            r = rows_of[j]
                            wait_work(act, b, ("u", o, j))
                            ins = nc.scalar.activation(padded[0:r, j, 1:H + 1, 1:W + 1],
                                                       work[uses.buf[("u", o, j)]][0:r, :].rearrange(
                                                           "p (h w) -> p h w", w=W),
                                                       ACT.Identity, bias=in_bias[0:r, 0, j:j + 1])
                            free_work(ins, ("u", o, j))
                        for j in range(2):
                            r = rows_of[j]
                            act.wait_ge(conved_s, b * 18 + (j + 1) * 9)
                            nc.scalar.activation(u[0:r, j, :], conved[0:r, j, :], ACT.Silu,
                                                 bias=conv_b[0:r, j:j + 1]).then_inc(u_ready, 1)
                    else:
                        for j in range(NJ):
                            wait_work(act, b, ("u", o, j))
                            nc.scalar.copy(u[:, j, :], work[uses.buf[("u", o, j)]][:, :]).then_inc(u_ready, 1)
                            act.wait_ge(u_ready, it * NJ + j + 1)
                            act.sem_inc(work_free[uses.buf[("u", o, j)]], 1)
                    key = ("ranks", o, 0)
                    wait_work(act, b, key)
                    nc.scalar.copy(ranks[:, :], work[uses.buf[key]][0:RANKS, :]).then_inc(ranks_ready, 1)
                    act.wait_ge(ranks_ready, it + 1)
                    act.sem_inc(work_free[uses.buf[key]], 1)
                    for d in range(dirs):
                        key = ("bc", o, d)
                        wait_work(act, b, key)
                        nc.scalar.copy(bc[:, d, :], work[uses.buf[key]][:, :]).then_inc(bc_hi, 1)
                        act.wait_ge(bc_rest, it * dirs + d + 1)
                        nc.scalar.copy(bc[BLK:128, d, :], rest[BLK:128, :]).then_inc(bc_mid, 1)
                    for j in range(NJ):
                        key, r = ("dt", o, j), rows_of[j]
                        src, bias = work[uses.buf[key]][0:r, :], dt_bias[0:r, o, j:j + 1]
                        n = it * NJ + j
                        wait_work(act, b, key)
                        if j == 0:
                            act.wait_ge(bc_ready, (it + 1) * dirs)
                        else:
                            act.wait_ge(sp_step, n * 4)
                        nc.scalar.activation(sp_e[0:r, :], src, ACT.Abs, bias=bias).then_inc(sp_abs, 1)
                        free_work(nc.scalar.activation(sp_r[0:r, :], src, ACT.Relu, bias=bias), key)
                        act.wait_ge(sp_abs, n + 1)
                        nc.scalar.activation(sp_e[0:r, :], sp_e[0:r, :], ACT.Exp, scale=-1.0).then_inc(sp_exp, 1)
                        act.wait_ge(sp_exp, n + 1)
                        nc.scalar.activation(sp_w[0:r, :], sp_e[0:r, :], ACT.Identity, bias=1.0).then_inc(sp_one, 1)
                        act.wait_ge(sp_one, n + 1)
                        nc.scalar.activation(sp_l[0:r, :], sp_w[0:r, :], ACT.Ln).then_inc(sp_log, 1)

                    def copy_c(g):
                        G = it * dirs * NP + g
                        act.wait_ge(multiplied, G * NBLK + 1)
                        for i, s in halves():
                            act.wait_ge(c_ready, G * 2 + i + 1)
                            nc.scalar.copy(c_rows[:, g % 2, s], c_ps[:, :]).then_inc(c_copied, 1)

                    copy_c(0)
                    for t, (d, p, c) in enumerate(tiles):
                        if p == 0 and c == 0:
                            act.wait_ge(delta2_in[d], (it + 1) * 16 * 2 * NBLK)
                        act.wait_ge(scanned, it * NT + t + RING - 1)
                        nc.scalar.activation(decay[:, t % 2, :], delta2[:, d * NBLK + c, :], ACT.Exp,
                                             scale=a_neg[:, o * dirs + d, c, p:p + 1]).then_inc(decay_ready, 1)
                        if c == 2 and t + 1 < NT:
                            copy_c(t // NBLK + 1)
                    act.wait_ge(y_added, (it + 1) * NT + RING)
                    to_a, to_b = (y_a, y_b) if o == 0 else (sp_e, sp_l)
                    nc.scalar.copy(to_a[:, :], y_flat).then_inc(y_out, 1)
                    for i, s in halves():
                        ins = nc.scalar.copy(to_b[0:BLK, s], y_ps[i * BLK:(i + 1) * BLK, 2, :]).then_inc(y_out, 1)
                    act.wait_ge(y_out, 3 * (it + 1))
                    act.sem_inc(y_free, 1)

                act.wait_ge(centred, b * 2 + 2)
                nc.scalar.activation(sp_e[:, :], y_a[:, :], ACT.Square).then_inc(squared, 1)
                nc.scalar.activation(sp_l[0:BLK, :], y_b[:, :], ACT.Square).then_inc(squared, 1)
                key = ("var", 0, 0)
                wait_work(act, b, key)
                ins = nc.scalar.activation(sp_r[:, :], work[uses.buf[key]][:, :], ACT.Ln, bias=eps_col[:, :])
                ins.then_inc(logged, 1)
                act.wait_ge(logged, b + 1)
                act.sem_inc(work_free[uses.buf[key]], 1)
                nc.scalar.activation(sp_r[:, :], sp_r[:, :], ACT.Exp, scale=-0.5).then_inc(rooted, 1)
                act.wait_ge(scaled, b * 2 + 2)
                nc.scalar.activation(y_a[:, :], y_a[:, :], ACT.Identity, bias=norm_w[:, 1, 0:1],
                                     scale=norm_w[:, 0, 0:1]).then_inc(affine, 1)
                nc.scalar.activation(y_b[:, :], y_b[:, :], ACT.Identity, bias=norm_w[0:BLK, 1, 1:2],
                                     scale=norm_w[0:BLK, 0, 1:2]).then_inc(affine, 1)
                for j, (dst, r) in enumerate(((sp_w, 128), (sp_l, BLK))):
                    key = ("z", 0, j)
                    wait_work(act, b, key)
                    zb = in_bias[0:r, 1, j:j + 1] if conv else 0.0
                    nc.scalar.activation(dst[0:r, :], work[uses.buf[key]][0:r, :], ACT.Silu, bias=zb).then_inc(silued, 1)
                    act.wait_ge(silued, b * 2 + j + 1)
                    act.sem_inc(work_free[uses.buf[key]], 1)

        @block.gpsimd
        def _(pool):
            with pool.Fori(0, B) as b:
                for o in range(orders):
                    it = turn(b, o)
                    for t in range(NT):
                        g = t // NBLK
                        pool.wait_ge(scanned, it * NT + t + 1 + RING)
                        if t % NBLK == 0:
                            pool.wait_ge(c_copied, (it * dirs * NP + g) * 2 + 2 + 1)
                        pool.wait_ge(y_added, it * NT + t + 1)
                        nc.gpsimd.tensor_tensor(read[:, t % RING, :], state[:, t % RING, :], c_rows[:, g % 2, :],
                                                ALU.mult).then_inc(multiplied, 1)

        @block.vector
        def _(dve):
            for s, n in ((scanned, RING), (multiplied, RING + 1), (y_added, RING), (injected, 1), (c_copied, 1),
                         (y_free, 1), (work_free[0], 1), (work_free[1], 1)):
                for _ in range(n):
                    dve.sem_inc(s, 1)
            n = [0]

            def setup(ins):
                n[0] += 1
                ins.then_inc(set_up, 1)

            dve.wait_ge(weights, 16 * len(loads))
            setup(nc.vector.memset(mean_w[:, :], 1.0 / DI))
            setup(nc.vector.memset(eps_col[:, :], eps))
            for m in range(2 * NS):
                src = (m // NS) * NS + (m % NS) // 2 + NP * (m % 2)
                setup(nc.vector.tensor_copy(pick[:, m, :], cols_e[:, src:src + 1].to_broadcast([128, BLK])))
            for side, v in ((0, 0.0), (2, 0.0)):
                setup(nc.vector.memset(fold[:, side * BLK:(side + 1) * BLK], v))
            setup(nc.vector.tensor_tensor(fold[:, BLK:2 * BLK], ident[:, 0:BLK], ident[:, BLK:128], ALU.add))
            if conv:
                setup(nc.vector.memset(padded[:, :, :, :], 0.0))
            for o in range(orders):
                if dirs == 2:
                    setup(nc.vector.tensor_tensor(skip_sum[:, o, :], skip_w[:, o, 0, :], skip_w[:, o, 1, :], ALU.add))
                else:
                    setup(nc.vector.tensor_copy(skip_sum[:, o, :], skip_w[:, o, 0, :]))
            dve.wait_ge(set_up, n[0])
            for o in range(orders):
                for j in range(2):
                    setup(nc.vector.tensor_scalar(skip_diag[:, o, j, :], ident, skip_sum[:, o, j:j + 1], None,
                                                  ALU.mult))
            setup(nc.vector.memset(rest[:, :], 0.0))
            assert n[0] == n_setup
            dve.wait_ge(set_up, n_setup)

            with dve.Fori(0, B) as b:
                for o in range(orders):
                    it = turn(b, o)
                    if conv:
                        for j in range(2):
                            r = rows_of[j]
                            key = ("u", o, j)
                            acc = conved[0:r, j, :].rearrange("p (h w) -> p h w", w=W)
                            dve.wait_ge(work_free[uses.buf[key]], b * uses.count[uses.buf[key]] + uses.nth[key] + 2)
                            for k in range(9):
                                tap = padded[0:r, j, k // 3:k // 3 + H, k % 3:k % 3 + W]
                                wk = conv_w[0:r, j, k:k + 1]
                                if k == 0:
                                    ins = nc.vector.tensor_scalar(acc, tap, wk, None, ALU.mult)
                                else:
                                    dve.wait_ge(conved_s, b * 18 + j * 9 + k)
                                    ins = nc.vector.scalar_tensor_tensor(out=acc, in0=tap, scalar=wk, in1=acc,
                                                                         op0=ALU.mult, op1=ALU.add)
                                ins.then_inc(conved_s, 1)
                    for d in range(dirs):
                        key = ("bc", o, d)
                        dve.wait_ge(bc_hi, it * dirs + d + 1)
                        if d > 0:
                            dve.wait_ge(bc_ready, it * dirs + d)
                        nc.vector.tensor_tensor(rest[BLK:128, :], work[uses.buf[key]][BLK:128, :], bc[BLK:128, d, :],
                                                ALU.subtract).then_inc(bc_rest, 1)
                        dve.wait_ge(bc_rest, it * dirs + d + 1)
                        dve.sem_inc(work_free[uses.buf[key]], 1)
                        dve.wait_ge(bc_mid, it * dirs + d + 1)
                        nc.vector.tensor_tensor(bc[96:128, d, :], rest[96:128, :], bc[96:128, d, :],
                                                ALU.subtract).then_inc(bc_ready, 1)
                    for j in range(NJ):
                        r, n4 = rows_of[j], (it * NJ + j) * 4
                        e, l, w, dl = sp_e[0:r, :], sp_l[0:r, :], sp_w[0:r, :], delta[0:r, j, :]
                        dve.wait_ge(sp_log, it * NJ + j + 1)
                        nc.vector.scalar_tensor_tensor(out=w, in0=w, scalar=1.0, in1=l, op0=ALU.subtract,
                                                       op1=ALU.subtract).then_inc(sp_step, 1)
                        dve.wait_ge(sp_step, n4 + 1)
                        nc.vector.scalar_tensor_tensor(out=w, in0=w, scalar=0.0, in1=e, op0=ALU.max,
                                                       op1=ALU.subtract).then_inc(sp_step, 1)
                        dve.wait_ge(sp_step, n4 + 2)
                        nc.vector.tensor_tensor(dl, sp_r[0:r, :], w, ALU.subtract).then_inc(sp_step, 1)
                        dve.wait_ge(sp_step, n4 + 3)
                        nc.vector.tensor_tensor(du[0:r, j, :], dl, u[0:r, j, :], ALU.mult).then_inc(sp_step, 1)

                    for t, (d, p, c) in enumerate(tiles):
                        T = it * NT + t
                        if p == 0 and c == 0:
                            dve.wait_ge(du2_in[d], (it + 1) * 16 * 2 * NBLK)
                        if c == 0:
                            dve.wait_ge(b_ready, it * dirs * NP + t // NBLK + 1)
                        dve.wait_ge(scanned, T + RING)
                        nc.vector.tensor_tensor(inject_ps[:, :], du2[:, d * NBLK + c, :], b_ps[:, :],
                                                ALU.mult).then_inc(injected, 1)
                        dve.wait_ge(injected, T + 1 + 1)
                        dve.wait_ge(decay_ready, T + 1)
                        dve.wait_ge(multiplied, T + 2)
                        way = slice(None, None, 1 if d == 0 else -1)
                        nc.vector.tensor_tensor_scan(state[:, t % RING, way], decay[:, t % 2, way],
                                                     inject_ps[:, way], 0.0, ALU.mult, ALU.add).then_inc(scanned, 1)

                dve.wait_ge(y_out, 3 * orders * (b + 1))
                if orders == 2:
                    for dst, src in ((y_a[:, :], sp_e[:, :]), (y_b[:, :], sp_l[0:BLK, :])):
                        dst = dst.rearrange("p (h w) -> p w h", w=W)
                        ins = nc.vector.tensor_tensor(dst, dst, src.rearrange("p (w h) -> p w h", h=H), ALU.add)
                        ins.then_inc(z_done, 1)
                    dve.wait_ge(z_done, 2 * (b + 1))
                dve.sem_inc(y_summed, 1)
                key = ("mean", 0, 0)
                wait_work(dve, b, key)
                nc.vector.tensor_tensor(y_a[:, :], y_a[:, :], work[uses.buf[key]][:, :], ALU.subtract).then_inc(centred, 1)
                nc.vector.tensor_tensor(y_b[:, :], y_b[:, :], work[uses.buf[key]][0:BLK, :],
                                        ALU.subtract).then_inc(centred, 1)
                dve.wait_ge(centred, 2 * (b + 1))
                dve.sem_inc(work_free[uses.buf[key]], 1)
                dve.wait_ge(rooted, b + 1)
                dve.wait_ge(squared, 2 * (b + 1))
                nc.vector.tensor_tensor(y_a[:, :], y_a[:, :], sp_r[:, :], ALU.mult).then_inc(scaled, 1)
                nc.vector.tensor_tensor(y_b[:, :], y_b[:, :], sp_r[0:BLK, :], ALU.mult).then_inc(scaled, 1)
                dve.wait_ge(affine, 2 * (b + 1))
                dve.wait_ge(silued, 2 * (b + 1))
                nc.vector.tensor_tensor(y_a[:, :], y_a[:, :], sp_w[:, :], ALU.mult).then_inc(gated, 1)
                nc.vector.tensor_tensor(y_b[:, :], y_b[:, :], sp_l[0:BLK, :], ALU.mult).then_inc(gated, 1)
                key = ("out", 0, 0)
                wait_work(dve, b, key)
                xs = x_cm[:, bass.ts(b, L)]
                if conv:
                    nc.vector.scalar_tensor_tensor(out=xs, in0=work[uses.buf[key]][0:C, :], scalar=out_bias[:, 0:1],
                                                   in1=xs, op0=ALU.add, op1=ALU.add).then_inc(x_added, 1)
                else:
                    nc.vector.tensor_tensor(xs, xs, work[uses.buf[key]][0:C, :], ALU.add).then_inc(x_added, 1)
                dve.wait_ge(x_added, b + 1)
                dve.sem_inc(work_free[uses.buf[key]], 1)


def network(nc, hbm, out):
    with ExitStack() as ctx:
        def sb(n, shape):
            return ctx.enter_context(nc.sbuf_tensor(n, shape, F32))

        x_cm = sb("x_cm", [C, B * L])
        g_cm = sb("g_cm", [C, B * L])
        ident = sb("ident", [128, 128])
        group_mean = sb("group_mean", [C, C])
        state_cols = sb("state_cols", [128, 2 * NS])
        row_cols = sb("row_cols", [128, 3])
        loaded = ctx.enter_context(nc.semaphore("loaded"))
        stored = ctx.enter_context(nc.semaphore("stored"))
        with nc.Block() as block:
            @block.sync
            def _(sp):
                sp.dma_start(x_cm[:, :], hbm["x"]).then_inc(loaded, 16)
                sp.dma_start(ident[:, :], hbm["ident"]).then_inc(loaded, 16)
                sp.dma_start(group_mean[:, :], hbm["group_mean"]).then_inc(loaded, 16)
                sp.dma_start(state_cols[:, :], hbm["state_cols"]).then_inc(loaded, 16)
                sp.dma_start(row_cols[:, :], hbm["row_cols"]).then_inc(loaded, 16)
                sp.wait_ge(loaded, 5 * 16)

        def ssm(n, orders, dirs, rank, conv, eps):
            weights = {k[3:]: v for k, v in hbm.items() if k.startswith(n + "_")}
            group_norm(nc, f"{n}_gn", x_cm[:, :], g_cm[:, :], group_mean[:, :])
            scan_layer(nc, n, x_cm, g_cm, ident[:, :], state_cols, weights, orders, dirs, rank, conv, eps)

        ssm("L0", 2, 2, 12, False, 1e-6)
        group_norm(nc, "L1_gn", x_cm[:, :], g_cm[:, :], group_mean[:, :])
        motif_layer(nc, x_cm[:, :], g_cm[:, :], ident[:, :], row_cols)
        ssm("L2", 1, 1, 6, True, 1e-5)
        ssm("L3", 2, 2, 12, False, 1e-6)
        with nc.Block() as block:
            @block.sync
            def _(sp):
                sp.dma_start(out, x_cm[:, :]).then_inc(stored, 16)
                sp.wait_ge(stored, 16)


def _ssm_arrays(np, n, in_w, out_w, xp, dtw, dtb, a_logs, ds, norm_w, norm_b, orders, dirs):
    K, rank = dtw.shape[0], dtw.shape[2]
    ks = [[o + orders * d for d in range(dirs)] for o in range(orders)]
    flat = [k for o in ks for k in o]
    nj = -(-dirs * NBLK // 2)

    def tiles(v):
        r = np.zeros((256,), np.float32)
        r[:DI] = v
        return r.reshape(2, 128).T

    wt = in_w.T
    r = {"w_u": np.concatenate([wt[:, :DI], wt[:, :DI]], 1), "w_z": np.concatenate([wt[:, DI:], wt[:, DI:DI + BLK]], 1)}
    bc = np.stack([np.tile(xp[k, rank:].T, (1, 4)) for k in flat], 1)
    r["w_bc_a"], r["w_bc_b"] = bc[:128], bc[128:]
    rk = np.stack([np.concatenate([xp[k, :rank].T for k in o], 1) for o in ks], 1)
    r["w_r_a"], r["w_r_b"] = rk[:128], rk[128:]
    w_dt = np.zeros((dirs * rank, orders, 128 * nj), np.float32)
    bias = np.zeros((orders, 128 * nj), np.float32)
    for o in range(orders):
        for d, k in enumerate(ks[o]):
            w_dt[d * rank:(d + 1) * rank, o, d * DI:(d + 1) * DI] = dtw[k].T
            bias[o, d * DI:(d + 1) * DI] = dtb[k]
    r["w_dt"] = w_dt
    r["dt_bias"] = bias.reshape(orders, nj, 128).transpose(2, 0, 1)
    a = a_logs.reshape(K, NBLK, BLK, 2, NP)[flat]
    r["a_logs"] = a.transpose(3, 2, 0, 1, 4).reshape(128, len(flat), NBLK, NP)
    d = ds.reshape(K, DI)
    r["skip"] = np.stack([np.stack([tiles(d[k]) for k in o], 1) for o in ks], 1)
    r["norm"] = np.stack([tiles(norm_w), tiles(norm_b)], 1)
    r["w_o_a"], r["w_o_b"] = out_w.T[:128], out_w.T[128:]
    return {f"{n}_{k}": v for k, v in r.items()}, tiles


def kernel(**inputs):
    import numpy as np
    import concourse.bacc as _bacc
    from concourse.bass_utils import run_bass_kernel_spmd as _run

    v = {k: np.asarray(a) for k, a in inputs.items()}
    arrays = {"x": v["x"].reshape(B * L, C).T, "ident": np.eye(128, dtype=np.float32)}
    group = np.arange(C) // (C // 32)
    arrays["group_mean"] = (group[:, None] == group[None, :]).astype(np.float32) / np.float32(C // 32)
    rows = np.arange(128)
    part = np.arange(128) // 32
    arrays["state_cols"] = ((rows[:, None] % 32 == np.arange(32)[None, :]) & (part != 1)[:, None]).astype(np.float32)
    arrays["row_cols"] = np.stack([rows % 2 == 0, rows % 2 == 1, rows >= H], 1).astype(np.float32)
    for n in ("L0", "L3"):
        g = lambda s: v[f"{n}_conv_{s}"]
        a, _ = _ssm_arrays(np, n, g("in_proj_weight"), g("out_proj_weight"), g("x_proj_weight"),
                           g("dt_projs_weight"), g("dt_projs_bias"), g("A_logs"), g("Ds"), g("out_norm_weight"),
                           g("out_norm_bias"), 2, 2)
        arrays.update(a)
    g = lambda s: v[f"L2_conv_{s}"]
    a, tiles = _ssm_arrays(np, "L2", g("in_proj_w"), g("out_proj_w"), g("x_proj_w")[None], g("dt_proj_w")[None],
                           g("dt_proj_b")[None], g("A_log"), g("Ds"), g("ln_g"), g("ln_b"), 1, 1)
    arrays.update(a)
    cw = g("conv_w").reshape(DI, 9)
    arrays["L2_conv_w"] = np.stack([tiles(cw[:, k]) for k in range(9)], 2)
    arrays["L2_in_bias"] = np.stack([tiles(g("in_proj_b")[:DI]), tiles(g("in_proj_b")[DI:])], 1)
    arrays["L2_conv_b"] = tiles(g("conv_b"))
    arrays["L2_out_bias"] = g("out_proj_b").reshape(C, 1)
    arrays = {f"in_{k}": np.ascontiguousarray(a) for k, a in arrays.items()}

    nc = _bacc.Bacc("TRN2", target_bir_lowering=False, num_devices=1)
    hbm = {k[3:]: nc.dram_tensor(k, a.shape, mybir.dt.from_np(a.dtype), kind="ExternalInput").ap()
           for k, a in arrays.items()}
    out = nc.dram_tensor("out_y", [C, B * L], F32, kind="ExternalOutput").ap()
    network(nc, hbm, out)
    r = _run(nc, [arrays], core_ids=[0])
    return np.ascontiguousarray(r.results[0]["out_y"].T).reshape(B, H, W, C)
```

```python
from contextlib import ExitStack, contextmanager

import concourse.bass as bass
from concourse import mybir

F32 = mybir.dt.float32
BF16 = mybir.dt.bfloat16
ALU = mybir.AluOpType
ACT = mybir.ActivationFunctionType

B, H, W, C = 4, 32, 32, 96
L = H * W
DI = 192
NS = 16
HALF = 512
BLK = 64
NBLK = DI // BLK
NP = NS // 2
RING = 3
ROUND = 12582912.0
GN_EPS = 1e-5


def halves():
    return [(i, slice(i * HALF, (i + 1) * HALF)) for i in range(L // HALF)]


@contextmanager
def cleared(nc):
    sems = []
    with ExitStack() as ctx:
        yield ctx, sems
    nc.clear_and_free_semaphores(sems)
    nc.all_engine_barrier()


def group_norm(nc, name, x_cm, g_cm, group_mean):
    with cleared(nc) as (ctx, sems):
        def sb(n, shape):
            return ctx.enter_context(nc.sbuf_tensor(f"{name}_{n}", shape, F32))

        def sem(n):
            sems.append(nc.alloc_semaphore(name=f"{name}_{n}"))
            return sems[-1]

        stats = sb("stats", [C, B, 2, 6])
        mv = sb("mv", [C, B, 2])
        spread = sb("spread", [C, B])
        mean = sb("mean", [C, B])
        vare = sb("vare", [C, B])
        logv = sb("logv", [C, B])
        rstd = sb("rstd", [C, B])
        newton = sb("newton", [C, B])
        eps = sb("eps", [C, 1])
        ps = ctx.enter_context(nc.psum_tensor(f"{name}_ps", [C, 2, HALF], F32))
        dve_step, means_ready, vars_ready, logs, roots = (
            sem(s) for s in ("dve_step", "means_ready", "vars_ready", "logs", "roots"))
        block = ctx.enter_context(nc.Block())
        n_stats = 2 * B + B + 1

        @block.vector
        def _(dve):
            done = [0]

            def chained(ins):
                done[0] += 1
                ins.then_inc(dve_step, 1)
                dve.wait_ge(dve_step, done[0])

            for b in range(B):
                for i in range(2):
                    chained(nc.vector.bn_stats(stats[:, b, i, :], x_cm[:, b * L + i * HALF:b * L + (i + 1) * HALF]))
                chained(nc.vector.bn_aggr(mv[:, b, :], stats[:, b, :, :]))
            chained(nc.vector.memset(eps[:, :], GN_EPS))
            dve.wait_ge(means_ready, 1)
            chained(nc.vector.tensor_copy(mean[:, :], ps[:, 0, 0:B]))
            chained(nc.vector.tensor_tensor(spread[:, :], mv[:, :, 0], mean[:, :], ALU.subtract))
            chained(nc.vector.tensor_tensor(spread[:, :], spread[:, :], spread[:, :], ALU.mult))
            chained(nc.vector.tensor_tensor(spread[:, :], spread[:, :], mv[:, :, 1], ALU.add))
            dve.wait_ge(vars_ready, 1)
            chained(nc.vector.tensor_scalar(vare[:, :], ps[:, 1, 0:B], GN_EPS, None, ALU.add))
            dve.wait_ge(roots, 1)
            chained(nc.vector.tensor_tensor(newton[:, :], rstd[:, :], rstd[:, :], ALU.mult))
            chained(nc.vector.tensor_tensor(newton[:, :], newton[:, :], vare[:, :], ALU.mult))
            chained(nc.vector.tensor_scalar(newton[:, :], newton[:, :], -0.5, 1.5, ALU.mult, ALU.add))
            chained(nc.vector.tensor_tensor(rstd[:, :], rstd[:, :], newton[:, :], ALU.mult))
            for b in range(B):
                chained(nc.vector.tensor_scalar(g_cm[:, b * L:(b + 1) * L], x_cm[:, b * L:(b + 1) * L],
                                                mean[:, b:b + 1], rstd[:, b:b + 1], ALU.subtract, ALU.mult))

        @block.tensor
        def _(pe):
            pe.wait_ge(dve_step, n_stats)
            nc.tensor.matmul(ps[:, 0, 0:B], group_mean, mv[:, :, 0], start=True, stop=True).then_inc(means_ready, 1)
            pe.wait_ge(dve_step, n_stats + 4)
            nc.tensor.matmul(ps[:, 1, 0:B], group_mean, spread[:, :], start=True, stop=True).then_inc(vars_ready, 1)

        @block.scalar
        def _(act):
            act.wait_ge(dve_step, n_stats + 5)
            nc.scalar.activation(logv[:, :], vare[:, :], ACT.Ln).then_inc(logs, 1)
            act.wait_ge(logs, 1)
            nc.scalar.activation(rstd[:, :], logv[:, :], ACT.Exp, scale=-0.5).then_inc(roots, 1)


def motif_layer(nc, x_cm, g_cm, ident, cols):
    with cleared(nc) as (ctx, sems):
        def sb(n, shape=(128, W, C)):
            return ctx.enter_context(nc.sbuf_tensor(f"motif_{n}", list(shape), F32))

        def sem(n):
            sems.append(nc.alloc_semaphore(name=f"motif_{n}"))
            return sems[-1]

        f, below, base, own, right, diag, cross, acc, val, rnd = (
            sb(n) for n in ("f", "below", "base", "own", "right", "diag", "cross", "acc", "val", "rnd"))
        ps = ctx.enter_context(nc.psum_tensor("motif_ps", [128, 8, HALF], F32))
        turned, f_ready, below_ready, dve_step, back, added = (
            sem(s) for s in ("turned", "f_ready", "below_ready", "dve_step", "back", "added"))
        block = ctx.enter_context(nc.Block())
        g_v = g_cm.rearrange("p (q w) -> p q w", w=W)
        x_v = x_cm.rearrange("p (q w) -> p q w", w=W)
        per_bank, back_bank = 5, 4
        banks_in = -(-W // per_bank)
        banks_out = W // back_bank
        motif_steps = 2 + 4 * 5 + 9 * 3

        @block.tensor
        def _(pe):
            for k in range(banks_in):
                ws = range(k * per_bank, min((k + 1) * per_bank, W))
                if k >= 8:
                    pe.wait_ge(f_ready, k - 7)
                for j, w in enumerate(ws):
                    t = nc.tensor.transpose(ps[:, k % 8, j * C:(j + 1) * C], g_v[:, :, w], ident[0:C, 0:C])
                t.then_inc(turned, 1)
            pe.wait_ge(dve_step, motif_steps)
            pe.wait_ge(f_ready, banks_in)
            for k in range(banks_out):
                for j in range(back_bank):
                    t = nc.tensor.transpose(ps[0:C, k % 8, j * 128:(j + 1) * 128], acc[:, k * back_bank + j, :], ident)
                t.then_inc(back, 1)

        @block.scalar
        def _(act):
            for k in range(banks_in):
                a, z = k * per_bank, min((k + 1) * per_bank, W)
                act.wait_ge(turned, k + 1)
                nc.scalar.copy(f[:, a:z, :], ps[:, k % 8, 0:(z - a) * C]).then_inc(f_ready, 1)

        @block.sync
        def _(sp):
            sp.wait_ge(below_ready, 1)
            sp.wait_ge(f_ready, banks_in)
            sp.dma_start(below[0:127, :, :], f[1:128, :, :]).then_inc(below_ready, 16)

        even, odd, mask = cols[:, 0:1], cols[:, 1:2], cols[:, 2:3]
        R, S = H - 2, C - 2

        @block.vector
        def _(dve):
            done = [0]

            def chained(ins):
                done[0] += 1
                ins.then_inc(dve_step, 1)
                dve.wait_ge(dve_step, done[0])

            def floored(dst, a, b, rows, chans):
                d, v, r = (t[:, rows, chans] for t in (dst, val, rnd))
                chained(nc.vector.scalar_tensor_tensor(out=v, in0=a, scalar=0.5, in1=b, op0=ALU.mult, op1=ALU.mult))
                chained(nc.vector.tensor_scalar(r, v, ROUND, None, ALU.add))
                chained(nc.vector.tensor_scalar(r, r, ROUND, None, ALU.subtract))
                chained(nc.vector.tensor_tensor(v, r, v, ALU.is_gt))
                chained(nc.vector.tensor_tensor(d, r, v, ALU.subtract))

            nc.vector.memset(below[:, :, :], 0.0).then_inc(below_ready, 1)
            dve.wait_ge(f_ready, banks_in)
            chained(nc.vector.memset(acc[:, :, :], 0.0))
            chained(nc.vector.tensor_scalar(base[:, :, :], f[:, :, :], mask, None, ALU.mult))
            floored(own, f[:, :, :], f[:, :, :], slice(0, W), slice(0, C))
            floored(right, f[:, :, 0:C - 1], f[:, :, 1:C], slice(0, W), slice(0, C - 1))
            floored(diag, f[:, 0:W - 1, 2:C], f[:, 1:W, 0:C - 2], slice(0, W - 1), slice(2, C))
            dve.wait_ge(below_ready, 17)
            floored(cross, f[:, 2:W, 2:C], below[:, 0:W - 2, 0:C - 2], slice(2, W), slice(2, C))
            partner = [(right, own), (own, right), (diag, own), (own, right), (right, own), (own, diag),
                       (right, own), (own, right), (cross, own)]
            for k, (pe_, po_) in enumerate(partner):
                ki, kj = divmod(k, 3)
                at = (slice(None), slice(ki, ki + R), slice(kj, kj + S))
                chained(nc.vector.scalar_tensor_tensor(out=val[at], in0=pe_[at], scalar=even, in1=base[at],
                                                       op0=ALU.mult, op1=ALU.add))
                chained(nc.vector.scalar_tensor_tensor(out=val[at], in0=po_[at], scalar=odd, in1=val[at],
                                                       op0=ALU.mult, op1=ALU.add))
                chained(nc.vector.tensor_tensor(acc[at], acc[at], val[at], ALU.add))
            assert done[0] == motif_steps
            for k in range(banks_out):
                dve.wait_ge(back, k + 1)
                xs = x_v[:, :, k * back_bank:(k + 1) * back_bank].rearrange("p q w -> p w q")
                nc.vector.tensor_tensor(xs, xs, ps[0:C, k % 8, :].rearrange("p (w q) -> p w q", w=back_bank),
                                        ALU.add).then_inc(added, 1)


class Uses:

    def __init__(self, keys):
        self.index = {k: i for i, (k, _) in enumerate(keys)}
        self.buf = dict(keys)
        self.nth, count = {}, [0, 0]
        for k, b in keys:
            self.nth[k] = count[b]
            count[b] += 1
        self.count, self.total = count, len(keys)


def scan_layer(nc, name, x_cm, g_cm, ident, cols_e, hbm, orders, dirs, rank, conv, eps):
    NJ = -(-dirs * NBLK // 2)
    NT = dirs * NP * NBLK
    RANKS = dirs * rank
    rows_of = [min(128, dirs * DI - 128 * j) for j in range(NJ)]
    with cleared(nc) as (ctx, sems):
        def sb(n, shape, dt=F32):
            return ctx.enter_context(nc.sbuf_tensor(f"{name}_{n}", shape, dt))

        def sem(n):
            sems.append(nc.alloc_semaphore(name=f"{name}_{n}"))
            return sems[-1]

        w_u = sb("w_u", [C, 2 * DI])
        w_z = sb("w_z", [C, 256])
        w_bc_a = sb("w_bc_a", [128, orders * dirs, 128])
        w_bc_b = sb("w_bc_b", [BLK, orders * dirs, 128])
        w_r_a = sb("w_r_a", [128, orders, RANKS])
        w_r_b = sb("w_r_b", [BLK, orders, RANKS])
        w_dt = sb("w_dt", [RANKS, orders, 128 * NJ])
        dt_bias = sb("dt_bias", [128, orders, NJ])
        a_neg = sb("a_neg", [128, orders * dirs, NBLK, NP])
        skip_w = sb("skip_w", [128, orders, dirs, 2])
        skip_sum = sb("skip_sum", [128, orders, 2])
        skip_diag = sb("skip_diag", [128, orders, 2, 128])
        norm_w = sb("norm_w", [128, 2, 2])
        w_o_a = sb("w_o_a", [128, C])
        w_o_b = sb("w_o_b", [BLK, C])
        pick = sb("pick", [128, 2 * NS, BLK], BF16)
        fold = sb("fold", [128, 3 * BLK])
        mean_w = sb("mean_w", [128, 128])
        eps_col = sb("eps_col", [128, 1])
        loads = [(w_u, "w_u"), (w_z, "w_z"), (w_bc_a, "w_bc_a"), (w_bc_b, "w_bc_b"), (w_r_a, "w_r_a"),
                 (w_r_b, "w_r_b"), (w_dt, "w_dt"), (dt_bias, "dt_bias"), (a_neg, "a_logs"), (skip_w, "skip"),
                 (norm_w, "norm"), (w_o_a, "w_o_a"), (w_o_b, "w_o_b")]
        if conv:
            conv_w = sb("conv_w", [128, 2, 9])
            in_bias = sb("in_bias", [128, 2, 2])
            conv_b = sb("conv_b", [128, 2])
            out_bias = sb("out_bias", [C, 1])
            padded = sb("padded", [128, 2, H + 2, W + 2])
            conved = sb("conved", [128, 2, L])
            loads += [(conv_w, "conv_w"), (in_bias, "in_bias"), (conv_b, "conv_b"), (out_bias, "out_bias")]

        u = sb("u", [128, NJ, L])
        ranks = sb("ranks", [RANKS, L])
        bc = sb("bc", [128, dirs, L], BF16)
        sp_e, sp_l, sp_r, sp_w = (sb(n, [128, L]) for n in ("sp_e", "sp_l", "sp_r", "sp_w"))
        rest = sp_r
        delta = sb("delta", [128, NJ, L])
        du = sb("du", [128, NJ, L])
        delta2 = sb("delta2", [128, dirs * NBLK, L])
        du2 = sb("du2", [128, dirs * NBLK, L])
        decay = sb("decay", [128, 2, L])
        state = sb("state", [128, RING, L])
        read = sb("read", [128, RING, L])
        c_rows = sb("c_rows", [128, 2, L])
        y_a = sb("y_a", [128, L])
        y_b = sb("y_b", [BLK, L])

        y_ps = ctx.enter_context(nc.psum_tensor(f"{name}_y_ps", [128, 3, HALF], F32))
        work0 = ctx.enter_context(nc.psum_tensor(f"{name}_work0", [128, L], F32))
        work1 = ctx.enter_context(nc.psum_tensor(f"{name}_work1", [128, L], F32))
        c_ps = ctx.enter_context(nc.psum_tensor(f"{name}_c_ps", [128, HALF], F32))
        work = [work0, work1]
        inject_ps, b_ps = work0, work1
        y_flat = y_ps[:, 0:2, :].rearrange("p a n -> p (a n)")

        (weights, w_used, set_up, consts, conv_padded, conv_step, conved_s, u_ready, ranks_ready, bc_hi, bc_rest, bc_mid,
         bc_ready, sp_abs, sp_exp, sp_one, sp_log, sp_step, decay_ready, scanned, injected, b_ready, c_ready, c_copied,
         multiplied, y_added, y_free, y_out, y_summed, centred, squared, logged, rooted, scaled, affine, gated,
         silued, z_done, x_added, ctx_done) = (
            sem(s) for s in (
                "weights", "w_used", "set_up", "consts", "conv_padded", "conv_step", "conved", "u_ready", "ranks_ready",
                "bc_hi", "bc_rest", "bc_mid", "bc_ready", "sp_abs", "sp_exp", "sp_one", "sp_log", "sp_step", "decay_ready",
                "scanned", "injected", "b_ready", "c_ready", "c_copied", "multiplied", "y_added", "y_free", "y_out",
                "y_summed", "centred", "squared", "logged", "rooted", "scaled", "affine", "gated", "silued", "z_done",
                "x_added", "ctx_done"))
        work_ready = sem("work_ready")
        work_free = [sem("work_free0"), sem("work_free1")]
        delta2_in = [sem(f"delta2_in{d}") for d in range(dirs)]
        du2_in = [sem(f"du2_in{d}") for d in range(dirs)]

        keys = []
        for o in range(orders):
            seq = [("u", o, j) for j in range(2 if conv else NJ)] + [("ranks", o, 0)]
            seq += [("bc", o, d) for d in range(dirs)] + [("dt", o, j) for j in range(NJ)]
            keys += [(k, i % 2) for i, k in enumerate(seq)]
        keys += [(("mean", 0, 0), 0), (("var", 0, 0), 1), (("z", 0, 0), 0), (("z", 0, 1), 1), (("out", 0, 0), 0)]
        uses = Uses(keys)

        def wait_work(eng, b, key):
            eng.wait_ge(work_ready, b * uses.total + uses.index[key] + 1)

        def free_work(ins, key):
            ins.then_inc(work_free[uses.buf[key]], 1)

        def turn(b, o):
            return b * orders + o

        block = ctx.enter_context(nc.Block())
        tiles = [(d, p, c) for d in range(dirs) for p in range(NP) for c in range(NBLK)]
        n_setup = 2 + orders * (1 + 2) + 2 * NS + 3 + 1 + (1 if conv else 0)

        @block.sync
        def _(sp):
            for t, key in loads:
                sp.dma_start(t[tuple(slice(None) for _ in t.shape)], hbm[key]).then_inc(weights, 16)
            with sp.Fori(0, B) as b:
                for o in range(orders):
                    it = turn(b, o)
                    sp.wait_ge(y_added, it * NT + RING)
                    for q in range(dirs * NBLK):
                        j, half = q // 2, q % 2
                        rows = slice(half * BLK, half * BLK + BLK)
                        sp.wait_ge(sp_step, (it * NJ + j) * 4 + 4)
                        for side in range(2):
                            to = slice(side * BLK, side * BLK + BLK)
                            sp.dma_start(delta2[to, q, :], delta[rows, j, :]).then_inc(delta2_in[q // NBLK], 16)
                            sp.dma_start(du2[to, q, :], du[rows, j, :]).then_inc(du2_in[q // NBLK], 16)

        @block.tensor
        def _(pe):
            pe.wait_ge(weights, 16 * len(loads))
            pe.wait_ge(set_up, n_setup)

            with pe.Fori(0, B) as b:
                def claim(key):
                    k = uses.buf[key]
                    pe.wait_ge(work_free[k], b * uses.count[k] + uses.nth[key] + 1)
                    return work[k]

                def product(key, rows, parts):
                    dst = claim(key)
                    for i, s in halves():
                        for n, (lhs, rhs) in enumerate(parts):
                            m = nc.tensor.matmul(dst[0:rows, s], lhs, rhs(i, s), start=(n == 0),
                                                 stop=(n == len(parts) - 1))
                    m.then_inc(work_ready, 1)

                def g_half(o):
                    img = g_cm[:, bass.ts(b, L)]
                    if o == 0:
                        return lambda i, s: img[:, s]
                    turned = img.rearrange("p (h w) -> p w h", w=W)
                    return lambda i, s: turned[:, i * (W // 2):(i + 1) * (W // 2), :]

                for o in range(orders):
                    it = turn(b, o)
                    for j in range(2 if conv else NJ):
                        product(("u", o, j), 128, [(w_u[:, j * 128:(j + 1) * 128], g_half(o))])
                    pe.wait_ge(u_ready, it * NJ + NJ)
                    u_parts = (lambda i, s: u[:, 0, s], lambda i, s: u[0:BLK, 1, s])
                    product(("ranks", o, 0), RANKS, [(w_r_a[:, o, :], u_parts[0]), (w_r_b[:, o, :], u_parts[1])])
                    for d in range(dirs):
                        product(("bc", o, d), 128, [(w_bc_a[:, o * dirs + d, :], u_parts[0]),
                                                    (w_bc_b[:, o * dirs + d, :], u_parts[1])])
                    pe.wait_ge(ranks_ready, it + 1)
                    for j in range(NJ):
                        product(("dt", o, j), rows_of[j], [(w_dt[:, o, j * 128:j * 128 + rows_of[j]],
                                                            lambda i, s: ranks[:, s])])
                    pe.wait_ge(y_free, it + 1)
                    for i, s in halves():
                        nc.tensor.matmul(y_ps[:, i, :], skip_diag[:, o, 0, :], u[:, 0, s], start=True, stop=False)
                    for i, s in halves():
                        nc.tensor.matmul(y_ps[i * BLK:(i + 1) * BLK, 2, :], skip_diag[0:BLK, o, 1, 0:BLK],
                                         u[0:BLK, 1, s], start=True, stop=False, skip_group_check=True)

                    def spread_rows(g, d, p):
                        G = it * dirs * NP + g
                        pe.wait_ge(bc_ready, it * dirs + d + 1)
                        pe.wait_ge(injected, G * NBLK + 1)
                        for i, s in halves():
                            m = nc.tensor.matmul(b_ps[:, s], pick[:, 2 * p:2 * p + 2, :], bc[:, d, s],
                                                 start=True, stop=True)
                        m.then_inc(b_ready, 1)
                        for i, s in halves():
                            pe.wait_ge(c_copied, G * 2 + i + 1)
                            nc.tensor.matmul(c_ps[:, :], pick[:, NS + 2 * p:NS + 2 * p + 2, :], bc[:, d, s],
                                             start=True, stop=True).then_inc(c_ready, 1)

                    def sum_states(t, c):
                        pe.wait_ge(multiplied, it * NT + t + 1 + RING + 1)
                        for i, s in halves():
                            src = read[:, t % RING, s]
                            if c < 2:
                                lhs = fold[:, BLK * (1 - c):BLK * (1 - c) + 128]
                                m = nc.tensor.matmul(y_ps[:, i, :], lhs, src, start=False, stop=(t == NT - 2))
                            else:
                                m = nc.tensor.matmul(y_ps[i * BLK:(i + 1) * BLK, 2, :], fold[:, BLK:2 * BLK], src,
                                                     start=False, stop=(t == NT - 1), skip_group_check=True)
                        m.then_inc(y_added, 1)

                    for k in range(2):
                        last = [key for key in uses.buf if uses.buf[key] == k and key[1] == o and
                                key[0] in ("u", "ranks", "bc", "dt")][-1]
                        pe.wait_ge(work_free[k], b * uses.count[k] + uses.nth[last] + 2)
                    spread_rows(0, 0, 0)
                    for t, (d, p, c) in enumerate(tiles):
                        if c == 1 and t // NBLK + 1 < dirs * NP:
                            g = t // NBLK + 1
                            spread_rows(g, g // NP, g % NP)
                        sum_states(t, c)

                pe.wait_ge(y_summed, b + 1)
                product(("mean", 0, 0), 128, [(mean_w[:, :], lambda i, s: y_a[:, s]),
                                              (mean_w[0:BLK, :], lambda i, s: y_b[:, s])])
                pe.wait_ge(squared, b * 2 + 2)
                product(("var", 0, 0), 128, [(mean_w[:, :], lambda i, s: sp_e[:, s]),
                                             (mean_w[0:BLK, :], lambda i, s: sp_l[0:BLK, s])])
                product(("z", 0, 0), 128, [(w_z[:, 0:128], g_half(0))])
                product(("z", 0, 1), 128, [(w_z[:, 128:256], g_half(0))])
                pe.wait_ge(gated, b * 2 + 2)
                product(("out", 0, 0), C, [(w_o_a[:, :], lambda i, s: y_a[:, s]),
                                           (w_o_b[:, :], lambda i, s: y_b[:, s])])
                pe.wait_ge(x_added, b + 1)

        @block.scalar
        def _(act):
            act.wait_ge(weights, 16 * len(loads))
            nc.scalar.activation(a_neg[:, :, :, :], a_neg[:, :, :, :], ACT.Exp).then_inc(consts, 1)
            act.wait_ge(consts, 1)
            nc.scalar.mul(a_neg[:, :, :, :], a_neg[:, :, :, :], -1.0).then_inc(consts, 1)
            act.wait_ge(consts, 2)
            act.wait_ge(set_up, n_setup)
            with act.Fori(0, B) as b:
                for o in range(orders):
                    it = turn(b, o)
                    if conv:
                        for j in range(2):
                            r = rows_of[j]
                            wait_work(act, b, ("u", o, j))
                            ins = nc.scalar.activation(padded[0:r, j, 1:H + 1, 1:W + 1],
                                                       work[uses.buf[("u", o, j)]][0:r, :].rearrange(
                                                           "p (h w) -> p h w", w=W),
                                                       ACT.Identity, bias=in_bias[0:r, 0, j:j + 1])
                            free_work(ins, ("u", o, j))
                        for j in range(2):
                            r = rows_of[j]
                            act.wait_ge(conved_s, b * 18 + (j + 1) * 9)
                            nc.scalar.activation(u[0:r, j, :], conved[0:r, j, :], ACT.Silu,
                                                 bias=conv_b[0:r, j:j + 1]).then_inc(u_ready, 1)
                    else:
                        for j in range(NJ):
                            wait_work(act, b, ("u", o, j))
                            nc.scalar.copy(u[:, j, :], work[uses.buf[("u", o, j)]][:, :]).then_inc(u_ready, 1)
                            act.wait_ge(u_ready, it * NJ + j + 1)
                            act.sem_inc(work_free[uses.buf[("u", o, j)]], 1)
                    key = ("ranks", o, 0)
                    wait_work(act, b, key)
                    nc.scalar.copy(ranks[:, :], work[uses.buf[key]][0:RANKS, :]).then_inc(ranks_ready, 1)
                    act.wait_ge(ranks_ready, it + 1)
                    act.sem_inc(work_free[uses.buf[key]], 1)
                    for d in range(dirs):
                        key = ("bc", o, d)
                        wait_work(act, b, key)
                        nc.scalar.copy(bc[:, d, :], work[uses.buf[key]][:, :]).then_inc(bc_hi, 1)
                        act.wait_ge(bc_rest, it * dirs + d + 1)
                        nc.scalar.copy(bc[BLK:128, d, :], rest[BLK:128, :]).then_inc(bc_mid, 1)
                    for j in range(NJ):
                        key, r = ("dt", o, j), rows_of[j]
                        src, bias = work[uses.buf[key]][0:r, :], dt_bias[0:r, o, j:j + 1]
                        n = it * NJ + j
                        wait_work(act, b, key)
                        if j == 0:
                            act.wait_ge(bc_ready, (it + 1) * dirs)
                        else:
                            act.wait_ge(sp_step, n * 4)
                        nc.scalar.activation(sp_e[0:r, :], src, ACT.Abs, bias=bias).then_inc(sp_abs, 1)
                        free_work(nc.scalar.activation(sp_r[0:r, :], src, ACT.Relu, bias=bias), key)
                        act.wait_ge(sp_abs, n + 1)
                        nc.scalar.activation(sp_e[0:r, :], sp_e[0:r, :], ACT.Exp, scale=-1.0).then_inc(sp_exp, 1)
                        act.wait_ge(sp_exp, n + 1)
                        nc.scalar.activation(sp_w[0:r, :], sp_e[0:r, :], ACT.Identity, bias=1.0).then_inc(sp_one, 1)
                        act.wait_ge(sp_one, n + 1)
                        nc.scalar.activation(sp_l[0:r, :], sp_w[0:r, :], ACT.Ln).then_inc(sp_log, 1)

                    def copy_c(g):
                        G = it * dirs * NP + g
                        act.wait_ge(multiplied, G * NBLK + 1)
                        for i, s in halves():
                            act.wait_ge(c_ready, G * 2 + i + 1)
                            nc.scalar.copy(c_rows[:, g % 2, s], c_ps[:, :]).then_inc(c_copied, 1)

                    for t, (d, p, c) in enumerate(tiles):
                        if p == 0 and c == 0:
                            act.wait_ge(delta2_in[d], (it + 1) * 16 * 2 * NBLK)
                        act.wait_ge(scanned, it * NT + t + RING - 1)
                        nc.scalar.activation(decay[:, t % 2, :], delta2[:, d * NBLK + c, :], ACT.Exp,
                                             scale=a_neg[:, o * dirs + d, c, p:p + 1]).then_inc(decay_ready, 1)
                        if c == 0:
                            copy_c(t // NBLK)
                    act.wait_ge(y_added, (it + 1) * NT + RING)
                    to_a, to_b = (y_a, y_b) if o == 0 else (sp_e, sp_l)
                    nc.scalar.copy(to_a[:, :], y_flat).then_inc(y_out, 1)
                    for i, s in halves():
                        ins = nc.scalar.copy(to_b[0:BLK, s], y_ps[i * BLK:(i + 1) * BLK, 2, :]).then_inc(y_out, 1)
                    act.wait_ge(y_out, 3 * (it + 1))
                    act.sem_inc(y_free, 1)

                act.wait_ge(centred, b * 2 + 2)
                nc.scalar.activation(sp_e[:, :], y_a[:, :], ACT.Square).then_inc(squared, 1)
                nc.scalar.activation(sp_l[0:BLK, :], y_b[:, :], ACT.Square).then_inc(squared, 1)
                key = ("var", 0, 0)
                wait_work(act, b, key)
                ins = nc.scalar.activation(sp_r[:, :], work[uses.buf[key]][:, :], ACT.Ln, bias=eps_col[:, :])
                ins.then_inc(logged, 1)
                act.wait_ge(logged, b + 1)
                act.sem_inc(work_free[uses.buf[key]], 1)
                nc.scalar.activation(sp_r[:, :], sp_r[:, :], ACT.Exp, scale=-0.5).then_inc(rooted, 1)
                act.wait_ge(scaled, b * 2 + 2)
                nc.scalar.activation(y_a[:, :], y_a[:, :], ACT.Identity, bias=norm_w[:, 1, 0:1],
                                     scale=norm_w[:, 0, 0:1]).then_inc(affine, 1)
                nc.scalar.activation(y_b[:, :], y_b[:, :], ACT.Identity, bias=norm_w[0:BLK, 1, 1:2],
                                     scale=norm_w[0:BLK, 0, 1:2]).then_inc(affine, 1)
                for j, (dst, r) in enumerate(((sp_w, 128), (sp_l, BLK))):
                    key = ("z", 0, j)
                    wait_work(act, b, key)
                    zb = in_bias[0:r, 1, j:j + 1] if conv else 0.0
                    nc.scalar.activation(dst[0:r, :], work[uses.buf[key]][0:r, :], ACT.Silu, bias=zb).then_inc(silued, 1)
                    act.wait_ge(silued, b * 2 + j + 1)
                    act.sem_inc(work_free[uses.buf[key]], 1)

        @block.gpsimd
        def _(pool):
            with pool.Fori(0, B) as b:
                for o in range(orders):
                    it = turn(b, o)
                    for t in range(NT):
                        g = t // NBLK
                        pool.wait_ge(scanned, it * NT + t + 1 + RING)
                        if t % NBLK == 0:
                            pool.wait_ge(c_copied, (it * dirs * NP + g) * 2 + 2 + 1)
                        pool.wait_ge(y_added, it * NT + t + 1)
                        nc.gpsimd.tensor_tensor(read[:, t % RING, :], state[:, t % RING, :], c_rows[:, g % 2, :],
                                                ALU.mult).then_inc(multiplied, 1)

        @block.vector
        def _(dve):
            for s, n in ((scanned, RING), (multiplied, RING + 1), (y_added, RING), (injected, 1), (c_copied, 1),
                         (y_free, 1), (work_free[0], 1), (work_free[1], 1)):
                for _ in range(n):
                    dve.sem_inc(s, 1)
            n = [0]

            def setup(ins):
                n[0] += 1
                ins.then_inc(set_up, 1)

            dve.wait_ge(weights, 16 * len(loads))
            setup(nc.vector.memset(mean_w[:, :], 1.0 / DI))
            setup(nc.vector.memset(eps_col[:, :], eps))
            for m in range(2 * NS):
                src = (m // NS) * NS + (m % NS) // 2 + NP * (m % 2)
                setup(nc.vector.tensor_copy(pick[:, m, :], cols_e[:, src:src + 1].to_broadcast([128, BLK])))
            for side, v in ((0, 0.0), (2, 0.0)):
                setup(nc.vector.memset(fold[:, side * BLK:(side + 1) * BLK], v))
            setup(nc.vector.tensor_tensor(fold[:, BLK:2 * BLK], ident[:, 0:BLK], ident[:, BLK:128], ALU.add))
            if conv:
                setup(nc.vector.memset(padded[:, :, :, :], 0.0))
            for o in range(orders):
                if dirs == 2:
                    setup(nc.vector.tensor_tensor(skip_sum[:, o, :], skip_w[:, o, 0, :], skip_w[:, o, 1, :], ALU.add))
                else:
                    setup(nc.vector.tensor_copy(skip_sum[:, o, :], skip_w[:, o, 0, :]))
            dve.wait_ge(set_up, n[0])
            for o in range(orders):
                for j in range(2):
                    setup(nc.vector.tensor_scalar(skip_diag[:, o, j, :], ident, skip_sum[:, o, j:j + 1], None,
                                                  ALU.mult))
            setup(nc.vector.memset(rest[:, :], 0.0))
            assert n[0] == n_setup
            dve.wait_ge(set_up, n_setup)

            with dve.Fori(0, B) as b:
                for o in range(orders):
                    it = turn(b, o)
                    if conv:
                        for j in range(2):
                            r = rows_of[j]
                            key = ("u", o, j)
                            acc = conved[0:r, j, :].rearrange("p (h w) -> p h w", w=W)
                            dve.wait_ge(work_free[uses.buf[key]], b * uses.count[uses.buf[key]] + uses.nth[key] + 2)
                            for k in range(9):
                                tap = padded[0:r, j, k // 3:k // 3 + H, k % 3:k % 3 + W]
                                wk = conv_w[0:r, j, k:k + 1]
                                if k == 0:
                                    ins = nc.vector.tensor_scalar(acc, tap, wk, None, ALU.mult)
                                else:
                                    dve.wait_ge(conved_s, b * 18 + j * 9 + k)
                                    ins = nc.vector.scalar_tensor_tensor(out=acc, in0=tap, scalar=wk, in1=acc,
                                                                         op0=ALU.mult, op1=ALU.add)
                                ins.then_inc(conved_s, 1)
                    for d in range(dirs):
                        key = ("bc", o, d)
                        dve.wait_ge(bc_hi, it * dirs + d + 1)
                        if d > 0:
                            dve.wait_ge(bc_ready, it * dirs + d)
                        nc.vector.tensor_tensor(rest[BLK:128, :], work[uses.buf[key]][BLK:128, :], bc[BLK:128, d, :],
                                                ALU.subtract).then_inc(bc_rest, 1)
                        dve.wait_ge(bc_rest, it * dirs + d + 1)
                        dve.sem_inc(work_free[uses.buf[key]], 1)
                        dve.wait_ge(bc_mid, it * dirs + d + 1)
                        nc.vector.tensor_tensor(bc[96:128, d, :], rest[96:128, :], bc[96:128, d, :],
                                                ALU.subtract).then_inc(bc_ready, 1)
                    for j in range(NJ):
                        r, n4 = rows_of[j], (it * NJ + j) * 4
                        e, l, w, dl = sp_e[0:r, :], sp_l[0:r, :], sp_w[0:r, :], delta[0:r, j, :]
                        dve.wait_ge(sp_log, it * NJ + j + 1)
                        nc.vector.scalar_tensor_tensor(out=w, in0=w, scalar=1.0, in1=l, op0=ALU.subtract,
                                                       op1=ALU.subtract).then_inc(sp_step, 1)
                        dve.wait_ge(sp_step, n4 + 1)
                        nc.vector.scalar_tensor_tensor(out=w, in0=w, scalar=0.0, in1=e, op0=ALU.max,
                                                       op1=ALU.subtract).then_inc(sp_step, 1)
                        dve.wait_ge(sp_step, n4 + 2)
                        nc.vector.tensor_tensor(dl, sp_r[0:r, :], w, ALU.subtract).then_inc(sp_step, 1)
                        dve.wait_ge(sp_step, n4 + 3)
                        nc.vector.tensor_tensor(du[0:r, j, :], dl, u[0:r, j, :], ALU.mult).then_inc(sp_step, 1)

                    for t, (d, p, c) in enumerate(tiles):
                        T = it * NT + t
                        if p == 0 and c == 0:
                            dve.wait_ge(du2_in[d], (it + 1) * 16 * 2 * NBLK)
                        if c == 0:
                            dve.wait_ge(b_ready, it * dirs * NP + t // NBLK + 1)
                        dve.wait_ge(scanned, T + RING)
                        nc.vector.tensor_tensor(inject_ps[:, :], du2[:, d * NBLK + c, :], b_ps[:, :],
                                                ALU.mult).then_inc(injected, 1)
                        dve.wait_ge(injected, T + 1 + 1)
                        dve.wait_ge(decay_ready, T + 1)
                        dve.wait_ge(multiplied, T + 2)
                        way = slice(None, None, 1 if d == 0 else -1)
                        nc.vector.tensor_tensor_scan(state[:, t % RING, way], decay[:, t % 2, way],
                                                     inject_ps[:, way], 0.0, ALU.mult, ALU.add).then_inc(scanned, 1)

                dve.wait_ge(y_out, 3 * orders * (b + 1))
                if orders == 2:
                    for dst, src in ((y_a[:, :], sp_e[:, :]), (y_b[:, :], sp_l[0:BLK, :])):
                        dst = dst.rearrange("p (h w) -> p w h", w=W)
                        ins = nc.vector.tensor_tensor(dst, dst, src.rearrange("p (w h) -> p w h", h=H), ALU.add)
                        ins.then_inc(z_done, 1)
                    dve.wait_ge(z_done, 2 * (b + 1))
                dve.sem_inc(y_summed, 1)
                key = ("mean", 0, 0)
                wait_work(dve, b, key)
                nc.vector.tensor_tensor(y_a[:, :], y_a[:, :], work[uses.buf[key]][:, :], ALU.subtract).then_inc(centred, 1)
                nc.vector.tensor_tensor(y_b[:, :], y_b[:, :], work[uses.buf[key]][0:BLK, :],
                                        ALU.subtract).then_inc(centred, 1)
                dve.wait_ge(centred, 2 * (b + 1))
                dve.sem_inc(work_free[uses.buf[key]], 1)
                dve.wait_ge(rooted, b + 1)
                dve.wait_ge(squared, 2 * (b + 1))
                nc.vector.tensor_tensor(y_a[:, :], y_a[:, :], sp_r[:, :], ALU.mult).then_inc(scaled, 1)
                nc.vector.tensor_tensor(y_b[:, :], y_b[:, :], sp_r[0:BLK, :], ALU.mult).then_inc(scaled, 1)
                dve.wait_ge(affine, 2 * (b + 1))
                dve.wait_ge(silued, 2 * (b + 1))
                nc.vector.tensor_tensor(y_a[:, :], y_a[:, :], sp_w[:, :], ALU.mult).then_inc(gated, 1)
                nc.vector.tensor_tensor(y_b[:, :], y_b[:, :], sp_l[0:BLK, :], ALU.mult).then_inc(gated, 1)
                key = ("out", 0, 0)
                wait_work(dve, b, key)
                xs = x_cm[:, bass.ts(b, L)]
                if conv:
                    nc.vector.scalar_tensor_tensor(out=xs, in0=work[uses.buf[key]][0:C, :], scalar=out_bias[:, 0:1],
                                                   in1=xs, op0=ALU.add, op1=ALU.add).then_inc(x_added, 1)
                else:
                    nc.vector.tensor_tensor(xs, xs, work[uses.buf[key]][0:C, :], ALU.add).then_inc(x_added, 1)
                dve.wait_ge(x_added, b + 1)
                dve.sem_inc(work_free[uses.buf[key]], 1)


TURN_TILES = 2 * NP * NBLK
GROUPS = 2 * NP
DEPTH = 2
READS = 3
LAG = 3
FINISH = {("z", 0): (1, 2), ("mean", 0): (4, 5), ("z", 1): (7, 8), ("var", 0): (13, 14), ("out", 0): (40, 41)}
PREPARE = {("u", 0): (10, 11), ("u", 1): (16, 17), ("u", 2): (19, 20), ("bc", 0): (22, 23), ("bc", 1): (25, 26),
           ("dt", 0): (31, 32), ("dt", 1): (34, 35), ("dt", 2): (37, 38)}
ACT_STEPS = {12: [("square", 0)], 13: [("square", 1)], 15: [("silu", 0)], 18: [("rstd", 0)], 22: [("affine", 0)],
             23: [("affine", 1)], 27: [("hi", 0)], 29: [("mid", 0)], 30: [("hi", 1)], 32: [("mid", 1)],
             36: [("exp", 0)], 37: [("log", 0)], 39: [("exp", 1)], 40: [("log", 1)], 42: [("exp", 2)],
             43: [("log", 2)]}
DVE_STEPS = {3: [("join", 0)], 4: [("join", 1)], 10: [("centre", 0)], 11: [("centre", 1)], 20: [("scale", 0)],
             21: [("scale", 1)], 24: [("gate", 0)], 25: [("gate", 1)], 27: [("rest", 0)], 29: [("lo", 0)],
             30: [("rest", 1)], 32: [("lo", 1)], 37: [("fix", 0)], 38: [("part", 0)], 40: [("fix", 1)],
             41: [("part", 1)], 43: [("fix", 2)], 44: [("part", 2)], 46: [("residual", 0)]}
POOL_STEPS = {38: [("delta", 0)], 39: [("du", 0)], 41: [("delta", 1)], 42: [("du", 1)], 44: [("delta", 2)],
              45: [("du", 2)]}
FINISH_STEPS = {"square", "silu", "rstd", "affine", "join", "centre", "scale", "gate", "residual"}


def side_uses(finish):
    table = {**(FINISH if finish else {}), **PREPARE}
    return sorted((t, key, i) for key, ts in table.items() for i, t in enumerate(ts))


class BankUses:

    def __init__(self):
        self.head = {(key, i): n for n, (_, key, i) in enumerate(side_uses(False))}
        self.n_head = len(self.head) + 2
        self.body = {}
        for first in (True, False):
            n, table = 0, {}
            for r in range(2):
                sides = side_uses(r == 0 and not first)
                for t in range(TURN_TILES):
                    if t % NBLK == 0:
                        for i in range(2):
                            table[r, "C", t // NBLK + 1, i] = n
                            n += 1
                    for at, key, i in sides:
                        if at == t:
                            table[r, key, i] = n
                            n += 1
            self.body[first] = (table, n)

    def base(self, b, first):
        if first:
            return self.n_head
        return b * self.body[False][1] + (self.n_head + self.body[True][1] - self.body[False][1])


def cross_scan_layer(nc, name, x_cm, g_cm, ident, cols_e, hbm, rank, eps):
    DIRS, NT, RANKS = 2, TURN_TILES, 32 + rank
    NJ = DIRS * NBLK // 2
    bank = BankUses()
    with cleared(nc) as (ctx, sems):
        def sb(n, shape, dt=F32):
            return ctx.enter_context(nc.sbuf_tensor(f"{name}_{n}", shape, dt))

        def sem(n):
            sems.append(nc.alloc_semaphore(name=f"{name}_{n}"))
            return sems[-1]

        w_u = sb("w_u", [C, 2 * DI])
        w_z = sb("w_z", [C, 256])
        w_bc_a = sb("w_bc_a", [128, 4, 128])
        w_bc_b = sb("w_bc_b", [BLK, 4, 128])
        w_dt = sb("w_dt", [RANKS, 2, 128 * NJ])
        dt_bias = sb("dt_bias", [128, 2, NJ])
        a_neg = sb("a_neg", [128, 4, NBLK, NP])
        skip_w = sb("skip_w", [128, 2, DIRS, 2])
        skip_sum = sb("skip_sum", [128, 2, 2])
        skip_diag = sb("skip_diag", [128, 2, 2, 128])
        norm_w = sb("norm_w", [128, 2, 2])
        w_o_a = sb("w_o_a", [128, C])
        w_o_b = sb("w_o_b", [BLK, C])
        pick = sb("pick", [128, 2 * NS, BLK], BF16)
        fold = sb("fold", [128, 3 * BLK])
        mean_w = sb("mean_w", [128, 128])
        eps_col = sb("eps_col", [128, 1])
        loads = [(w_u, "w_u"), (w_z, "w_z"), (w_bc_a, "w_bc_a"), (w_bc_b, "w_bc_b"), (w_dt, "w_dt"), (dt_bias, "dt_bias"), (a_neg, "a_logs"), (skip_w, "skip"),
                 (norm_w, "norm"), (w_o_a, "w_o_a"), (w_o_b, "w_o_b")]

        u = sb("u", [128, NJ, L])
        ranks = sb("ranks", [RANKS, L])
        bc = sb("bc", [128, 2, DIRS, L], BF16)
        t_e, t_l, t_r, t_w = (sb(n, [128, L]) for n in ("t_e", "t_l", "t_r", "t_w"))
        delta = sb("delta", [128, NJ, L])
        du = sb("du", [128, NJ, L])
        delta2 = sb("delta2", [128, DIRS * NBLK, L])
        du2 = sb("du2", [128, DIRS * NBLK, L])
        decay = sb("decay", [128, DEPTH, L])
        state = sb("state", [128, DEPTH, L])
        read = sb("read", [128, READS, L])
        c_rows = sb("c_rows", [128, 2, L])
        y_a = sb("y_a", [128, L])
        y_b = sb("y_b", [BLK, L])
        e_of = [t_e, t_r, t_e]
        raw_of = [t_w, t_l]

        y_ps = ctx.enter_context(nc.psum_tensor(f"{name}_y_ps", [128, 3, HALF], F32))
        pair_ps = [ctx.enter_context(nc.psum_tensor(f"{name}_pair_ps{k}", [128, L], F32)) for k in range(2)]
        side_ps = ctx.enter_context(nc.psum_tensor(f"{name}_side_ps", [128, HALF], F32))
        y_flat = y_ps[:, 0:2, :].rearrange("p a n -> p (a n)")

        (weights, set_up, consts, ranked, side_ready, side_free, bc_hi, bc_rest, bc_mid, bc_ready, sp_abs, sp_exp, sp_one,
         sp_log, sp_part, sp_delta, decay_ready, scanned, injected, b_ready, multiplied, y_added, y_free, y_out,
         joined, centred, squared, logged, rooted, scaled, affine, silued, gated, x_added) = (
            sem(s) for s in (
                "weights", "set_up", "consts", "ranked", "side_ready", "side_free", "bc_hi", "bc_rest", "bc_mid", "bc_ready",
                "sp_abs", "sp_exp", "sp_one", "sp_log", "sp_part", "sp_delta", "decay_ready", "scanned", "injected",
                "b_ready", "multiplied", "y_added", "y_free", "y_out", "joined", "centred", "squared", "logged",
                "rooted", "scaled", "affine", "silued", "gated", "x_added"))
        delta2_in = [sem(f"delta2_in{d}") for d in range(DIRS)]
        du2_in = [sem(f"du2_in{d}") for d in range(DIRS)]
        PER_DIR = 16 * 2 * NBLK
        MULT0, SCAN0, SUM0 = DEPTH + 2, DEPTH, READS

        class Turn:

            def __init__(self, b, r, first):
                self.b, self.r, self.first = b, r, first
                self.number = b * 2 + r
                self.finish = r == 0 and not first
                self.table, self.base = bank.body[first][0], bank.base(b, first)
                self.next = self.number + 1
                self.next_image = b if r == 0 else ((b + 1) % B)
                self.next_order = 1 - r
                self.done_image = b - 1 if self.finish else None

            def use(self, *key):
                return self.table[(self.r, *key)] + self.base

        class Head:
            next, next_image, next_order, done_image, finish = 0, 0, 0, None, False

            def use(self, key, i):
                return bank.head[key, i]

        class Tail:
            done_image, finish = B - 1, True
            base = bank.base(B, False)

            def use(self, key, i):
                order = [(k, h) for _, k, h in side_uses(True) if k in FINISH]
                return self.base + order.index((key, i))

        def over_turns(eng, turn):
            for r in range(2):
                turn(Turn(0, r, True))
            with eng.Fori(1, B) as b:
                for r in range(2):
                    turn(Turn(b, r, False))

        def wait_side(eng, n):
            eng.wait_ge(side_free, n + 2)

        block = ctx.enter_context(nc.Block())
        tiles = [(d, p, c) for d in range(DIRS) for p in range(NP) for c in range(NBLK)]
        n_setup = 3 + 2 * (1 + 2) + 2 * NS + 3

        @block.sync
        def _(sp):
            for t, key in loads:
                sp.dma_start(t[tuple(slice(None) for _ in t.shape)], hbm[key]).then_inc(weights, 16)

            def copy_blocks(n, q):
                j, half = q // 2, q % 2
                rows = slice(half * BLK, half * BLK + BLK)
                sp.wait_ge(sp_delta, n * 2 * NJ + 2 * j + 2)
                for side in range(2):
                    to = slice(side * BLK, side * BLK + BLK)
                    sp.dma_start(delta2[to, q, :], delta[rows, j, :]).then_inc(delta2_in[q // NBLK], 16)
                    sp.dma_start(du2[to, q, :], du[rows, j, :]).then_inc(du2_in[q // NBLK], 16)

            def copies(n, running):
                if running:
                    sp.wait_ge(y_added, n * NT - NT // 2 + SUM0)
                for q in range(NBLK):
                    copy_blocks(n, q)
                sp.wait_ge(y_added, n * NT + SUM0)
                for q in range(NBLK, 2 * NBLK):
                    copy_blocks(n, q)

            copies(0, False)
            over_turns(sp, lambda turn: copies(turn.next, True))
            for d in range(DIRS):
                sp.wait_ge(delta2_in[d], (2 * B + 1) * PER_DIR)
                sp.wait_ge(du2_in[d], (2 * B + 1) * PER_DIR)

        @block.tensor
        def _(pe):
            pe.wait_ge(weights, 16 * len(loads))
            pe.wait_ge(set_up, n_setup)

            def g_half(image, order, i):
                img = g_cm[:, bass.ts(image, L)]
                if order == 0:
                    return img[:, i * HALF:(i + 1) * HALF]
                return img.rearrange("p (h w) -> p w h", w=W)[:, i * (W // 2):(i + 1) * (W // 2), :]

            def side(turn, key, i):
                kind, j = key
                n, s = turn.use(key, i), slice(i * HALF, (i + 1) * HALF)
                if kind == "u":
                    o = turn.next_order
                    rows, parts = 128, [(w_u[:, j * 128:(j + 1) * 128], g_half(turn.next_image, o, i))]
                elif kind == "bc":
                    k = turn.next_order * 2 + j
                    wait_side(pe, turn.use(("u", 1), 1))
                    rows, parts = 128, [(w_bc_a[:, k, :], u[:, 0, s]), (w_bc_b[:, k, :], u[0:BLK, 1, s])]
                elif kind == "dt":
                    pe.wait_ge(ranked, turn.next * 4 + 4)
                    rows, parts = 128, [(w_dt[:, turn.next_order, j * 128:(j + 1) * 128], ranks[:, s])]
                elif kind == "z":
                    rows, parts = 128, [(w_z[:, j * 128:(j + 1) * 128], g_half(turn.done_image, 0, i))]
                elif kind == "mean":
                    pe.wait_ge(joined, 2 * turn.done_image + 2)
                    rows, parts = 128, [(mean_w[:, :], y_a[:, s]), (mean_w[0:BLK, :], y_b[:, s])]
                elif kind == "var":
                    pe.wait_ge(squared, 2 * turn.done_image + 2)
                    rows, parts = 128, [(mean_w[:, :], t_e[:, s]), (mean_w[0:BLK, :], t_r[0:BLK, s])]
                else:
                    pe.wait_ge(gated, 2 * turn.done_image + 2)
                    rows, parts = C, [(w_o_a[:, :], y_a[:, s]), (w_o_b[:, :], y_b[:, s])]
                pe.wait_ge(side_free, n + 1)
                for k, (lhs, rhs) in enumerate(parts):
                    m = nc.tensor.matmul(side_ps[0:rows, :], lhs, rhs, start=(k == 0), stop=(k == len(parts) - 1))
                m.then_inc(side_ready, 1)

            def spread_rows(number, order, g, use):
                d, p = g // NP, g % NP
                pe.wait_ge(bc_ready, number * 2 + d + 1)
                pe.wait_ge(scanned, (number * GROUPS + g) * NBLK - 1 + SCAN0)
                for i, s in halves():
                    m = nc.tensor.matmul(pair_ps[g % 2][:, s], pick[:, 2 * p:2 * p + 2, :], bc[:, order, d, s],
                                         start=True, stop=True)
                m.then_inc(b_ready, 1)
                for i, s in halves():
                    pe.wait_ge(side_free, use + i + 1)
                    nc.tensor.matmul(side_ps[:, :], pick[:, NS + 2 * p:NS + 2 * p + 2, :], bc[:, order, d, s],
                                     start=True, stop=True).then_inc(side_ready, 1)

            def turn_of(turn):
                o, number = turn.r, turn.number
                sides = side_uses(turn.finish)
                for t, (d, p, c) in enumerate(tiles):
                    if c == 0:
                        g, use = t // NBLK + 1, turn.use("C", t // NBLK + 1, 0)
                        if g < GROUPS:
                            spread_rows(number, o, g, use)
                        else:
                            spread_rows(turn.next, turn.next_order, 0, use)
                    for at, key, i in sides:
                        if at == t:
                            side(turn, key, i)
                    if t == 0:
                        pe.wait_ge(y_free, number + 1)
                    pe.wait_ge(multiplied, number * NT + t + 1 + MULT0)
                    for i, s in halves():
                        src = read[:, t % READS, s]
                        if c < 2:
                            lhs = fold[:, BLK * (1 - c):BLK * (1 - c) + 128]
                            m = nc.tensor.matmul(y_ps[:, i, :], lhs, src, start=(t == 0), stop=(t == NT - 2))
                        else:
                            m = nc.tensor.matmul(y_ps[i * BLK:(i + 1) * BLK, 2, :], fold[:, BLK:2 * BLK], src,
                                                 start=(t == 2), stop=(t == NT - 1), skip_group_check=True)
                    m.then_inc(y_added, 1)
                    if t == 3:
                        for i, s in halves():
                            nc.tensor.matmul(y_ps[:, i, :], skip_diag[:, o, 0, :], u[:, 0, s], start=False, stop=False)
                    if t == 6:
                        for i, s in halves():
                            nc.tensor.matmul(y_ps[i * BLK:(i + 1) * BLK, 2, :], skip_diag[0:BLK, o, 1, 0:BLK],
                                             u[0:BLK, 1, s], start=False, stop=False, skip_group_check=True)

            for _, key, i in side_uses(False):
                side(Head(), key, i)
            spread_rows(0, 0, 0, bank.n_head - 2)
            over_turns(pe, turn_of)
            for _, key, i in side_uses(True):
                if key in FINISH:
                    side(Tail(), key, i)

        @block.scalar
        def _(act):
            act.preload_act_table_set("natural_log_exp_and_others")
            act.wait_ge(weights, 16 * len(loads))
            nc.scalar.activation(a_neg[:, :, :, :], a_neg[:, :, :, :], ACT.Exp).then_inc(consts, 1)
            act.wait_ge(consts, 1)
            nc.scalar.mul(a_neg[:, :, :, :], a_neg[:, :, :, :], -1.0).then_inc(consts, 1)
            act.wait_ge(consts, 2)
            act.wait_ge(set_up, n_setup)

            def take(turn, key, i):
                kind, j = key
                n, s = turn.use(key, i), slice(i * HALF, (i + 1) * HALF)
                act.wait_ge(side_ready, n + 1)
                if kind == "u":
                    ins = nc.scalar.copy(u[:, j, s], side_ps[:, :])
                elif kind == "bc":
                    if turn.finish:
                        act.wait_ge(gated, 2 * turn.done_image + 2)
                    nc.scalar.copy(ranks[32 * j:32 * j + rank, s], side_ps[32:32 + rank, :]).then_inc(ranked, 1)
                    ins = nc.scalar.copy(raw_of[j][:, s], side_ps[:, :])
                elif kind == "dt":
                    bias = dt_bias[:, turn.next_order, j:j + 1]
                    if not isinstance(turn, Head):
                        for d in range(DIRS):
                            act.wait_ge(delta2_in[d], turn.next * PER_DIR)
                        act.wait_ge(sp_delta, turn.next * 2 * NJ)
                    if j == 2:
                        act.wait_ge(sp_delta, turn.next * 2 * NJ + 1)
                    nc.scalar.activation(e_of[j][:, s], side_ps[:, :], ACT.Abs, bias=bias).then_inc(sp_abs, 1)
                    ins = nc.scalar.activation(delta[:, j, s], side_ps[:, :], ACT.Relu, bias=bias)
                elif kind == "z":
                    if j == 1:
                        act.wait_ge(joined, 2 * turn.done_image + 2)
                    ins = nc.scalar.copy((t_w[:, s], t_l[:, s])[j], side_ps[:, :])
                elif kind == "mean":
                    ins = nc.scalar.copy(t_r[:, s], side_ps[:, :])
                elif kind == "var":
                    ins = nc.scalar.activation(t_e[:, s], side_ps[:, :], ACT.Ln, bias=eps_col[:, :])
                else:
                    if not isinstance(turn, Tail):
                        act.wait_ge(sp_delta, turn.next * 2 * NJ + 3)
                    ins = nc.scalar.copy(t_r[0:C, s], side_ps[0:C, :])
                ins.then_inc(side_free, 1)

            def step(turn, kind, j):
                if kind in FINISH_STEPS:
                    done = turn.done_image
                if kind == "square":
                    act.wait_ge(centred, 2 * done + 2)
                    if j == 0:
                        nc.scalar.activation(t_e[:, :], y_a[:, :], ACT.Square).then_inc(squared, 1)
                    else:
                        nc.scalar.activation(t_r[0:BLK, :], y_b[:, :], ACT.Square).then_inc(squared, 1)
                elif kind == "silu":
                    wait_side(act, turn.use(("z", 1), 1))
                    nc.scalar.activation(t_w[:, :], t_w[:, :], ACT.Silu).then_inc(silued, 1)
                    nc.scalar.activation(t_l[0:BLK, :], t_l[0:BLK, :], ACT.Silu).then_inc(silued, 1)
                    act.preload_act_table_set("natural_log_exp_and_others")
                elif kind == "rstd":
                    wait_side(act, turn.use(("var", 0), 1))
                    nc.scalar.activation(t_e[:, :], t_e[:, :], ACT.Exp, scale=-0.5).then_inc(rooted, 1)
                elif kind == "affine":
                    act.wait_ge(scaled, 2 * done + 2)
                    y, r = ((y_a, 128), (y_b, BLK))[j]
                    nc.scalar.activation(y[:, :], y[:, :], ACT.Identity, bias=norm_w[0:r, 1, j:j + 1],
                                         scale=norm_w[0:r, 0, j:j + 1]).then_inc(affine, 1)
                elif kind == "hi":
                    wait_side(act, turn.use(("bc", j), 1))
                    nc.scalar.copy(bc[:, turn.next_order, j, :], raw_of[j][:, :]).then_inc(bc_hi, 1)
                elif kind == "mid":
                    act.wait_ge(bc_rest, turn.next * 2 + j + 1)
                    nc.scalar.copy(bc[BLK:128, turn.next_order, j, :], raw_of[j][BLK:128, :]).then_inc(bc_mid, 1)
                elif kind == "exp":
                    act.wait_ge(sp_abs, (turn.next * NJ + j) * 2 + 2)
                    nc.scalar.activation(e_of[j][:, :], e_of[j][:, :], ACT.Exp, scale=-1.0).then_inc(sp_exp, 1)
                else:
                    n = turn.next * NJ + j
                    act.wait_ge(sp_exp, n + 1)
                    act.wait_ge(bc_ready, turn.next * 2 + 2)
                    if j > 0:
                        act.wait_ge(sp_part, n * 2)
                    nc.scalar.activation(t_w[:, :], e_of[j][:, :], ACT.Identity, bias=1.0).then_inc(sp_one, 1)
                    act.wait_ge(sp_one, n + 1)
                    nc.scalar.activation(t_l[:, :], t_w[:, :], ACT.Ln).then_inc(sp_log, 1)

            def take_y(number, order):
                act.wait_ge(y_added, (number + 1) * NT + SUM0)
                to_a, to_b = (y_a, y_b) if order == 0 else (t_e, t_l)
                if order == 1:
                    act.wait_ge(sp_delta, (number + 2) * 2 * NJ)
                    act.wait_ge(sp_part, (number + 2) * 2 * NJ)
                nc.scalar.copy(to_a[:, :], y_flat).then_inc(y_out, 1)
                for i, s in halves():
                    nc.scalar.copy(to_b[0:BLK, s], y_ps[i * BLK:(i + 1) * BLK, 2, :]).then_inc(y_out, 1)
                act.wait_ge(y_out, 3 * (number + 1))
                act.sem_inc(y_free, 1)

            def copy_c(G, slot, use):
                act.wait_ge(multiplied, G * NBLK + 1)
                for i, s in halves():
                    act.wait_ge(side_ready, use + i + 1)
                    nc.scalar.copy(c_rows[:, slot, s], side_ps[:, :]).then_inc(side_free, 1)

            def turn_of(turn):
                o, number = turn.r, turn.number
                sides = side_uses(turn.finish)
                for t, (d, p, c) in enumerate(tiles):
                    if p == 0 and c == 0:
                        act.wait_ge(delta2_in[d], (number + 1) * PER_DIR)
                    act.wait_ge(scanned, number * NT + t - DEPTH + 1 + SCAN0)
                    nc.scalar.activation(decay[:, t % DEPTH, :], delta2[:, d * NBLK + c, :], ACT.Exp,
                                         scale=a_neg[:, o * 2 + d, c, p:p + 1]).then_inc(decay_ready, 1)
                    for at, key, i in sides:
                        if at == t - LAG:
                            take(turn, key, i)
                    if c == 0:
                        g = t // NBLK
                        if g > 0:
                            use = turn.use("C", g, 0)
                        else:
                            use = turn.base - 2 if o == 0 else bank.body[turn.first][0][0, "C", GROUPS, 0] + turn.base
                        copy_c(number * GROUPS + g, g % 2, use)
                    if t == 2 and not (turn.first and o == 0):
                        take_y(number - 1, 1 - o)
                    for kind, j in ACT_STEPS.get(t, []):
                        if turn.finish or kind not in FINISH_STEPS:
                            step(turn, kind, j)

            for _, key, i in side_uses(False):
                take(Head(), key, i)
                if i == 1 and key[0] == "bc":
                    step(Head(), "hi", key[1])
                    step(Head(), "mid", key[1])
                if i == 1 and key[0] == "dt":
                    step(Head(), "exp", key[1])
                    step(Head(), "log", key[1])
            over_turns(act, turn_of)
            copy_c(2 * B * GROUPS, 0, Tail.base - 2)
            take_y(2 * B - 1, 1)
            for _, key, i in side_uses(True):
                if key in FINISH:
                    take(Tail(), key, i)
                    if (key, i) == (("mean", 0), 1):
                        step(Tail(), "square", 0)
                        step(Tail(), "square", 1)
                    if (key, i) == (("z", 1), 1):
                        step(Tail(), "silu", 0)
                    if (key, i) == (("var", 0), 1):
                        step(Tail(), "rstd", 0)
                        step(Tail(), "affine", 0)
                        step(Tail(), "affine", 1)

        @block.gpsimd
        def _(pool):
            def step(turn, kind, j):
                if kind == "delta":
                    pool.wait_ge(sp_part, (turn.next * NJ + j) * 2 + 2)
                    nc.gpsimd.tensor_tensor(delta[:, j, :], delta[:, j, :], e_of[j][:, :],
                                            ALU.subtract).then_inc(sp_delta, 1)
                else:
                    if not isinstance(turn, Head):
                        for d in range(DIRS):
                            pool.wait_ge(du2_in[d], turn.next * PER_DIR)
                    pool.wait_ge(sp_delta, (turn.next * NJ + j) * 2 + 1)
                    nc.gpsimd.tensor_tensor(du[:, j, :], delta[:, j, :], u[:, j, :], ALU.mult).then_inc(sp_delta, 1)

            def turn_of(turn):
                number = turn.number
                for t in range(NT):
                    g = t // NBLK
                    pool.wait_ge(scanned, number * NT + t + 1 + SCAN0)
                    if t % NBLK == 0:
                        if g > 0:
                            use = turn.use("C", g, 1)
                        else:
                            use = turn.base - 1 if turn.r == 0 else (
                                bank.body[turn.first][0][0, "C", GROUPS, 1] + turn.base)
                        wait_side(pool, use)
                    pool.wait_ge(y_added, number * NT + t - READS + 1 + SUM0)
                    nc.gpsimd.tensor_tensor(read[:, t % READS, :], state[:, t % DEPTH, :], c_rows[:, g % 2, :],
                                            ALU.mult).then_inc(multiplied, 1)
                    for kind, j in POOL_STEPS.get(t, []):
                        step(turn, kind, j)

            for j in range(NJ):
                step(Head(), "delta", j)
                step(Head(), "du", j)
            over_turns(pool, turn_of)

        @block.vector
        def _(dve):
            for s, n in ((scanned, SCAN0), (multiplied, MULT0), (y_added, SUM0), (injected, 1), (side_free, 1),
                         (y_free, 1)):
                for _ in range(n):
                    dve.sem_inc(s, 1)
            n = [0]

            def setup(ins):
                n[0] += 1
                ins.then_inc(set_up, 1)

            dve.wait_ge(weights, 16 * len(loads))
            setup(nc.vector.memset(mean_w[:, :], 1.0 / DI))
            setup(nc.vector.memset(eps_col[:, :], eps))
            setup(nc.vector.memset(ranks[:, :], 0.0))
            for m in range(2 * NS):
                src = (m // NS) * NS + (m % NS) // 2 + NP * (m % 2)
                setup(nc.vector.tensor_copy(pick[:, m, :], cols_e[:, src:src + 1].to_broadcast([128, BLK])))
            for side in (0, 2):
                setup(nc.vector.memset(fold[:, side * BLK:(side + 1) * BLK], 0.0))
            setup(nc.vector.tensor_tensor(fold[:, BLK:2 * BLK], ident[:, 0:BLK], ident[:, BLK:128], ALU.add))
            for o in range(2):
                setup(nc.vector.tensor_tensor(skip_sum[:, o, :], skip_w[:, o, 0, :], skip_w[:, o, 1, :], ALU.add))
            dve.wait_ge(set_up, n[0])
            for o in range(2):
                for j in range(2):
                    setup(nc.vector.tensor_scalar(skip_diag[:, o, j, :], ident, skip_sum[:, o, j:j + 1], None,
                                                  ALU.mult))
            assert n[0] == n_setup

            def step(turn, kind, j):
                if kind in FINISH_STEPS:
                    done = turn.done_image
                    y, t_of, r = ((y_a, (t_e, t_r, t_w), 128), (y_b, (t_l, t_r, t_l), BLK))[j]
                if kind == "join":
                    dve.wait_ge(y_out, 6 * done + 6)
                    dst = y[:, :].rearrange("p (h w) -> p w h", w=W)
                    nc.vector.tensor_tensor(dst, dst, t_of[0][0:r, :].rearrange("p (w h) -> p w h", h=H),
                                            ALU.add).then_inc(joined, 1)
                elif kind == "centre":
                    wait_side(dve, turn.use(("mean", 0), 1))
                    nc.vector.tensor_tensor(y[:, :], y[:, :], t_r[0:r, :], ALU.subtract).then_inc(centred, 1)
                elif kind == "scale":
                    dve.wait_ge(rooted, done + 1)
                    nc.vector.tensor_tensor(y[:, :], y[:, :], t_e[0:r, :], ALU.mult).then_inc(scaled, 1)
                elif kind == "gate":
                    dve.wait_ge(affine, 2 * done + 2)
                    dve.wait_ge(silued, 2 * done + 2)
                    nc.vector.tensor_tensor(y[:, :], y[:, :], t_of[2][0:r, :], ALU.mult).then_inc(gated, 1)
                elif kind == "residual":
                    wait_side(dve, turn.use(("out", 0), 1))
                    xs = x_cm[:, bass.ts(done, L)]
                    nc.vector.tensor_tensor(xs, xs, t_r[0:C, :], ALU.add).then_inc(x_added, 1)
                elif kind == "rest":
                    dve.wait_ge(bc_hi, turn.next * 2 + j + 1)
                    raw = raw_of[j][BLK:128, :]
                    nc.vector.tensor_tensor(raw, raw, bc[BLK:128, turn.next_order, j, :],
                                            ALU.subtract).then_inc(bc_rest, 1)
                elif kind == "lo":
                    dve.wait_ge(bc_mid, turn.next * 2 + j + 1)
                    low = bc[96:128, turn.next_order, j, :]
                    nc.vector.tensor_tensor(low, raw_of[j][96:128, :], low, ALU.subtract).then_inc(bc_ready, 1)
                elif kind == "fix":
                    dve.wait_ge(sp_log, turn.next * NJ + j + 1)
                    nc.vector.scalar_tensor_tensor(out=t_w[:, :], in0=t_w[:, :], scalar=1.0, in1=t_l[:, :],
                                                   op0=ALU.subtract, op1=ALU.subtract).then_inc(sp_part, 1)
                else:
                    dve.wait_ge(sp_part, (turn.next * NJ + j) * 2 + 1)
                    nc.vector.scalar_tensor_tensor(out=e_of[j][:, :], in0=t_w[:, :], scalar=0.0, in1=e_of[j][:, :],
                                                   op0=ALU.max, op1=ALU.subtract).then_inc(sp_part, 1)

            def turn_of(turn):
                number = turn.number
                for t, (d, p, c) in enumerate(tiles):
                    T = number * NT + t
                    if p == 0 and c == 0:
                        dve.wait_ge(du2_in[d], (number + 1) * PER_DIR)
                    if c == 0:
                        dve.wait_ge(b_ready, number * GROUPS + t // NBLK + 1)
                    dve.wait_ge(scanned, T + SCAN0)
                    b_ps = pair_ps[p % 2]
                    inject_ps = pair_ps[(p + (c < 2)) % 2]
                    nc.vector.tensor_tensor(inject_ps[:, :], du2[:, d * NBLK + c, :], b_ps[:, :],
                                            ALU.mult).then_inc(injected, 1)
                    dve.wait_ge(injected, T + 1 + 1)
                    dve.wait_ge(decay_ready, T + 1)
                    dve.wait_ge(multiplied, T - DEPTH + 1 + MULT0)
                    way = slice(None, None, 1 if d == 0 else -1)
                    nc.vector.tensor_tensor_scan(state[:, t % DEPTH, way], decay[:, t % DEPTH, way],
                                                 inject_ps[:, way], 0.0, ALU.mult, ALU.add).then_inc(scanned, 1)
                    for kind, j in DVE_STEPS.get(t, []):
                        if turn.finish or kind not in FINISH_STEPS:
                            step(turn, kind, j)

            for j in range(DIRS):
                step(Head(), "rest", j)
                step(Head(), "lo", j)
            for j in range(NJ):
                step(Head(), "fix", j)
                step(Head(), "part", j)
            over_turns(dve, turn_of)
            for kind in ("join", "centre", "scale", "gate"):
                for j in range(2):
                    step(Tail(), kind, j)
            step(Tail(), "residual", 0)


def network(nc, hbm, out):
    with ExitStack() as ctx:
        def sb(n, shape):
            return ctx.enter_context(nc.sbuf_tensor(n, shape, F32))

        x_cm = sb("x_cm", [C, B * L])
        g_cm = sb("g_cm", [C, B * L])
        ident = sb("ident", [128, 128])
        group_mean = sb("group_mean", [C, C])
        state_cols = sb("state_cols", [128, 2 * NS])
        row_cols = sb("row_cols", [128, 3])
        loaded = ctx.enter_context(nc.semaphore("loaded"))
        stored = ctx.enter_context(nc.semaphore("stored"))
        with nc.Block() as block:
            @block.sync
            def _(sp):
                sp.dma_start(x_cm[:, :], hbm["x"]).then_inc(loaded, 16)
                sp.dma_start(ident[:, :], hbm["ident"]).then_inc(loaded, 16)
                sp.dma_start(group_mean[:, :], hbm["group_mean"]).then_inc(loaded, 16)
                sp.dma_start(state_cols[:, :], hbm["state_cols"]).then_inc(loaded, 16)
                sp.dma_start(row_cols[:, :], hbm["row_cols"]).then_inc(loaded, 16)
                sp.wait_ge(loaded, 5 * 16)

        def ssm(n, orders, dirs, rank, conv, eps):
            weights = {k[3:]: v for k, v in hbm.items() if k.startswith(n + "_")}
            group_norm(nc, f"{n}_gn", x_cm[:, :], g_cm[:, :], group_mean[:, :])
            if conv:
                scan_layer(nc, n, x_cm, g_cm, ident[:, :], state_cols, weights, orders, dirs, rank, conv, eps)
            else:
                cross_scan_layer(nc, n, x_cm, g_cm, ident[:, :], state_cols, weights, rank, eps)

        ssm("L0", 2, 2, 12, False, 1e-6)
        group_norm(nc, "L1_gn", x_cm[:, :], g_cm[:, :], group_mean[:, :])
        motif_layer(nc, x_cm[:, :], g_cm[:, :], ident[:, :], row_cols)
        ssm("L2", 1, 1, 6, True, 1e-5)
        ssm("L3", 2, 2, 12, False, 1e-6)
        with nc.Block() as block:
            @block.sync
            def _(sp):
                sp.dma_start(out, x_cm[:, :]).then_inc(stored, 16)
                sp.wait_ge(stored, 16)


def _ssm_arrays(np, n, in_w, out_w, xp, dtw, dtb, a_logs, ds, norm_w, norm_b, orders, dirs):
    K, rank = dtw.shape[0], dtw.shape[2]
    ks = [[o + orders * d for d in range(dirs)] for o in range(orders)]
    flat = [k for o in ks for k in o]
    nj = -(-dirs * NBLK // 2)

    def tiles(v):
        r = np.zeros((256,), np.float32)
        r[:DI] = v
        return r.reshape(2, 128).T

    wt = in_w.T
    r = {"w_u": np.concatenate([wt[:, :DI], wt[:, :DI]], 1), "w_z": np.concatenate([wt[:, DI:], wt[:, DI:DI + BLK]], 1)}
    bc = np.stack([np.tile(xp[k, rank:].T, (1, 4)) for k in flat], 1)
    if dirs == 2:
        for i, k in enumerate(flat):
            bc[:, i, 32:32 + rank] = xp[k, :rank].T
    r["w_bc_a"], r["w_bc_b"] = bc[:128], bc[128:]
    if dirs == 1:
        rk = np.stack([np.concatenate([xp[k, :rank].T for k in o], 1) for o in ks], 1)
        r["w_r_a"], r["w_r_b"] = rk[:128], rk[128:]
    w_dt = np.zeros((32 * (dirs - 1) + rank, orders, 128 * nj), np.float32)
    bias = np.zeros((orders, 128 * nj), np.float32)
    for o in range(orders):
        for d, k in enumerate(ks[o]):
            w_dt[32 * d:32 * d + rank, o, d * DI:(d + 1) * DI] = dtw[k].T
            bias[o, d * DI:(d + 1) * DI] = dtb[k]
    r["w_dt"] = w_dt
    r["dt_bias"] = bias.reshape(orders, nj, 128).transpose(2, 0, 1)
    a = a_logs.reshape(K, NBLK, BLK, 2, NP)[flat]
    r["a_logs"] = a.transpose(3, 2, 0, 1, 4).reshape(128, len(flat), NBLK, NP)
    d = ds.reshape(K, DI)
    r["skip"] = np.stack([np.stack([tiles(d[k]) for k in o], 1) for o in ks], 1)
    r["norm"] = np.stack([tiles(norm_w), tiles(norm_b)], 1)
    r["w_o_a"], r["w_o_b"] = out_w.T[:128], out_w.T[128:]
    return {f"{n}_{k}": v for k, v in r.items()}, tiles


def kernel(**inputs):
    import numpy as np
    import concourse.bacc as _bacc
    from concourse.bass_utils import run_bass_kernel_spmd as _run

    v = {k: np.asarray(a) for k, a in inputs.items()}
    arrays = {"x": v["x"].reshape(B * L, C).T, "ident": np.eye(128, dtype=np.float32)}
    group = np.arange(C) // (C // 32)
    arrays["group_mean"] = (group[:, None] == group[None, :]).astype(np.float32) / np.float32(C // 32)
    rows = np.arange(128)
    part = np.arange(128) // 32
    arrays["state_cols"] = ((rows[:, None] % 32 == np.arange(32)[None, :]) & (part != 1)[:, None]).astype(np.float32)
    arrays["row_cols"] = np.stack([rows % 2 == 0, rows % 2 == 1, rows >= H], 1).astype(np.float32)
    for n in ("L0", "L3"):
        g = lambda s: v[f"{n}_conv_{s}"]
        a, _ = _ssm_arrays(np, n, g("in_proj_weight"), g("out_proj_weight"), g("x_proj_weight"),
                           g("dt_projs_weight"), g("dt_projs_bias"), g("A_logs"), g("Ds"), g("out_norm_weight"),
                           g("out_norm_bias"), 2, 2)
        arrays.update(a)
    g = lambda s: v[f"L2_conv_{s}"]
    a, tiles = _ssm_arrays(np, "L2", g("in_proj_w"), g("out_proj_w"), g("x_proj_w")[None], g("dt_proj_w")[None],
                           g("dt_proj_b")[None], g("A_log"), g("Ds"), g("ln_g"), g("ln_b"), 1, 1)
    arrays.update(a)
    cw = g("conv_w").reshape(DI, 9)
    arrays["L2_conv_w"] = np.stack([tiles(cw[:, k]) for k in range(9)], 2)
    arrays["L2_in_bias"] = np.stack([tiles(g("in_proj_b")[:DI]), tiles(g("in_proj_b")[DI:])], 1)
    arrays["L2_conv_b"] = tiles(g("conv_b"))
    arrays["L2_out_bias"] = g("out_proj_b").reshape(C, 1)
    arrays = {f"in_{k}": np.ascontiguousarray(a) for k, a in arrays.items()}

    nc = _bacc.Bacc("TRN2", target_bir_lowering=False, num_devices=1)
    hbm = {k[3:]: nc.dram_tensor(k, a.shape, mybir.dt.from_np(a.dtype), kind="ExternalInput").ap()
           for k, a in arrays.items()}
    out = nc.dram_tensor("out_y", [C, B * L], F32, kind="ExternalOutput").ap()
    network(nc, hbm, out)
    r = _run(nc, [arrays], core_ids=[0])
    return np.ascontiguousarray(r.results[0]["out_y"].T).reshape(B, H, W, C)
```

```python
from contextlib import ExitStack, contextmanager

import concourse.bass as bass
from concourse import mybir

F32 = mybir.dt.float32
BF16 = mybir.dt.bfloat16
ALU = mybir.AluOpType
ACT = mybir.ActivationFunctionType

B, H, W, C = 4, 32, 32, 96
L = H * W
DI = 192
NS = 16
HALF = 512
BLK = 64
NBLK = DI // BLK
NP = NS // 2
RING = 3
ROUND = 12582912.0
GN_EPS = 1e-5


def halves():
    return [(i, slice(i * HALF, (i + 1) * HALF)) for i in range(L // HALF)]


@contextmanager
def cleared(nc):
    sems = []
    with ExitStack() as ctx:
        yield ctx, sems
    nc.clear_and_free_semaphores(sems)
    nc.all_engine_barrier()


def group_norm(nc, name, x_cm, g_cm, group_mean):
    with cleared(nc) as (ctx, sems):
        def sb(n, shape):
            return ctx.enter_context(nc.sbuf_tensor(f"{name}_{n}", shape, F32))

        def sem(n):
            sems.append(nc.alloc_semaphore(name=f"{name}_{n}"))
            return sems[-1]

        stats = sb("stats", [C, B, 2, 6])
        mv = sb("mv", [C, B, 2])
        spread = sb("spread", [C, B])
        mean = sb("mean", [C, B])
        vare = sb("vare", [C, B])
        logv = sb("logv", [C, B])
        rstd = sb("rstd", [C, B])
        newton = sb("newton", [C, B])
        eps = sb("eps", [C, 1])
        ps = ctx.enter_context(nc.psum_tensor(f"{name}_ps", [C, 2, HALF], F32))
        dve_step, means_ready, vars_ready, logs, roots = (
            sem(s) for s in ("dve_step", "means_ready", "vars_ready", "logs", "roots"))
        block = ctx.enter_context(nc.Block())
        n_stats = 2 * B + B + 1

        @block.vector
        def _(dve):
            done = [0]

            def chained(ins):
                done[0] += 1
                ins.then_inc(dve_step, 1)
                dve.wait_ge(dve_step, done[0])

            for b in range(B):
                for i in range(2):
                    chained(nc.vector.bn_stats(stats[:, b, i, :], x_cm[:, b * L + i * HALF:b * L + (i + 1) * HALF]))
                chained(nc.vector.bn_aggr(mv[:, b, :], stats[:, b, :, :]))
            chained(nc.vector.memset(eps[:, :], GN_EPS))
            dve.wait_ge(means_ready, 1)
            chained(nc.vector.tensor_copy(mean[:, :], ps[:, 0, 0:B]))
            chained(nc.vector.tensor_tensor(spread[:, :], mv[:, :, 0], mean[:, :], ALU.subtract))
            chained(nc.vector.tensor_tensor(spread[:, :], spread[:, :], spread[:, :], ALU.mult))
            chained(nc.vector.tensor_tensor(spread[:, :], spread[:, :], mv[:, :, 1], ALU.add))
            dve.wait_ge(vars_ready, 1)
            chained(nc.vector.tensor_scalar(vare[:, :], ps[:, 1, 0:B], GN_EPS, None, ALU.add))
            dve.wait_ge(roots, 1)
            chained(nc.vector.tensor_tensor(newton[:, :], rstd[:, :], rstd[:, :], ALU.mult))
            chained(nc.vector.tensor_tensor(newton[:, :], newton[:, :], vare[:, :], ALU.mult))
            chained(nc.vector.tensor_scalar(newton[:, :], newton[:, :], -0.5, 1.5, ALU.mult, ALU.add))
            chained(nc.vector.tensor_tensor(rstd[:, :], rstd[:, :], newton[:, :], ALU.mult))
            for b in range(B):
                chained(nc.vector.tensor_scalar(g_cm[:, b * L:(b + 1) * L], x_cm[:, b * L:(b + 1) * L],
                                                mean[:, b:b + 1], rstd[:, b:b + 1], ALU.subtract, ALU.mult))

        @block.tensor
        def _(pe):
            pe.wait_ge(dve_step, n_stats)
            nc.tensor.matmul(ps[:, 0, 0:B], group_mean, mv[:, :, 0], start=True, stop=True).then_inc(means_ready, 1)
            pe.wait_ge(dve_step, n_stats + 4)
            nc.tensor.matmul(ps[:, 1, 0:B], group_mean, spread[:, :], start=True, stop=True).then_inc(vars_ready, 1)

        @block.scalar
        def _(act):
            act.preload_act_table_set("natural_log_exp_and_others")
            act.wait_ge(dve_step, n_stats + 5)
            nc.scalar.activation(logv[:, :], vare[:, :], ACT.Ln).then_inc(logs, 1)
            act.wait_ge(logs, 1)
            nc.scalar.activation(rstd[:, :], logv[:, :], ACT.Exp, scale=-0.5).then_inc(roots, 1)


def motif_layer(nc, x_cm, g_cm, ident, cols):
    with cleared(nc) as (ctx, sems):
        def sb(n, shape=(128, W, C)):
            return ctx.enter_context(nc.sbuf_tensor(f"motif_{n}", list(shape), F32))

        def sem(n):
            sems.append(nc.alloc_semaphore(name=f"motif_{n}"))
            return sems[-1]

        f, below, base, own, right, diag, cross, acc, val, rnd = (
            sb(n) for n in ("f", "below", "base", "own", "right", "diag", "cross", "acc", "val", "rnd"))
        ps = ctx.enter_context(nc.psum_tensor("motif_ps", [128, 8, HALF], F32))
        turned, f_ready, below_ready, dve_step, back, added = (
            sem(s) for s in ("turned", "f_ready", "below_ready", "dve_step", "back", "added"))
        block = ctx.enter_context(nc.Block())
        g_v = g_cm.rearrange("p (q w) -> p q w", w=W)
        x_v = x_cm.rearrange("p (q w) -> p q w", w=W)
        per_bank, back_bank = 5, 4
        banks_in = -(-W // per_bank)
        banks_out = W // back_bank
        motif_steps = 2 + 4 * 5 + 9 * 3

        @block.tensor
        def _(pe):
            for k in range(banks_in):
                ws = range(k * per_bank, min((k + 1) * per_bank, W))
                if k >= 8:
                    pe.wait_ge(f_ready, k - 7)
                for j, w in enumerate(ws):
                    t = nc.tensor.transpose(ps[:, k % 8, j * C:(j + 1) * C], g_v[:, :, w], ident[0:C, 0:C])
                t.then_inc(turned, 1)
            pe.wait_ge(dve_step, motif_steps)
            pe.wait_ge(f_ready, banks_in)
            for k in range(banks_out):
                for j in range(back_bank):
                    t = nc.tensor.transpose(ps[0:C, k % 8, j * 128:(j + 1) * 128], acc[:, k * back_bank + j, :], ident)
                t.then_inc(back, 1)

        @block.scalar
        def _(act):
            for k in range(banks_in):
                a, z = k * per_bank, min((k + 1) * per_bank, W)
                act.wait_ge(turned, k + 1)
                nc.scalar.copy(f[:, a:z, :], ps[:, k % 8, 0:(z - a) * C]).then_inc(f_ready, 1)

        @block.sync
        def _(sp):
            sp.wait_ge(below_ready, 1)
            sp.wait_ge(f_ready, banks_in)
            sp.dma_start(below[0:127, :, :], f[1:128, :, :]).then_inc(below_ready, 16)

        even, odd, mask = cols[:, 0:1], cols[:, 1:2], cols[:, 2:3]
        R, S = H - 2, C - 2

        @block.vector
        def _(dve):
            done = [0]

            def chained(ins):
                done[0] += 1
                ins.then_inc(dve_step, 1)
                dve.wait_ge(dve_step, done[0])

            def floored(dst, a, b, rows, chans):
                d, v, r = (t[:, rows, chans] for t in (dst, val, rnd))
                chained(nc.vector.scalar_tensor_tensor(out=v, in0=a, scalar=0.5, in1=b, op0=ALU.mult, op1=ALU.mult))
                chained(nc.vector.tensor_scalar(r, v, ROUND, None, ALU.add))
                chained(nc.vector.tensor_scalar(r, r, ROUND, None, ALU.subtract))
                chained(nc.vector.tensor_tensor(v, r, v, ALU.is_gt))
                chained(nc.vector.tensor_tensor(d, r, v, ALU.subtract))

            nc.vector.memset(below[:, :, :], 0.0).then_inc(below_ready, 1)
            dve.wait_ge(f_ready, banks_in)
            chained(nc.vector.memset(acc[:, :, :], 0.0))
            chained(nc.vector.tensor_scalar(base[:, :, :], f[:, :, :], mask, None, ALU.mult))
            floored(own, f[:, :, :], f[:, :, :], slice(0, W), slice(0, C))
            floored(right, f[:, :, 0:C - 1], f[:, :, 1:C], slice(0, W), slice(0, C - 1))
            floored(diag, f[:, 0:W - 1, 2:C], f[:, 1:W, 0:C - 2], slice(0, W - 1), slice(2, C))
            dve.wait_ge(below_ready, 17)
            floored(cross, f[:, 2:W, 2:C], below[:, 0:W - 2, 0:C - 2], slice(2, W), slice(2, C))
            partner = [(right, own), (own, right), (diag, own), (own, right), (right, own), (own, diag),
                       (right, own), (own, right), (cross, own)]
            for k, (pe_, po_) in enumerate(partner):
                ki, kj = divmod(k, 3)
                at = (slice(None), slice(ki, ki + R), slice(kj, kj + S))
                chained(nc.vector.scalar_tensor_tensor(out=val[at], in0=pe_[at], scalar=even, in1=base[at],
                                                       op0=ALU.mult, op1=ALU.add))
                chained(nc.vector.scalar_tensor_tensor(out=val[at], in0=po_[at], scalar=odd, in1=val[at],
                                                       op0=ALU.mult, op1=ALU.add))
                chained(nc.vector.tensor_tensor(acc[at], acc[at], val[at], ALU.add))
            assert done[0] == motif_steps
            for k in range(banks_out):
                dve.wait_ge(back, k + 1)
                xs = x_v[:, :, k * back_bank:(k + 1) * back_bank].rearrange("p q w -> p w q")
                nc.vector.tensor_tensor(xs, xs, ps[0:C, k % 8, :].rearrange("p (w q) -> p w q", w=back_bank),
                                        ALU.add).then_inc(added, 1)


class Uses:

    def __init__(self, keys):
        self.index = {k: i for i, (k, _) in enumerate(keys)}
        self.buf = dict(keys)
        self.nth, count = {}, [0, 0]
        for k, b in keys:
            self.nth[k] = count[b]
            count[b] += 1
        self.count, self.total = count, len(keys)


def scan_layer(nc, name, x_cm, g_cm, ident, cols_e, hbm, orders, dirs, rank, eps):
    assert orders == dirs == 1
    NJ = -(-dirs * NBLK // 2)
    NT = dirs * NP * NBLK
    RANKS = dirs * rank
    INJECT0 = NBLK + 1
    rows_of = [min(128, dirs * DI - 128 * j) for j in range(NJ)]
    with cleared(nc) as (ctx, sems):
        def sb(n, shape, dt=F32):
            return ctx.enter_context(nc.sbuf_tensor(f"{name}_{n}", shape, dt))

        def sem(n):
            sems.append(nc.alloc_semaphore(name=f"{name}_{n}"))
            return sems[-1]

        w_u = sb("w_u", [C, 2 * DI])
        w_z = sb("w_z", [C, 256])
        w_bc_a = sb("w_bc_a", [128, orders * dirs, 128])
        w_bc_b = sb("w_bc_b", [BLK, orders * dirs, 128])
        w_r_a = sb("w_r_a", [128, orders, RANKS])
        w_r_b = sb("w_r_b", [BLK, orders, RANKS])
        w_dt = sb("w_dt", [RANKS, orders, 128 * NJ])
        dt_bias = sb("dt_bias", [128, orders, NJ])
        a_neg = sb("a_neg", [128, orders * dirs, NBLK, NP])
        skip_w = sb("skip_w", [128, orders, dirs, 2])
        skip_sum = sb("skip_sum", [128, orders, 2])
        skip_diag = sb("skip_diag", [128, orders, 2, 128])
        norm_w = sb("norm_w", [128, 2, 2])
        w_o_a = sb("w_o_a", [128, C])
        w_o_b = sb("w_o_b", [BLK, C])
        pick = sb("pick", [128, 2 * NS, BLK], BF16)
        fold = sb("fold", [128, 3 * BLK])
        mean_w = sb("mean_w", [128, 128])
        eps_col = sb("eps_col", [128, 1])
        loads = [(w_u, "w_u"), (w_z, "w_z"), (w_bc_a, "w_bc_a"), (w_bc_b, "w_bc_b"), (w_r_a, "w_r_a"),
                 (w_r_b, "w_r_b"), (w_dt, "w_dt"), (dt_bias, "dt_bias"), (a_neg, "a_logs"), (skip_w, "skip"),
                 (norm_w, "norm"), (w_o_a, "w_o_a"), (w_o_b, "w_o_b")]
        conv_w = sb("conv_w", [128, 2, 9])
        in_bias = sb("in_bias", [128, 2, 2])
        conv_b = sb("conv_b", [128, 2])
        out_bias = sb("out_bias", [C, 1])
        padded = sb("padded", [128, 2, H + 2, W + 2])
        conv_diag = sb("conv_diag", [BLK, 9, 128])
        conved = sb("conved", [128, L])
        z_a = sb("z_a", [128, L])
        z_b = sb("z_b", [BLK, L])
        loads += [(conv_w, "conv_w"), (in_bias, "in_bias"), (conv_b, "conv_b"), (out_bias, "out_bias")]

        u = sb("u", [128, NJ, L])
        ranks = sb("ranks", [RANKS, L])
        bc = sb("bc", [128, dirs, L], BF16)
        sp_e, sp_l, sp_r, sp_w = (sb(n, [128, L]) for n in ("sp_e", "sp_l", "sp_r", "sp_w"))
        rest = sp_r
        delta = sb("delta", [128, NJ, L])
        du = sb("du", [128, NJ, L])
        delta2 = sb("delta2", [128, dirs * NBLK, L])
        du2 = sb("du2", [128, dirs * NBLK, L])
        decay = sb("decay", [128, 2, L])
        inject = sb("inject", [128, 2, L])
        state = sb("state", [128, RING, L])
        read = sb("read", [128, RING, L])
        c_rows = sb("c_rows", [128, 2, L])
        y_a = sb("y_a", [128, L])
        y_b = sb("y_b", [BLK, L])

        y_ps = ctx.enter_context(nc.psum_tensor(f"{name}_y_ps", [128, 3, HALF], F32))
        work0 = ctx.enter_context(nc.psum_tensor(f"{name}_work0", [128, L], F32))
        work1 = ctx.enter_context(nc.psum_tensor(f"{name}_work1", [128, L], F32))
        c_ps = ctx.enter_context(nc.psum_tensor(f"{name}_c_ps", [128, HALF], F32))
        work = [work0, work1]
        y_flat = y_ps[:, 0:2, :].rearrange("p a n -> p (a n)")

        (weights, set_up, consts, conved_s, u_ready, ranks_ready, bc_hi, bc_rest, bc_mid,
         bc_ready, sp_abs, sp_exp, sp_one, sp_log, sp_step, decay_ready, scanned, injected, b_ready, c_ready, c_copied,
         multiplied, y_added, y_free, y_out, y_summed, centred, squared, logged, rooted, scaled, affine, gated,
         silued, x_added) = (
            sem(s) for s in (
                "weights", "set_up", "consts", "conved", "u_ready", "ranks_ready",
                "bc_hi", "bc_rest", "bc_mid", "bc_ready", "sp_abs", "sp_exp", "sp_one", "sp_log", "sp_step", "decay_ready",
                "scanned", "injected", "b_ready", "c_ready", "c_copied", "multiplied", "y_added", "y_free", "y_out",
                "y_summed", "centred", "squared", "logged", "rooted", "scaled", "affine", "gated", "silued",
                "x_added"))
        work_ready = sem("work_ready")
        work_free = [sem("work_free0"), sem("work_free1")]
        delta2_in = [sem(f"delta2_in{d}") for d in range(dirs)]
        du2_in = [sem(f"du2_in{d}") for d in range(dirs)]

        seq = [("u", 0, 0), ("u", 0, 1), ("z", 0, 0), ("z", 0, 1), ("conv", 0, 1), ("ranks", 0, 0), ("bc", 0, 0),
               ("dt", 0, 0), ("dt", 0, 1), ("mean", 0, 0), ("var", 0, 0), ("out", 0, 0)]
        keys = [(k, i % 2) for i, k in enumerate(seq)]
        uses = Uses(keys)

        def wait_work(eng, b, key):
            eng.wait_ge(work_ready, b * uses.total + uses.index[key] + 1)

        def free_work(ins, key):
            ins.then_inc(work_free[uses.buf[key]], 1)

        def turn(b, o):
            return b * orders + o

        block = ctx.enter_context(nc.Block())
        tiles = [(d, p, c) for d in range(dirs) for p in range(NP) for c in range(NBLK)]
        n_setup = 2 + orders * (1 + 2) + 2 * NS + 3 + 1 + 1 + 9

        @block.sync
        def _(sp):
            for t, key in loads:
                sp.dma_start(t[tuple(slice(None) for _ in t.shape)], hbm[key]).then_inc(weights, 16)
            with sp.Fori(0, B) as b:
                for o in range(orders):
                    it = turn(b, o)
                    sp.wait_ge(y_added, it * NT + RING)
                    for q in range(dirs * NBLK):
                        j, half = q // 2, q % 2
                        rows = slice(half * BLK, half * BLK + BLK)
                        sp.wait_ge(sp_step, (it * NJ + j) * 4 + 4)
                        for side in range(2):
                            to = slice(side * BLK, side * BLK + BLK)
                            sp.dma_start(delta2[to, q, :], delta[rows, j, :]).then_inc(delta2_in[q // NBLK], 16)
                            sp.dma_start(du2[to, q, :], du[rows, j, :]).then_inc(du2_in[q // NBLK], 16)

        @block.tensor
        def _(pe):
            pe.wait_ge(weights, 16 * len(loads))
            pe.wait_ge(set_up, n_setup)

            with pe.Fori(0, B) as b:
                def claim(key):
                    k = uses.buf[key]
                    pe.wait_ge(work_free[k], b * uses.count[k] + uses.nth[key] + 1)
                    return work[k]

                def product(key, rows, parts):
                    dst = claim(key)
                    for i, s in halves():
                        for n, (lhs, rhs) in enumerate(parts):
                            m = nc.tensor.matmul(dst[0:rows, s], lhs, rhs(i, s), start=(n == 0),
                                                 stop=(n == len(parts) - 1))
                    m.then_inc(work_ready, 1)

                def g_half(o):
                    img = g_cm[:, bass.ts(b, L)]
                    if o == 0:
                        return lambda i, s: img[:, s]
                    turned = img.rearrange("p (h w) -> p w h", w=W)
                    return lambda i, s: turned[:, i * (W // 2):(i + 1) * (W // 2), :]

                for o in range(orders):
                    it = turn(b, o)
                    for j in range(2):
                        product(("u", o, j), 128, [(w_u[:, j * 128:(j + 1) * 128], g_half(o))])
                    for j in range(2):
                        product(("z", 0, j), 128, [(w_z[:, j * 128:(j + 1) * 128], g_half(0))])
                    pe.wait_ge(work_free[1], b * uses.count[1] + uses.nth[("u", 0, 1)] + 2)
                    product(("conv", 0, 1), 128, [
                        (conv_diag[:, k, :], lambda i, s, k=k: padded[0:BLK, 1, k // 3 + i * H // 2:
                                                                      k // 3 + (i + 1) * H // 2, k % 3:k % 3 + W])
                        for k in range(9)])
                    pe.wait_ge(u_ready, it * NJ + NJ)
                    u_parts = (lambda i, s: u[:, 0, s], lambda i, s: u[0:BLK, 1, s])
                    product(("ranks", o, 0), RANKS, [(w_r_a[:, o, :], u_parts[0]), (w_r_b[:, o, :], u_parts[1])])
                    for d in range(dirs):
                        product(("bc", o, d), 128, [(w_bc_a[:, o * dirs + d, :], u_parts[0]),
                                                    (w_bc_b[:, o * dirs + d, :], u_parts[1])])
                    pe.wait_ge(ranks_ready, it + 1)
                    for j in range(NJ):
                        product(("dt", o, j), rows_of[j], [(w_dt[:, o, j * 128:j * 128 + rows_of[j]],
                                                            lambda i, s: ranks[:, s])])
                    pe.wait_ge(y_free, it + 1)
                    for i, s in halves():
                        nc.tensor.matmul(y_ps[:, i, :], skip_diag[:, o, 0, :], u[:, 0, s], start=True, stop=False)
                    for i, s in halves():
                        nc.tensor.matmul(y_ps[i * BLK:(i + 1) * BLK, 2, :], skip_diag[0:BLK, o, 1, 0:BLK],
                                         u[0:BLK, 1, s], start=True, stop=False, skip_group_check=True)

                    def spread_b(g, d, p):
                        G = it * dirs * NP + g
                        pe.wait_ge(bc_ready, it * dirs + d + 1)
                        pe.wait_ge(injected, (G - 1) * NBLK + INJECT0)
                        for i, s in halves():
                            m = nc.tensor.matmul(work[g % 2][:, s], pick[:, 2 * p:2 * p + 2, :], bc[:, d, s],
                                                 start=True, stop=True)
                        m.then_inc(b_ready, 1)

                    def spread_c(g, d, p):
                        G = it * dirs * NP + g
                        for i, s in halves():
                            pe.wait_ge(c_copied, G * 2 + i + 1)
                            nc.tensor.matmul(c_ps[:, :], pick[:, NS + 2 * p:NS + 2 * p + 2, :], bc[:, d, s],
                                             start=True, stop=True).then_inc(c_ready, 1)

                    def sum_states(t, c):
                        pe.wait_ge(multiplied, it * NT + t + 1 + RING + 1)
                        for i, s in halves():
                            src = read[:, t % RING, s]
                            if c < 2:
                                lhs = fold[:, BLK * (1 - c):BLK * (1 - c) + 128]
                                m = nc.tensor.matmul(y_ps[:, i, :], lhs, src, start=False, stop=(t == NT - 2))
                            else:
                                m = nc.tensor.matmul(y_ps[i * BLK:(i + 1) * BLK, 2, :], fold[:, BLK:2 * BLK], src,
                                                     start=False, stop=(t == NT - 1), skip_group_check=True)
                        m.then_inc(y_added, 1)

                    for k in range(2):
                        last = [key for key in uses.buf if uses.buf[key] == k and key[1] == o and
                                key[0] in ("u", "ranks", "bc", "dt")][-1]
                        pe.wait_ge(work_free[k], b * uses.count[k] + uses.nth[last] + 2)
                    spread_b(0, 0, 0)
                    spread_b(1, 0, 1)
                    spread_c(0, 0, 0)
                    for t, (d, p, c) in enumerate(tiles):
                        g = t // NBLK
                        if c == 0:
                            if g + 2 < dirs * NP:
                                spread_b(g + 2, (g + 2) // NP, (g + 2) % NP)
                            if g + 1 < dirs * NP:
                                spread_c(g + 1, (g + 1) // NP, (g + 1) % NP)
                        sum_states(t, c)

                pe.wait_ge(y_summed, b + 1)
                product(("mean", 0, 0), 128, [(mean_w[:, :], lambda i, s: y_a[:, s]),
                                              (mean_w[0:BLK, :], lambda i, s: y_b[:, s])])
                pe.wait_ge(squared, b * 2 + 2)
                product(("var", 0, 0), 128, [(mean_w[:, :], lambda i, s: sp_e[:, s]),
                                             (mean_w[0:BLK, :], lambda i, s: sp_l[0:BLK, s])])
                pe.wait_ge(gated, b * 2 + 2)
                product(("out", 0, 0), C, [(w_o_a[:, :], lambda i, s: y_a[:, s]),
                                           (w_o_b[:, :], lambda i, s: y_b[:, s])])
                pe.wait_ge(x_added, b + 1)

        @block.scalar
        def _(act):
            act.preload_act_table_set("natural_log_exp_and_others")
            act.wait_ge(weights, 16 * len(loads))
            nc.scalar.activation(a_neg[:, :, :, :], a_neg[:, :, :, :], ACT.Exp).then_inc(consts, 1)
            act.wait_ge(consts, 1)
            nc.scalar.mul(a_neg[:, :, :, :], a_neg[:, :, :, :], -1.0).then_inc(consts, 1)
            act.wait_ge(consts, 2)
            act.wait_ge(set_up, n_setup)
            with act.Fori(0, B) as b:
                for o in range(orders):
                    it = turn(b, o)
                    for j in range(2):
                        r = rows_of[j]
                        wait_work(act, b, ("u", o, j))
                        ins = nc.scalar.activation(padded[0:r, j, 1:H + 1, 1:W + 1],
                                                   work[uses.buf[("u", o, j)]][0:r, :].rearrange(
                                                       "p (h w) -> p h w", w=W),
                                                   ACT.Identity, bias=in_bias[0:r, 0, j:j + 1])
                        free_work(ins, ("u", o, j))
                    for j, (dst, r) in enumerate(((z_a, 128), (z_b, BLK))):
                        key = ("z", 0, j)
                        wait_work(act, b, key)
                        nc.scalar.activation(dst[:, :], work[uses.buf[key]][0:r, :], ACT.Silu,
                                             bias=in_bias[0:r, 1, j:j + 1]).then_inc(silued, 1)
                        act.wait_ge(silued, b * 2 + j + 1)
                        act.sem_inc(work_free[uses.buf[key]], 1)
                    act.wait_ge(conved_s, (b + 1) * 9)
                    nc.scalar.activation(u[:, 0, :], conved[:, :], ACT.Silu, bias=conv_b[:, 0:1]).then_inc(u_ready, 1)
                    key = ("conv", 0, 1)
                    wait_work(act, b, key)
                    nc.scalar.activation(u[0:BLK, 1, :], work[uses.buf[key]][0:BLK, :], ACT.Silu,
                                         bias=conv_b[0:BLK, 1:2]).then_inc(u_ready, 1)
                    act.wait_ge(u_ready, (b + 1) * 2)
                    act.sem_inc(work_free[uses.buf[key]], 1)
                    act.preload_act_table_set("natural_log_exp_and_others")
                    key = ("ranks", o, 0)
                    wait_work(act, b, key)
                    nc.scalar.copy(ranks[:, :], work[uses.buf[key]][0:RANKS, :]).then_inc(ranks_ready, 1)
                    act.wait_ge(ranks_ready, it + 1)
                    act.sem_inc(work_free[uses.buf[key]], 1)
                    for d in range(dirs):
                        key = ("bc", o, d)
                        wait_work(act, b, key)
                        nc.scalar.copy(bc[:, d, :], work[uses.buf[key]][:, :]).then_inc(bc_hi, 1)
                        act.wait_ge(bc_rest, it * dirs + d + 1)
                        nc.scalar.copy(bc[BLK:128, d, :], rest[BLK:128, :]).then_inc(bc_mid, 1)
                    for j in range(NJ):
                        key, r = ("dt", o, j), rows_of[j]
                        src, bias = work[uses.buf[key]][0:r, :], dt_bias[0:r, o, j:j + 1]
                        n = it * NJ + j
                        wait_work(act, b, key)
                        if j == 0:
                            act.wait_ge(bc_ready, (it + 1) * dirs)
                        else:
                            act.wait_ge(sp_step, n * 4)
                        nc.scalar.activation(sp_e[0:r, :], src, ACT.Abs, bias=bias).then_inc(sp_abs, 1)
                        free_work(nc.scalar.activation(sp_r[0:r, :], src, ACT.Relu, bias=bias), key)
                        act.wait_ge(sp_abs, n + 1)
                        nc.scalar.activation(sp_e[0:r, :], sp_e[0:r, :], ACT.Exp, scale=-1.0).then_inc(sp_exp, 1)
                        act.wait_ge(sp_exp, n + 1)
                        nc.scalar.activation(sp_w[0:r, :], sp_e[0:r, :], ACT.Identity, bias=1.0).then_inc(sp_one, 1)
                        act.wait_ge(sp_one, n + 1)
                        nc.scalar.activation(sp_l[0:r, :], sp_w[0:r, :], ACT.Ln).then_inc(sp_log, 1)

                    def copy_c(g):
                        G = it * dirs * NP + g
                        act.wait_ge(multiplied, G * NBLK + 1)
                        for i, s in halves():
                            act.wait_ge(c_ready, G * 2 + i + 1)
                            nc.scalar.copy(c_rows[:, g % 2, s], c_ps[:, :]).then_inc(c_copied, 1)

                    for t, (d, p, c) in enumerate(tiles):
                        if p == 0 and c == 0:
                            act.wait_ge(delta2_in[d], (it + 1) * 16 * 2 * NBLK)
                        act.wait_ge(scanned, it * NT + t + RING - 1)
                        nc.scalar.activation(decay[:, t % 2, :], delta2[:, d * NBLK + c, :], ACT.Exp,
                                             scale=a_neg[:, o * dirs + d, c, p:p + 1]).then_inc(decay_ready, 1)
                        if c == 0:
                            copy_c(t // NBLK)
                    act.wait_ge(y_added, (it + 1) * NT + RING)
                    to_a, to_b = (y_a, y_b) if o == 0 else (sp_e, sp_l)
                    nc.scalar.copy(to_a[:, :], y_flat).then_inc(y_out, 1)
                    for i, s in halves():
                        ins = nc.scalar.copy(to_b[0:BLK, s], y_ps[i * BLK:(i + 1) * BLK, 2, :]).then_inc(y_out, 1)
                    act.wait_ge(y_out, 3 * (it + 1))
                    act.sem_inc(y_free, 1)

                act.wait_ge(centred, b * 2 + 2)
                nc.scalar.activation(sp_e[:, :], y_a[:, :], ACT.Square).then_inc(squared, 1)
                nc.scalar.activation(sp_l[0:BLK, :], y_b[:, :], ACT.Square).then_inc(squared, 1)
                key = ("var", 0, 0)
                wait_work(act, b, key)
                ins = nc.scalar.activation(sp_r[:, :], work[uses.buf[key]][:, :], ACT.Ln, bias=eps_col[:, :])
                ins.then_inc(logged, 1)
                act.wait_ge(logged, b + 1)
                act.sem_inc(work_free[uses.buf[key]], 1)
                nc.scalar.activation(sp_r[:, :], sp_r[:, :], ACT.Exp, scale=-0.5).then_inc(rooted, 1)
                act.wait_ge(scaled, b * 2 + 2)
                nc.scalar.activation(y_a[:, :], y_a[:, :], ACT.Identity, bias=norm_w[:, 1, 0:1],
                                     scale=norm_w[:, 0, 0:1]).then_inc(affine, 1)
                nc.scalar.activation(y_b[:, :], y_b[:, :], ACT.Identity, bias=norm_w[0:BLK, 1, 1:2],
                                     scale=norm_w[0:BLK, 0, 1:2]).then_inc(affine, 1)

        @block.gpsimd
        def _(pool):
            with pool.Fori(0, B) as b:
                for o in range(orders):
                    it = turn(b, o)
                    for t in range(NT):
                        g = t // NBLK
                        pool.wait_ge(scanned, it * NT + t + 1 + RING)
                        if t % NBLK == 0:
                            pool.wait_ge(c_copied, (it * dirs * NP + g) * 2 + 2 + 1)
                        pool.wait_ge(y_added, it * NT + t + 1)
                        nc.gpsimd.tensor_tensor(read[:, t % RING, :], state[:, t % RING, :], c_rows[:, g % 2, :],
                                                ALU.mult).then_inc(multiplied, 1)

        @block.vector
        def _(dve):
            for s, n in ((scanned, RING), (multiplied, RING + 1), (y_added, RING), (injected, INJECT0), (c_copied, 1),
                         (y_free, 1), (work_free[0], 1), (work_free[1], 1)):
                for _ in range(n):
                    dve.sem_inc(s, 1)
            n = [0]

            def setup(ins):
                n[0] += 1
                ins.then_inc(set_up, 1)

            dve.wait_ge(weights, 16 * len(loads))
            setup(nc.vector.memset(mean_w[:, :], 1.0 / DI))
            setup(nc.vector.memset(eps_col[:, :], eps))
            for m in range(2 * NS):
                src = (m // NS) * NS + (m % NS) // 2 + NP * (m % 2)
                setup(nc.vector.tensor_copy(pick[:, m, :], cols_e[:, src:src + 1].to_broadcast([128, BLK])))
            for side, v in ((0, 0.0), (2, 0.0)):
                setup(nc.vector.memset(fold[:, side * BLK:(side + 1) * BLK], v))
            setup(nc.vector.tensor_tensor(fold[:, BLK:2 * BLK], ident[:, 0:BLK], ident[:, BLK:128], ALU.add))
            setup(nc.vector.memset(padded[:, :, :, :], 0.0))
            for k in range(9):
                setup(nc.vector.tensor_scalar(conv_diag[:, k, :], ident[0:BLK, :], conv_w[0:BLK, 1, k:k + 1],
                                              None, ALU.mult))
            for o in range(orders):
                setup(nc.vector.tensor_copy(skip_sum[:, o, :], skip_w[:, o, 0, :]))
            dve.wait_ge(set_up, n[0])
            for o in range(orders):
                for j in range(2):
                    setup(nc.vector.tensor_scalar(skip_diag[:, o, j, :], ident, skip_sum[:, o, j:j + 1], None,
                                                  ALU.mult))
            setup(nc.vector.memset(rest[:, :], 0.0))
            assert n[0] == n_setup
            dve.wait_ge(set_up, n_setup)

            with dve.Fori(0, B) as b:
                for o in range(orders):
                    it = turn(b, o)
                    key = ("u", 0, 0)
                    acc = conved[:, :].rearrange("p (h w) -> p h w", w=W)
                    dve.wait_ge(work_free[uses.buf[key]], b * uses.count[uses.buf[key]] + uses.nth[key] + 2)
                    for k in range(9):
                        tap = padded[:, 0, k // 3:k // 3 + H, k % 3:k % 3 + W]
                        wk = conv_w[:, 0, k:k + 1]
                        if k == 0:
                            ins = nc.vector.tensor_scalar(acc, tap, wk, None, ALU.mult)
                        else:
                            dve.wait_ge(conved_s, b * 9 + k)
                            ins = nc.vector.scalar_tensor_tensor(out=acc, in0=tap, scalar=wk, in1=acc,
                                                                 op0=ALU.mult, op1=ALU.add)
                        ins.then_inc(conved_s, 1)
                    for d in range(dirs):
                        key = ("bc", o, d)
                        dve.wait_ge(bc_hi, it * dirs + d + 1)
                        if d > 0:
                            dve.wait_ge(bc_ready, it * dirs + d)
                        nc.vector.tensor_tensor(rest[BLK:128, :], work[uses.buf[key]][BLK:128, :], bc[BLK:128, d, :],
                                                ALU.subtract).then_inc(bc_rest, 1)
                        dve.wait_ge(bc_rest, it * dirs + d + 1)
                        dve.sem_inc(work_free[uses.buf[key]], 1)
                        dve.wait_ge(bc_mid, it * dirs + d + 1)
                        nc.vector.tensor_tensor(bc[96:128, d, :], rest[96:128, :], bc[96:128, d, :],
                                                ALU.subtract).then_inc(bc_ready, 1)
                    for j in range(NJ):
                        r, n4 = rows_of[j], (it * NJ + j) * 4
                        e, l, w, dl = sp_e[0:r, :], sp_l[0:r, :], sp_w[0:r, :], delta[0:r, j, :]
                        dve.wait_ge(sp_log, it * NJ + j + 1)
                        nc.vector.scalar_tensor_tensor(out=w, in0=w, scalar=1.0, in1=l, op0=ALU.subtract,
                                                       op1=ALU.subtract).then_inc(sp_step, 1)
                        dve.wait_ge(sp_step, n4 + 1)
                        nc.vector.scalar_tensor_tensor(out=w, in0=w, scalar=0.0, in1=e, op0=ALU.max,
                                                       op1=ALU.subtract).then_inc(sp_step, 1)
                        dve.wait_ge(sp_step, n4 + 2)
                        nc.vector.tensor_tensor(dl, sp_r[0:r, :], w, ALU.subtract).then_inc(sp_step, 1)
                        dve.wait_ge(sp_step, n4 + 3)
                        nc.vector.tensor_tensor(du[0:r, j, :], dl, u[0:r, j, :], ALU.mult).then_inc(sp_step, 1)

                    def inject_tile(t):
                        T, (d, p, c) = it * NT + t, tiles[t]
                        if p == 0 and c == 0:
                            dve.wait_ge(du2_in[d], (it + 1) * 16 * 2 * NBLK)
                        if c == 0:
                            dve.wait_ge(b_ready, it * dirs * NP + t // NBLK + 1)
                        dve.wait_ge(scanned, T - 1 + RING)
                        nc.vector.tensor_tensor(inject[:, t % 2, :], du2[:, d * NBLK + c, :], work[p % 2][:, :],
                                                ALU.mult).then_inc(injected, 1)

                    inject_tile(0)
                    for t, (d, p, c) in enumerate(tiles):
                        T = it * NT + t
                        if t + 1 < NT:
                            inject_tile(t + 1)
                        dve.wait_ge(injected, T + 1 + INJECT0)
                        dve.wait_ge(decay_ready, T + 1)
                        dve.wait_ge(multiplied, T + 2)
                        way = slice(None, None, 1 if d == 0 else -1)
                        nc.vector.tensor_tensor_scan(state[:, t % RING, way], decay[:, t % 2, way],
                                                     inject[:, t % 2, way], 0.0, ALU.mult, ALU.add).then_inc(scanned, 1)

                dve.wait_ge(y_out, 3 * orders * (b + 1))
                dve.sem_inc(y_summed, 1)
                key = ("mean", 0, 0)
                wait_work(dve, b, key)
                nc.vector.tensor_tensor(y_a[:, :], y_a[:, :], work[uses.buf[key]][:, :], ALU.subtract).then_inc(centred, 1)
                nc.vector.tensor_tensor(y_b[:, :], y_b[:, :], work[uses.buf[key]][0:BLK, :],
                                        ALU.subtract).then_inc(centred, 1)
                dve.wait_ge(centred, 2 * (b + 1))
                dve.sem_inc(work_free[uses.buf[key]], 1)
                dve.wait_ge(rooted, b + 1)
                dve.wait_ge(squared, 2 * (b + 1))
                nc.vector.tensor_tensor(y_a[:, :], y_a[:, :], sp_r[:, :], ALU.mult).then_inc(scaled, 1)
                nc.vector.tensor_tensor(y_b[:, :], y_b[:, :], sp_r[0:BLK, :], ALU.mult).then_inc(scaled, 1)
                dve.wait_ge(affine, 2 * (b + 1))
                dve.wait_ge(silued, 2 * (b + 1))
                nc.vector.tensor_tensor(y_a[:, :], y_a[:, :], z_a[:, :], ALU.mult).then_inc(gated, 1)
                nc.vector.tensor_tensor(y_b[:, :], y_b[:, :], z_b[:, :], ALU.mult).then_inc(gated, 1)
                key = ("out", 0, 0)
                wait_work(dve, b, key)
                xs = x_cm[:, bass.ts(b, L)]
                nc.vector.scalar_tensor_tensor(out=xs, in0=work[uses.buf[key]][0:C, :], scalar=out_bias[:, 0:1],
                                               in1=xs, op0=ALU.add, op1=ALU.add).then_inc(x_added, 1)
                dve.wait_ge(x_added, b + 1)
                dve.sem_inc(work_free[uses.buf[key]], 1)


TURN_TILES = 2 * NP * NBLK
GROUPS = 2 * NP
DECAYS, STATES, READS = 2, 2, 3
LAG = 3
FINISH = {("z", 0): (1, 2), ("mean", 0): (4, 5), ("z", 1): (7, 8), ("var", 0): (10, 11), ("out", 0): (28, 29)}
PREPARE = [{("u", 0): (13, 14), ("u", 1): (16, 17), ("u", 2): (19, 20), ("bc", 0): (22, 23), ("bc", 1): (25, 26),
            ("dt", 0): (31, 32), ("dt", 1): (34, 35), ("dt", 2): (37, 38)},
           {("u", 0): (4, 5), ("u", 1): (7, 8), ("bc", 0): (10, 11), ("bc", 1): (16, 17), ("dt", 0): (19, 20),
            ("u", 2): (22, 23), ("dt", 1): (28, 29), ("dt", 2): (37, 38)}]
ACT_FINISH = {("square", 0): 10, ("square", 1): 11, ("silu", 0): 12, ("rstd", 0): 15, ("affine", 0): 18,
              ("affine", 1): 19}
ACT_PREPARE = [{("hi", 0): 27, ("mid", 0): 28, ("hi", 1): 30, ("mid", 1): 33, ("exp", 0): 36, ("one", 0): 36,
                ("log", 0): 37, ("exp", 1): 38, ("one", 1): 39, ("log", 1): 40, ("exp", 2): 42,
                ("one", 2): 43, ("log", 2): 44},
               {("hi", 0): 16, ("mid", 0): 20, ("hi", 1): 21, ("mid", 1): 25, ("exp", 0): 26, ("one", 0): 28,
                ("log", 0): 29, ("exp", 1): 33, ("one", 1): 34, ("log", 1): 35, ("exp", 2): 42,
                ("one", 2): 43, ("log", 2): 44}]
DVE_FINISH = {("join", 0): 3, ("join", 1): 4, ("centre", 0): 8, ("centre", 1): 9, ("scale", 0): 16, ("scale", 1): 17,
              ("gate", 0): 20, ("gate", 1): 20, ("residual", 0): 34}
DVE_PREPARE = [{("rest", 0): 27, ("lo", 0): 29, ("rest", 1): 30, ("lo", 1): 33, ("fix", 0): 38, ("part", 0): 38,
                ("du", 0): 41, ("fix", 1): 41, ("part", 1): 41, ("du", 1): 43, ("fix", 2): 45,
                ("part", 2): 45, ("du", 2): 47},
               {("rest", 0): 16, ("lo", 0): 22, ("rest", 1): 22, ("lo", 1): 25, ("fix", 0): 30, ("part", 0): 30,
                ("fix", 1): 36, ("part", 1): 36, ("du", 0): 39, ("du", 1): 42, ("fix", 2): 45,
                ("part", 2): 45, ("du", 2): 47}]
POOL_PREPARE = [{("delta", 0): 38, ("delta", 1): 41, ("delta", 2): 45},
                {("delta", 0): 36, ("delta", 1): 39, ("delta", 2): 45}]
FINISH_STEPS = {"square", "silu", "rstd", "affine", "join", "centre", "scale", "gate", "residual"}


def steps_at(t, turn, prepare, finish={}):
    table = {**(finish if turn.finish else {}), **prepare[turn.r]}
    return [key for key, at in table.items() if at == t]


def side_uses(r, finish):
    table = {**(FINISH if finish else {}), **PREPARE[r]}
    return sorted((t, key, i) for key, ts in table.items() for i, t in enumerate(ts))


class BankUses:

    def __init__(self):
        self.head = {(key, i): n for n, (_, key, i) in enumerate(side_uses(0, False))}
        self.n_head = len(self.head) + 2
        self.body = {}
        for first in (True, False):
            n, table = 0, {}
            for r in range(2):
                sides = side_uses(r, r == 0 and not first)
                for t in range(TURN_TILES):
                    if t % NBLK == 0:
                        for i in range(2):
                            table[r, "C", t // NBLK + 1, i] = n
                            n += 1
                    for at, key, i in sides:
                        if at == t:
                            table[r, key, i] = n
                            n += 1
            self.body[first] = (table, n)

    def base(self, b, first):
        if first:
            return self.n_head
        return b * self.body[False][1] + (self.n_head + self.body[True][1] - self.body[False][1])


def cross_scan_layer(nc, name, x_cm, g_cm, ident, cols_e, hbm, rank, eps):
    DIRS, NT, RANKS = 2, TURN_TILES, 32 + rank
    NJ = DIRS * NBLK // 2
    bank = BankUses()
    with cleared(nc) as (ctx, sems):
        def sb(n, shape, dt=F32):
            return ctx.enter_context(nc.sbuf_tensor(f"{name}_{n}", shape, dt))

        def sem(n):
            sems.append(nc.alloc_semaphore(name=f"{name}_{n}"))
            return sems[-1]

        w_u = sb("w_u", [C, 2 * DI])
        w_z = sb("w_z", [C, 256])
        w_bc_a = sb("w_bc_a", [128, 4, 128])
        w_bc_b = sb("w_bc_b", [BLK, 4, 128])
        w_dt = sb("w_dt", [BLK + RANKS, 2, 128 * NJ])[BLK:BLK + RANKS, :, :]
        dt_bias = sb("dt_bias", [128, 2, NJ])
        a_neg = sb("a_neg", [128, 4, NBLK, NP])
        skip_w = sb("skip_w", [128, 2, DIRS, 2])
        skip_sum = sb("skip_sum", [128, 2, 2])
        skip_diag = sb("skip_diag", [128, 2, 2, 128])
        norm_w = sb("norm_w", [128, 2, 2])
        w_o_a = sb("w_o_a", [128, C])
        w_o_b = sb("w_o_b", [BLK, C])
        pick = sb("pick", [128, 2 * NS, BLK], BF16)
        fold = sb("fold", [128, 3 * BLK])
        mean_w = sb("mean_w", [128, 128])
        eps_col = sb("eps_col", [128, 1])
        loads = [(w_u, "w_u"), (w_z, "w_z"), (w_bc_a, "w_bc_a"), (w_bc_b, "w_bc_b"), (w_dt, "w_dt"),
                 (dt_bias, "dt_bias"), (a_neg, "a_logs"), (skip_w, "skip"), (norm_w, "norm"), (w_o_a, "w_o_a"), (w_o_b, "w_o_b")]

        u = sb("u", [128, NJ, L])
        bc = sb("bc", [128, 2, DIRS, L], BF16)
        t_e, t_l, t_r, t_w = (sb(n, [128, L]) for n in ("t_e", "t_l", "t_r", "t_w"))
        delta = sb("delta", [128, NJ, L])
        du_01 = sb("du_01", [128, NJ - 1, L])
        du = [du_01[:, 0, :], du_01[:, 1, :], u[:, NJ - 1, :]]
        delta2 = sb("delta2", [128, DIRS * NBLK, L])
        du2 = sb("du2", [128, DIRS * NBLK, L])
        decay = sb("decay", [128, DECAYS, L])
        state = sb("state", [128, STATES, L])
        inject = sb("inject", [128, 2, L])
        read = sb("read", [128, READS, L])
        c_rows = sb("c_rows", [128, 2, L])
        y_a = sb("y_a", [128, L])
        y_b_ranks = sb("y_b_ranks", [BLK + RANKS, L])
        y_b, ranks = y_b_ranks[0:BLK, :], y_b_ranks[BLK:BLK + RANKS, :]
        e_of = [t_e, t_r, t_e]
        raw_of = [t_w, t_l]

        y_ps = ctx.enter_context(nc.psum_tensor(f"{name}_y_ps", [128, 3, HALF], F32))
        b_ps = [ctx.enter_context(nc.psum_tensor(f"{name}_b_ps{k}", [128, L], F32)) for k in range(2)]
        side_ps = ctx.enter_context(nc.psum_tensor(f"{name}_side_ps", [128, HALF], F32))
        y_flat = y_ps[:, 0:2, :].rearrange("p a n -> p (a n)")

        (weights, set_up, consts, ranked, side_ready, side_free, bc_hi, bc_rest, bc_mid, bc_ready, sp_abs, sp_exp, sp_one,
         sp_log, sp_part, sp_delta, sp_du, decay_ready, scanned, injected, b_ready, multiplied, y_added, y_free, y_out,
         joined, centred, squared, logged, rooted, scaled, affine, silued, gated, x_added) = (
            sem(s) for s in (
                "weights", "set_up", "consts", "ranked", "side_ready", "side_free", "bc_hi", "bc_rest", "bc_mid", "bc_ready",
                "sp_abs", "sp_exp", "sp_one", "sp_log", "sp_part", "sp_delta", "sp_du", "decay_ready", "scanned", "injected",
                "b_ready", "multiplied", "y_added", "y_free", "y_out", "joined", "centred", "squared", "logged",
                "rooted", "scaled", "affine", "silued", "gated", "x_added"))
        delta2_in = [sem(f"delta2_in{d}") for d in range(DIRS)]
        du2_in = [sem(f"du2_in{d}") for d in range(DIRS)]
        PER_DIR = 16 * 2 * NBLK
        MULT0, SCAN0, SUM0, INJECT0 = STATES + 2, DECAYS, READS, NBLK + 1

        class Turn:

            def __init__(self, b, r, first):
                self.b, self.r, self.first = b, r, first
                self.number = b * 2 + r
                self.finish = r == 0 and not first
                self.table, self.base = bank.body[first][0], bank.base(b, first)
                self.next = self.number + 1
                self.next_image = b if r == 0 else ((b + 1) % B)
                self.next_order = 1 - r
                self.done_image = b - 1 if self.finish else None

            def use(self, *key):
                return self.table[(self.r, *key)] + self.base

        class Head:
            next, next_image, next_order, done_image, finish = 0, 0, 0, None, False

            def use(self, key, i):
                return bank.head[key, i]

        class Tail:
            done_image, finish = B - 1, True
            base = bank.base(B, False)

            def use(self, key, i):
                order = [(k, h) for _, k, h in side_uses(0, True) if k in FINISH]
                return self.base + order.index((key, i))

        def over_turns(eng, turn):
            for r in range(2):
                turn(Turn(0, r, True))
            with eng.Fori(1, B) as b:
                for r in range(2):
                    turn(Turn(b, r, False))

        def wait_side(eng, n):
            eng.wait_ge(side_free, n + 2)

        block = ctx.enter_context(nc.Block())
        tiles = [(d, p, c) for d in range(DIRS) for p in range(NP) for c in range(NBLK)]
        n_setup = 3 + 2 * (1 + 2) + 2 * NS + 3

        @block.sync
        def _(sp):
            for t, key in loads:
                sp.dma_start(t[tuple(slice(None) for _ in t.shape)], hbm[key]).then_inc(weights, 16)

            def copy_blocks(n, q):
                j, half = q // 2, q % 2
                rows = slice(half * BLK, half * BLK + BLK)
                sp.wait_ge(sp_delta, n * NJ + j + 1)
                sp.wait_ge(sp_du, n * NJ + j + 1)
                for side in range(2):
                    to = slice(side * BLK, side * BLK + BLK)
                    sp.dma_start(delta2[to, q, :], delta[rows, j, :]).then_inc(delta2_in[q // NBLK], 16)
                    sp.dma_start(du2[to, q, :], du[j][rows, :]).then_inc(du2_in[q // NBLK], 16)

            def copies(n, running):
                if running:
                    sp.wait_ge(y_added, n * NT - NT // 2 + SUM0)
                for q in range(NBLK):
                    copy_blocks(n, q)
                sp.wait_ge(y_added, n * NT + SUM0)
                for q in range(NBLK, 2 * NBLK):
                    copy_blocks(n, q)

            copies(0, False)
            over_turns(sp, lambda turn: copies(turn.next, True))
            for d in range(DIRS):
                sp.wait_ge(delta2_in[d], (2 * B + 1) * PER_DIR)
                sp.wait_ge(du2_in[d], (2 * B + 1) * PER_DIR)

        @block.tensor
        def _(pe):
            pe.wait_ge(weights, 16 * len(loads))
            pe.wait_ge(set_up, n_setup)

            def g_half(image, order, i):
                img = g_cm[:, bass.ts(image, L)]
                if order == 0:
                    return img[:, i * HALF:(i + 1) * HALF]
                return img.rearrange("p (h w) -> p w h", w=W)[:, i * (W // 2):(i + 1) * (W // 2), :]

            def side(turn, key, i):
                kind, j = key
                n, s = turn.use(key, i), slice(i * HALF, (i + 1) * HALF)
                if kind == "u":
                    o = turn.next_order
                    rows, parts = 128, [(w_u[:, j * 128:(j + 1) * 128], g_half(turn.next_image, o, i))]
                elif kind == "bc":
                    k = turn.next_order * 2 + j
                    wait_side(pe, turn.use(("u", 1), 1))
                    rows, parts = 128, [(w_bc_a[:, k, :], u[:, 0, s]), (w_bc_b[:, k, :], u[0:BLK, 1, s])]
                elif kind == "dt":
                    pe.wait_ge(ranked, turn.next * 4 + 4)
                    rows, parts = 128, [(w_dt[:, turn.next_order, j * 128:(j + 1) * 128], ranks[:, s])]
                elif kind == "z":
                    rows, parts = 128, [(w_z[:, j * 128:(j + 1) * 128], g_half(turn.done_image, 0, i))]
                elif kind == "mean":
                    pe.wait_ge(joined, 2 * turn.done_image + 2)
                    rows, parts = 128, [(mean_w[:, :], y_a[:, s]), (mean_w[0:BLK, :], y_b[:, s])]
                elif kind == "var":
                    pe.wait_ge(squared, 2 * turn.done_image + 2)
                    rows, parts = 128, [(mean_w[:, :], t_e[:, s]), (mean_w[0:BLK, :], t_r[0:BLK, s])]
                else:
                    pe.wait_ge(gated, 2 * turn.done_image + 2)
                    rows, parts = C, [(w_o_a[:, :], y_a[:, s]), (w_o_b[:, :], y_b[:, s])]
                pe.wait_ge(side_free, n + 1)
                for k, (lhs, rhs) in enumerate(parts):
                    m = nc.tensor.matmul(side_ps[0:rows, :], lhs, rhs, start=(k == 0), stop=(k == len(parts) - 1))
                m.then_inc(side_ready, 1)

            def spread_b(number, order, g):
                d, p = g // NP, g % NP
                pe.wait_ge(bc_ready, number * 2 + d + 1)
                pe.wait_ge(injected, (number * GROUPS + g - 1) * NBLK + INJECT0)
                for i, s in halves():
                    m = nc.tensor.matmul(b_ps[g % 2][:, s], pick[:, 2 * p:2 * p + 2, :], bc[:, order, d, s],
                                         start=True, stop=True)
                m.then_inc(b_ready, 1)

            def spread_c(number, order, g, use):
                d, p = g // NP, g % NP
                pe.wait_ge(bc_ready, number * 2 + d + 1)
                for i, s in halves():
                    pe.wait_ge(side_free, use + i + 1)
                    nc.tensor.matmul(side_ps[:, :], pick[:, NS + 2 * p:NS + 2 * p + 2, :], bc[:, order, d, s],
                                     start=True, stop=True).then_inc(side_ready, 1)

            def turn_of(turn):
                o, number = turn.r, turn.number
                sides = side_uses(turn.r, turn.finish)
                for t, (d, p, c) in enumerate(tiles):
                    if c == 0:
                        def ahead(n):
                            g = t // NBLK + n
                            return (number, o, g) if g < GROUPS else (turn.next, turn.next_order, g - GROUPS)

                        spread_b(*ahead(2))
                        spread_c(*ahead(1), turn.use("C", t // NBLK + 1, 0))
                    for at, key, i in sides:
                        if at == t:
                            side(turn, key, i)
                    if t == 0:
                        pe.wait_ge(y_free, number + 1)
                    pe.wait_ge(multiplied, number * NT + t + 1 + MULT0)
                    for i, s in halves():
                        src = read[:, t % READS, s]
                        if c < 2:
                            lhs = fold[:, BLK * (1 - c):BLK * (1 - c) + 128]
                            m = nc.tensor.matmul(y_ps[:, i, :], lhs, src, start=(t == 0), stop=(t == NT - 2))
                        else:
                            m = nc.tensor.matmul(y_ps[i * BLK:(i + 1) * BLK, 2, :], fold[:, BLK:2 * BLK], src,
                                                 start=(t == 2), stop=(t == NT - 1), skip_group_check=True)
                    m.then_inc(y_added, 1)
                    if t == 3:
                        for i, s in halves():
                            nc.tensor.matmul(y_ps[:, i, :], skip_diag[:, o, 0, :], u[:, 0, s], start=False, stop=False)
                    if t == 6:
                        for i, s in halves():
                            nc.tensor.matmul(y_ps[i * BLK:(i + 1) * BLK, 2, :], skip_diag[0:BLK, o, 1, 0:BLK],
                                             u[0:BLK, 1, s], start=False, stop=False, skip_group_check=True)

            for _, key, i in side_uses(0, False):
                side(Head(), key, i)
            spread_b(0, 0, 0)
            spread_b(0, 0, 1)
            spread_c(0, 0, 0, bank.n_head - 2)
            over_turns(pe, turn_of)
            for _, key, i in side_uses(0, True):
                if key in FINISH:
                    side(Tail(), key, i)

        @block.scalar
        def _(act):
            act.preload_act_table_set("natural_log_exp_and_others")
            act.wait_ge(weights, 16 * len(loads))
            nc.scalar.activation(a_neg[:, :, :, :], a_neg[:, :, :, :], ACT.Exp).then_inc(consts, 1)
            act.wait_ge(consts, 1)
            nc.scalar.mul(a_neg[:, :, :, :], a_neg[:, :, :, :], -1.0).then_inc(consts, 1)
            act.wait_ge(consts, 2)
            act.wait_ge(set_up, n_setup)

            def take(turn, key, i):
                kind, j = key
                n, s = turn.use(key, i), slice(i * HALF, (i + 1) * HALF)
                act.wait_ge(side_ready, n + 1)
                if kind == "u":
                    if j == 2 and not isinstance(turn, Head):
                        act.wait_ge(du2_in[1], turn.next * PER_DIR)
                    ins = nc.scalar.copy(u[:, j, s], side_ps[:, :])
                elif kind == "bc":
                    if turn.finish:
                        act.wait_ge(gated, 2 * turn.done_image + 2)
                    nc.scalar.copy(ranks[32 * j:32 * j + rank, s], side_ps[32:32 + rank, :]).then_inc(ranked, 1)
                    ins = nc.scalar.copy(raw_of[j][:, s], side_ps[:, :])
                elif kind == "dt":
                    bias = dt_bias[:, turn.next_order, j:j + 1]
                    if not isinstance(turn, Head):
                        for d in range(DIRS):
                            act.wait_ge(delta2_in[d], turn.next * PER_DIR)
                        act.wait_ge(sp_delta, turn.next * NJ)
                        act.wait_ge(sp_du, turn.next * NJ)
                    if j == 1 and turn.finish:
                        act.wait_ge(x_added, turn.done_image + 1)
                    if j == 2:
                        act.wait_ge(sp_delta, turn.next * NJ + 1)
                    nc.scalar.activation(e_of[j][:, s], side_ps[:, :], ACT.Abs, bias=bias).then_inc(sp_abs, 1)
                    ins = nc.scalar.activation(delta[:, j, s], side_ps[:, :], ACT.Relu, bias=bias)
                elif kind == "z":
                    if j == 1:
                        act.wait_ge(joined, 2 * turn.done_image + 2)
                    ins = nc.scalar.copy((t_w[:, s], t_l[:, s])[j], side_ps[:, :])
                elif kind == "mean":
                    ins = nc.scalar.copy(t_r[:, s], side_ps[:, :])
                elif kind == "var":
                    ins = nc.scalar.activation(t_e[:, s], side_ps[:, :], ACT.Ln, bias=eps_col[:, :])
                else:
                    if not isinstance(turn, Tail):
                        act.wait_ge(sp_delta, turn.next * NJ)
                    ins = nc.scalar.copy(t_r[0:C, s], side_ps[0:C, :])
                ins.then_inc(side_free, 1)

            def step(turn, kind, j):
                if kind in FINISH_STEPS:
                    done = turn.done_image
                if kind == "square":
                    act.wait_ge(centred, 2 * done + 2)
                    if j == 0:
                        nc.scalar.activation(t_e[:, :], y_a[:, :], ACT.Square).then_inc(squared, 1)
                    else:
                        nc.scalar.activation(t_r[0:BLK, :], y_b[:, :], ACT.Square).then_inc(squared, 1)
                elif kind == "silu":
                    wait_side(act, turn.use(("z", 1), 1))
                    nc.scalar.activation(t_w[:, :], t_w[:, :], ACT.Silu).then_inc(silued, 1)
                    nc.scalar.activation(t_l[0:BLK, :], t_l[0:BLK, :], ACT.Silu).then_inc(silued, 1)
                    act.preload_act_table_set("natural_log_exp_and_others")
                elif kind == "rstd":
                    wait_side(act, turn.use(("var", 0), 1))
                    nc.scalar.activation(t_e[:, :], t_e[:, :], ACT.Exp, scale=-0.5).then_inc(rooted, 1)
                elif kind == "affine":
                    act.wait_ge(scaled, 2 * done + 2)
                    y, r = ((y_a, 128), (y_b, BLK))[j]
                    nc.scalar.activation(y[:, :], y[:, :], ACT.Identity, bias=norm_w[0:r, 1, j:j + 1],
                                         scale=norm_w[0:r, 0, j:j + 1]).then_inc(affine, 1)
                elif kind == "hi":
                    wait_side(act, turn.use(("bc", j), 1))
                    nc.scalar.copy(bc[:, turn.next_order, j, :], raw_of[j][:, :]).then_inc(bc_hi, 1)
                elif kind == "mid":
                    act.wait_ge(bc_rest, turn.next * 2 + j + 1)
                    nc.scalar.copy(bc[BLK:128, turn.next_order, j, :], raw_of[j][BLK:128, :]).then_inc(bc_mid, 1)
                elif kind == "exp":
                    act.wait_ge(sp_abs, (turn.next * NJ + j) * 2 + 2)
                    nc.scalar.activation(e_of[j][:, :], e_of[j][:, :], ACT.Exp, scale=-1.0).then_inc(sp_exp, 1)
                elif kind == "one":
                    n = turn.next * NJ + j
                    act.wait_ge(sp_exp, n + 1)
                    act.wait_ge(bc_ready, turn.next * 2 + 2)
                    if j > 0:
                        act.wait_ge(sp_part, n * 2)
                    nc.scalar.activation(t_w[:, :], e_of[j][:, :], ACT.Identity, bias=1.0).then_inc(sp_one, 1)
                else:
                    act.wait_ge(sp_one, turn.next * NJ + j + 1)
                    nc.scalar.activation(t_l[:, :], t_w[:, :], ACT.Ln).then_inc(sp_log, 1)

            def take_y(number, order):
                act.wait_ge(y_added, (number + 1) * NT + SUM0)
                to_a, to_b = (y_a, y_b) if order == 0 else (t_e, t_l)
                if order == 1:
                    act.wait_ge(sp_delta, (number + 2) * NJ)
                    act.wait_ge(sp_part, (number + 2) * 2 * NJ)
                nc.scalar.copy(to_a[:, :], y_flat).then_inc(y_out, 1)
                for i, s in halves():
                    nc.scalar.copy(to_b[0:BLK, s], y_ps[i * BLK:(i + 1) * BLK, 2, :]).then_inc(y_out, 1)
                act.wait_ge(y_out, 3 * (number + 1))
                act.sem_inc(y_free, 1)

            def copy_c(G, slot, use):
                act.wait_ge(multiplied, (G - 1) * NBLK + MULT0)
                for i, s in halves():
                    act.wait_ge(side_ready, use + i + 1)
                    nc.scalar.copy(c_rows[:, slot, s], side_ps[:, :]).then_inc(side_free, 1)

            def turn_of(turn):
                o, number = turn.r, turn.number
                sides = side_uses(turn.r, turn.finish)
                for t, (d, p, c) in enumerate(tiles):
                    if p == 0 and c == 0:
                        act.wait_ge(delta2_in[d], (number + 1) * PER_DIR)
                    act.wait_ge(scanned, number * NT + t - DECAYS + 1 + SCAN0)
                    nc.scalar.activation(decay[:, t % DECAYS, :], delta2[:, d * NBLK + c, :], ACT.Exp,
                                         scale=a_neg[:, o * 2 + d, c, p:p + 1]).then_inc(decay_ready, 1)
                    for at, key, i in sides:
                        if at == t - LAG:
                            take(turn, key, i)
                    if c == 0:
                        g = t // NBLK
                        if g > 0:
                            use = turn.use("C", g, 0)
                        else:
                            use = turn.base - 2 if o == 0 else bank.body[turn.first][0][0, "C", GROUPS, 0] + turn.base
                        copy_c(number * GROUPS + g, g % 2, use)
                    if t == 2 and not (turn.first and o == 0):
                        take_y(number - 1, 1 - o)
                    for kind, j in steps_at(t, turn, ACT_PREPARE, ACT_FINISH):
                        step(turn, kind, j)

            for _, key, i in side_uses(0, False):
                take(Head(), key, i)
                if i == 1 and key[0] == "bc":
                    step(Head(), "hi", key[1])
                    step(Head(), "mid", key[1])
                if i == 1 and key[0] == "dt":
                    step(Head(), "exp", key[1])
                    step(Head(), "one", key[1])
                    step(Head(), "log", key[1])
            over_turns(act, turn_of)
            copy_c(2 * B * GROUPS, 0, Tail.base - 2)
            take_y(2 * B - 1, 1)
            for _, key, i in side_uses(0, True):
                if key in FINISH:
                    take(Tail(), key, i)
                    if (key, i) == (("mean", 0), 1):
                        step(Tail(), "square", 0)
                        step(Tail(), "square", 1)
                    if (key, i) == (("z", 1), 1):
                        step(Tail(), "silu", 0)
                    if (key, i) == (("var", 0), 1):
                        step(Tail(), "rstd", 0)
                        step(Tail(), "affine", 0)
                        step(Tail(), "affine", 1)

        @block.gpsimd
        def _(pool):
            def step(turn, kind, j):
                pool.wait_ge(sp_part, (turn.next * NJ + j) * 2 + 2)
                nc.gpsimd.tensor_tensor(delta[:, j, :], delta[:, j, :], e_of[j][:, :], ALU.subtract).then_inc(sp_delta, 1)

            def turn_of(turn):
                number = turn.number
                for t in range(NT):
                    g = t // NBLK
                    pool.wait_ge(scanned, number * NT + t + 1 + SCAN0)
                    if t % NBLK == 0:
                        if g > 0:
                            use = turn.use("C", g, 1)
                        else:
                            use = turn.base - 1 if turn.r == 0 else (
                                bank.body[turn.first][0][0, "C", GROUPS, 1] + turn.base)
                        wait_side(pool, use)
                    pool.wait_ge(y_added, number * NT + t - READS + 1 + SUM0)
                    nc.gpsimd.tensor_tensor(read[:, t % READS, :], state[:, t % STATES, :], c_rows[:, g % 2, :],
                                            ALU.mult).then_inc(multiplied, 1)
                    for kind, j in steps_at(t, turn, POOL_PREPARE):
                        step(turn, kind, j)

            for j in range(NJ):
                step(Head(), "delta", j)
            over_turns(pool, turn_of)

        @block.vector
        def _(dve):
            for s, n in ((scanned, SCAN0), (multiplied, MULT0), (y_added, SUM0), (injected, INJECT0), (side_free, 1),
                         (y_free, 1)):
                for _ in range(n):
                    dve.sem_inc(s, 1)
            n = [0]

            def setup(ins):
                n[0] += 1
                ins.then_inc(set_up, 1)

            dve.wait_ge(weights, 16 * len(loads))
            setup(nc.vector.memset(mean_w[:, :], 1.0 / DI))
            setup(nc.vector.memset(eps_col[:, :], eps))
            setup(nc.vector.memset(ranks[:, :], 0.0))
            for m in range(2 * NS):
                src = (m // NS) * NS + (m % NS) // 2 + NP * (m % 2)
                setup(nc.vector.tensor_copy(pick[:, m, :], cols_e[:, src:src + 1].to_broadcast([128, BLK])))
            for side in (0, 2):
                setup(nc.vector.memset(fold[:, side * BLK:(side + 1) * BLK], 0.0))
            setup(nc.vector.tensor_tensor(fold[:, BLK:2 * BLK], ident[:, 0:BLK], ident[:, BLK:128], ALU.add))
            for o in range(2):
                setup(nc.vector.tensor_tensor(skip_sum[:, o, :], skip_w[:, o, 0, :], skip_w[:, o, 1, :], ALU.add))
            dve.wait_ge(set_up, n[0])
            for o in range(2):
                for j in range(2):
                    setup(nc.vector.tensor_scalar(skip_diag[:, o, j, :], ident, skip_sum[:, o, j:j + 1], None,
                                                  ALU.mult))
            assert n[0] == n_setup

            def step(turn, kind, j):
                if kind in FINISH_STEPS:
                    done = turn.done_image
                    y, t_of, r = ((y_a, (t_e, t_r, t_w), 128), (y_b, (t_l, t_r, t_l), BLK))[j]
                if kind == "join":
                    dve.wait_ge(y_out, 6 * done + 6)
                    dst = y[:, :].rearrange("p (h w) -> p w h", w=W)
                    nc.vector.tensor_tensor(dst, dst, t_of[0][0:r, :].rearrange("p (w h) -> p w h", h=H),
                                            ALU.add).then_inc(joined, 1)
                elif kind == "centre":
                    wait_side(dve, turn.use(("mean", 0), 1))
                    nc.vector.tensor_tensor(y[:, :], y[:, :], t_r[0:r, :], ALU.subtract).then_inc(centred, 1)
                elif kind == "scale":
                    dve.wait_ge(rooted, done + 1)
                    nc.vector.tensor_tensor(y[:, :], y[:, :], t_e[0:r, :], ALU.mult).then_inc(scaled, 1)
                elif kind == "gate":
                    dve.wait_ge(affine, 2 * done + 2)
                    dve.wait_ge(silued, 2 * done + 2)
                    nc.vector.tensor_tensor(y[:, :], y[:, :], t_of[2][0:r, :], ALU.mult).then_inc(gated, 1)
                elif kind == "residual":
                    wait_side(dve, turn.use(("out", 0), 1))
                    xs = x_cm[:, bass.ts(done, L)]
                    nc.vector.tensor_tensor(xs, xs, t_r[0:C, :], ALU.add).then_inc(x_added, 1)
                elif kind == "rest":
                    dve.wait_ge(bc_hi, turn.next * 2 + j + 1)
                    raw = raw_of[j][BLK:128, :]
                    nc.vector.tensor_tensor(raw, raw, bc[BLK:128, turn.next_order, j, :],
                                            ALU.subtract).then_inc(bc_rest, 1)
                elif kind == "lo":
                    dve.wait_ge(bc_mid, turn.next * 2 + j + 1)
                    low = bc[96:128, turn.next_order, j, :]
                    nc.vector.tensor_tensor(low, raw_of[j][96:128, :], low, ALU.subtract).then_inc(bc_ready, 1)
                elif kind == "fix":
                    dve.wait_ge(sp_log, turn.next * NJ + j + 1)
                    nc.vector.scalar_tensor_tensor(out=t_w[:, :], in0=t_w[:, :], scalar=1.0, in1=t_l[:, :],
                                                   op0=ALU.subtract, op1=ALU.subtract).then_inc(sp_part, 1)
                elif kind == "du":
                    if not isinstance(turn, Head):
                        for d in range(DIRS):
                            dve.wait_ge(du2_in[d], turn.next * PER_DIR)
                    dve.wait_ge(sp_delta, turn.next * NJ + j + 1)
                    nc.vector.tensor_tensor(du[j], delta[:, j, :], u[:, j, :], ALU.mult).then_inc(sp_du, 1)
                else:
                    dve.wait_ge(sp_part, (turn.next * NJ + j) * 2 + 1)
                    nc.vector.scalar_tensor_tensor(out=e_of[j][:, :], in0=t_w[:, :], scalar=0.0, in1=e_of[j][:, :],
                                                   op0=ALU.max, op1=ALU.subtract).then_inc(sp_part, 1)

            def inject_tile(number, t):
                T, (d, p, c) = number * NT + t, tiles[t]
                if p == 0 and c == 0:
                    dve.wait_ge(du2_in[d], (number + 1) * PER_DIR)
                if c == 0:
                    dve.wait_ge(b_ready, number * GROUPS + t // NBLK + 1)
                dve.wait_ge(scanned, T - 1 + SCAN0)
                nc.vector.tensor_tensor(inject[:, t % 2, :], du2[:, d * NBLK + c, :], b_ps[p % 2][:, :],
                                        ALU.mult).then_inc(injected, 1)

            def turn_of(turn):
                number = turn.number
                for t, (d, p, c) in enumerate(tiles):
                    T = number * NT + t
                    inject_tile(number + (t + 1) // NT, (t + 1) % NT)
                    dve.wait_ge(injected, T + 1 + INJECT0)
                    dve.wait_ge(decay_ready, T + 1)
                    dve.wait_ge(multiplied, T - STATES + 1 + MULT0)
                    way = slice(None, None, 1 if d == 0 else -1)
                    nc.vector.tensor_tensor_scan(state[:, t % STATES, way], decay[:, t % DECAYS, way],
                                                 inject[:, t % 2, way], 0.0, ALU.mult, ALU.add).then_inc(scanned, 1)
                    for kind, j in steps_at(t, turn, DVE_PREPARE, DVE_FINISH):
                        step(turn, kind, j)

            for j in range(DIRS):
                step(Head(), "rest", j)
                step(Head(), "lo", j)
            for j in range(NJ):
                step(Head(), "fix", j)
                step(Head(), "part", j)
            for j in range(NJ):
                step(Head(), "du", j)
            inject_tile(0, 0)
            over_turns(dve, turn_of)
            for kind in ("join", "centre", "scale", "gate"):
                for j in range(2):
                    step(Tail(), kind, j)
            step(Tail(), "residual", 0)


def network(nc, hbm, out):
    with ExitStack() as ctx:
        def sb(n, shape):
            return ctx.enter_context(nc.sbuf_tensor(n, shape, F32))

        x_cm = sb("x_cm", [C, B * L])
        g_cm = sb("g_cm", [C, B * L])
        ident = sb("ident", [128, 128])
        group_mean = sb("group_mean", [C, C])
        state_cols = sb("state_cols", [128, 2 * NS])
        row_cols = sb("row_cols", [128, 3])
        loaded = ctx.enter_context(nc.semaphore("loaded"))
        stored = ctx.enter_context(nc.semaphore("stored"))
        with nc.Block() as block:
            @block.sync
            def _(sp):
                sp.dma_start(x_cm[:, :], hbm["x"]).then_inc(loaded, 16)
                sp.dma_start(ident[:, :], hbm["ident"]).then_inc(loaded, 16)
                sp.dma_start(group_mean[:, :], hbm["group_mean"]).then_inc(loaded, 16)
                sp.dma_start(state_cols[:, :], hbm["state_cols"]).then_inc(loaded, 16)
                sp.dma_start(row_cols[:, :], hbm["row_cols"]).then_inc(loaded, 16)
                sp.wait_ge(loaded, 5 * 16)

        def ssm(n, orders, dirs, rank, conv, eps):
            weights = {k[3:]: v for k, v in hbm.items() if k.startswith(n + "_")}
            group_norm(nc, f"{n}_gn", x_cm[:, :], g_cm[:, :], group_mean[:, :])
            if conv:
                scan_layer(nc, n, x_cm, g_cm, ident[:, :], state_cols, weights, orders, dirs, rank, eps)
            else:
                cross_scan_layer(nc, n, x_cm, g_cm, ident[:, :], state_cols, weights, rank, eps)

        ssm("L0", 2, 2, 12, False, 1e-6)
        group_norm(nc, "L1_gn", x_cm[:, :], g_cm[:, :], group_mean[:, :])
        motif_layer(nc, x_cm[:, :], g_cm[:, :], ident[:, :], row_cols)
        ssm("L2", 1, 1, 6, True, 1e-5)
        ssm("L3", 2, 2, 12, False, 1e-6)
        with nc.Block() as block:
            @block.sync
            def _(sp):
                sp.dma_start(out, x_cm[:, :]).then_inc(stored, 16)
                sp.wait_ge(stored, 16)


def _ssm_arrays(np, n, in_w, out_w, xp, dtw, dtb, a_logs, ds, norm_w, norm_b, orders, dirs):
    K, rank = dtw.shape[0], dtw.shape[2]
    ks = [[o + orders * d for d in range(dirs)] for o in range(orders)]
    flat = [k for o in ks for k in o]
    nj = -(-dirs * NBLK // 2)

    def tiles(v):
        r = np.zeros((256,), np.float32)
        r[:DI] = v
        return r.reshape(2, 128).T

    wt = in_w.T
    r = {"w_u": np.concatenate([wt[:, :DI], wt[:, :DI]], 1), "w_z": np.concatenate([wt[:, DI:], wt[:, DI:DI + BLK]], 1)}
    bc = np.stack([np.tile(xp[k, rank:].T, (1, 4)) for k in flat], 1)
    if dirs == 2:
        for i, k in enumerate(flat):
            bc[:, i, 32:32 + rank] = xp[k, :rank].T
    r["w_bc_a"], r["w_bc_b"] = bc[:128], bc[128:]
    if dirs == 1:
        rk = np.stack([np.concatenate([xp[k, :rank].T for k in o], 1) for o in ks], 1)
        r["w_r_a"], r["w_r_b"] = rk[:128], rk[128:]
    w_dt = np.zeros((32 * (dirs - 1) + rank, orders, 128 * nj), np.float32)
    bias = np.zeros((orders, 128 * nj), np.float32)
    for o in range(orders):
        for d, k in enumerate(ks[o]):
            w_dt[32 * d:32 * d + rank, o, d * DI:(d + 1) * DI] = dtw[k].T
            bias[o, d * DI:(d + 1) * DI] = dtb[k]
    r["w_dt"] = w_dt
    r["dt_bias"] = bias.reshape(orders, nj, 128).transpose(2, 0, 1)
    a = a_logs.reshape(K, NBLK, BLK, 2, NP)[flat]
    r["a_logs"] = a.transpose(3, 2, 0, 1, 4).reshape(128, len(flat), NBLK, NP)
    d = ds.reshape(K, DI)
    r["skip"] = np.stack([np.stack([tiles(d[k]) for k in o], 1) for o in ks], 1)
    r["norm"] = np.stack([tiles(norm_w), tiles(norm_b)], 1)
    r["w_o_a"], r["w_o_b"] = out_w.T[:128], out_w.T[128:]
    return {f"{n}_{k}": v for k, v in r.items()}, tiles


def kernel(**inputs):
    import numpy as np
    import concourse.bacc as _bacc
    from concourse.bass_utils import run_bass_kernel_spmd as _run

    v = {k: np.asarray(a) for k, a in inputs.items()}
    arrays = {"x": v["x"].reshape(B * L, C).T, "ident": np.eye(128, dtype=np.float32)}
    group = np.arange(C) // (C // 32)
    arrays["group_mean"] = (group[:, None] == group[None, :]).astype(np.float32) / np.float32(C // 32)
    rows = np.arange(128)
    part = np.arange(128) // 32
    arrays["state_cols"] = ((rows[:, None] % 32 == np.arange(32)[None, :]) & (part != 1)[:, None]).astype(np.float32)
    arrays["row_cols"] = np.stack([rows % 2 == 0, rows % 2 == 1, rows >= H], 1).astype(np.float32)
    for n in ("L0", "L3"):
        g = lambda s: v[f"{n}_conv_{s}"]
        a, _ = _ssm_arrays(np, n, g("in_proj_weight"), g("out_proj_weight"), g("x_proj_weight"),
                           g("dt_projs_weight"), g("dt_projs_bias"), g("A_logs"), g("Ds"), g("out_norm_weight"),
                           g("out_norm_bias"), 2, 2)
        arrays.update(a)
    g = lambda s: v[f"L2_conv_{s}"]
    a, tiles = _ssm_arrays(np, "L2", g("in_proj_w"), g("out_proj_w"), g("x_proj_w")[None], g("dt_proj_w")[None],
                           g("dt_proj_b")[None], g("A_log"), g("Ds"), g("ln_g"), g("ln_b"), 1, 1)
    arrays.update(a)
    cw = g("conv_w").reshape(DI, 9)
    arrays["L2_conv_w"] = np.stack([tiles(cw[:, k]) for k in range(9)], 2)
    arrays["L2_in_bias"] = np.stack([tiles(g("in_proj_b")[:DI]), tiles(g("in_proj_b")[DI:])], 1)
    arrays["L2_conv_b"] = tiles(g("conv_b"))
    arrays["L2_out_bias"] = g("out_proj_b").reshape(C, 1)
    arrays = {f"in_{k}": np.ascontiguousarray(a) for k, a in arrays.items()}

    nc = _bacc.Bacc("TRN2", target_bir_lowering=False, num_devices=1)
    hbm = {k[3:]: nc.dram_tensor(k, a.shape, mybir.dt.from_np(a.dtype), kind="ExternalInput").ap()
           for k, a in arrays.items()}
    out = nc.dram_tensor("out_y", [C, B * L], F32, kind="ExternalOutput").ap()
    network(nc, hbm, out)
    r = _run(nc, [arrays], core_ids=[0])
    return np.ascontiguousarray(r.results[0]["out_y"].T).reshape(B, H, W, C)
```
